# Optimizing a Trainium2 kernel written in Bass

```python
import numpy as np
import jax
import jax.numpy as jnp

def _softmax(x, axis=-1):
    return jax.nn.softmax(x, axis=axis)

def _gelu(x):
    return jax.nn.gelu(x, approximate=True)

def _silu(x):
    return jax.nn.silu(x)

def _sigmoid(x):
    return jax.nn.sigmoid(x)

def _layernorm(x, axis=-1, eps=1e-05):
    m = jnp.mean(x, axis=axis, keepdims=True)
    v = jnp.var(x, axis=axis, keepdims=True)
    return (x - m) / jnp.sqrt(v + eps)

def _scatter_add(tgt, idx, src, axis=0):
    return tgt.at[idx].add(src)

def _segment_sum(src, seg, n):
    return jax.ops.segment_sum(src, seg, n)
kernel_name = 'mk_decoder_preln_d2_seqx_r8_97b7d1'

def setup_inputs(seed: int=0):
    np.random.seed(seed)
    _w = jnp.asarray

    def _rec_inputs():
        import jax
        import jax.numpy as jnp
        _rk = jax.random.key(seed)
        x = -0.0002928 + 1 * jax.random.normal(jax.random.fold_in(_rk, 1), (32, 128, 128), jnp.float32)
        _lenS = 128 - jax.random.randint(jax.random.fold_in(_rk, 7), (32,), 0, max(1, 128 // 4) + 1, jnp.int32)
        _lenS2 = 77 - jax.random.randint(jax.random.fold_in(_rk, 8), (32,), 0, max(1, 77 // 4) + 1, jnp.int32)
        _ctx_1024P = jax.random.normal(jax.random.fold_in(_rk, 11), (32, 16, 128), jnp.float32)
        _ctx_1024c = jax.random.dirichlet(jax.random.fold_in(_rk, 511), 0.3 * jnp.ones((16,), jnp.float32), (32, 77))
        _ctx_1024t = jnp.einsum('bsk,bkd->bsd', _ctx_1024c, _ctx_1024P)
        _ctx_1024t = _ctx_1024t * jax.lax.rsqrt(jnp.mean(jnp.square(_ctx_1024t)) + 1e-12) * 0.953939
        ctx_1024 = -1.39393e-06 + 0.999914 * (_ctx_1024t + 0.3 * jax.random.normal(jax.random.fold_in(_rk, 611), (32, 77, 128), jnp.float32))
        return (x, ctx_1024)
    x, ctx_1024 = _rec_inputs()

    def _L0_attn_setup():
        import jax, jax.numpy as jnp
        import numpy as np
        import math
        B, T, C = (8, 256, 128)
        DIM_ATT, DIM_FFN = (128, 512)
        N_LAYER, LAYER_ID = (12, 1)
        EPS = 1e-05

        def layer_norm(x, w, b):
            mu = jnp.mean(x, axis=-1, keepdims=True)
            var = jnp.mean(jnp.square(x - mu), axis=-1, keepdims=True)
            return (x - mu) * jax.lax.rsqrt(var + EPS) * w + b

        def time_shift(x):
            return jnp.pad(x, ((0, 0), (1, 0), (0, 0)))[:, :-1, :]

        def wkv(time_decay, time_first, k, v):
            w = -jnp.exp(time_decay)
            u = time_first

            def step(carry, kv_t):
                aa, bb, pp = carry
                kt, vt = kv_t
                ww = u + kt
                qq = jnp.maximum(pp, ww)
                e1 = jnp.exp(pp - qq)
                e2 = jnp.exp(ww - qq)
                y = (e1 * aa + e2 * vt) / (e1 * bb + e2)
                ww2 = pp + w
                qq2 = jnp.maximum(ww2, kt)
                e1b = jnp.exp(ww2 - qq2)
                e2b = jnp.exp(kt - qq2)
                return ((e1b * aa + e2b * vt, e1b * bb + e2b, qq2), y)
            init = (jnp.zeros_like(k[:, 0]), jnp.zeros_like(k[:, 0]), jnp.full_like(k[:, 0], -1e+38))
            kT = jnp.swapaxes(k, 0, 1)
            vT = jnp.swapaxes(v, 0, 1)
            _, yT = jax.lax.scan(step, init, (kT, vT))
            return jnp.swapaxes(yT, 0, 1)
        key = jax.random.key(seed)
        ks = jax.random.split(key, 16)
        r01 = LAYER_ID / (N_LAYER - 1)
        r1a0 = 1.0 - LAYER_ID / N_LAYER
        ddd = (np.arange(C, dtype=np.float32) / C)[None, None, :]
        decay_speed = -5.0 + 8.0 * (np.arange(DIM_ATT, dtype=np.float32) / (DIM_ATT - 1)) ** (0.7 + 1.3 * r01)
        zigzag = np.array([(i + 1) % 3 - 1 for i in range(DIM_ATT)], dtype=np.float32) * 0.5

        def lin(k, out_d, in_d):
            return jax.random.normal(k, (out_d, in_d), jnp.float32) * (1.0 / math.sqrt(in_d))
        return {'x': jax.random.normal(ks[0], (B, T, C), jnp.float32), 'ln1_w': jnp.ones((C,), jnp.float32), 'ln1_b': jnp.zeros((C,), jnp.float32), 'ln2_w': jnp.ones((C,), jnp.float32), 'ln2_b': jnp.zeros((C,), jnp.float32), 'att_tmk': jnp.asarray(ddd ** r1a0), 'att_tmv': jnp.asarray(ddd ** r1a0 + 0.3 * r01), 'att_tmr': jnp.asarray(ddd ** (0.5 * r1a0)), 'time_decay': jnp.asarray(decay_speed), 'time_first': jnp.asarray(np.full(DIM_ATT, math.log(0.3), np.float32) + zigzag), 'Wk': lin(ks[1], DIM_ATT, C), 'Wv': lin(ks[2], DIM_ATT, C), 'Wr': lin(ks[3], DIM_ATT, C), 'Wo': lin(ks[4], C, DIM_ATT), 'ffn_tmk': jnp.asarray(ddd ** r1a0), 'ffn_tmr': jnp.asarray(ddd ** r1a0), 'Wkey': lin(ks[5], DIM_FFN, C), 'Wrec': lin(ks[6], C, C), 'Wval': lin(ks[7], C, DIM_FFN)}
    _L0_attn_all = _L0_attn_setup()
    _L0_attn_in = {k: v for k, v in _L0_attn_all.items() if k in ('ln1_w', 'ln1_b', 'ln2_w', 'ln2_b', 'att_tmk', 'att_tmv', 'att_tmr', 'time_decay', 'time_first', 'Wk', 'Wv', 'Wr', 'Wo', 'ffn_tmk', 'ffn_tmr', 'Wkey', 'Wrec', 'Wval')}
    del _L0_attn_all

    def _L0_xattn_setup():
        import jax, jax.numpy as jnp
        import numpy as np
        import math
        D_MODEL = 128
        N_HEADS = 16
        key = jax.random.key(seed)
        ks = jax.random.split(key, 11)
        N, L, S = (2, 256, 256)
        d = D_MODEL
        s = 1.0 / math.sqrt(d)
        return {'queries': jax.random.normal(ks[0], (N, L, d), dtype=jnp.float32), 'keys': jax.random.normal(ks[1], (N, S, d), dtype=jnp.float32), 'values': jax.random.normal(ks[2], (N, S, d), dtype=jnp.float32), 'Wq': jax.random.normal(ks[3], (d, d), dtype=jnp.float32) * s, 'bq': jax.random.normal(ks[4], (d,), dtype=jnp.float32) * s, 'Wk': jax.random.normal(ks[5], (d, d), dtype=jnp.float32) * s, 'bk': jax.random.normal(ks[6], (d,), dtype=jnp.float32) * s, 'Wv': jax.random.normal(ks[7], (d, d), dtype=jnp.float32) * s, 'bv': jax.random.normal(ks[8], (d,), dtype=jnp.float32) * s, 'Wo': jax.random.normal(ks[9], (d, d), dtype=jnp.float32) * s, 'bo': jax.random.normal(ks[10], (d,), dtype=jnp.float32) * s}
    _L0_xattn_all = _L0_xattn_setup()
    _L0_xattn_in = {k: v for k, v in _L0_xattn_all.items() if k in ('Wq', 'bq', 'Wk', 'bk', 'Wv', 'bv', 'Wo', 'bo')}
    del _L0_xattn_all

    def _L0_ffn_setup():
        import math
        import jax, jax.numpy as jnp
        import numpy as np
        TOP_K = 2
        _GELU_C = math.sqrt(2.0 / math.pi)

        def gelu_new(x):
            return 0.5 * x * (1.0 + jnp.tanh(_GELU_C * (x + 0.044715 * x * x * x)))
        key = jax.random.key(seed)
        ks = jax.random.split(key, 6)
        B, T, C, E, H = (2, 256, 128, 8, 512)
        s_in = 1.0 / math.sqrt(C)
        s_hid = 1.0 / math.sqrt(H)
        return {'x': jax.random.normal(ks[0], (B, T, C), dtype=jnp.float32), 'router_w': jax.random.normal(ks[1], (E, C), dtype=jnp.float32) * s_in, 'w_fc': jax.random.normal(ks[2], (E, C, H), dtype=jnp.float32) * s_in, 'b_fc': jax.random.normal(ks[3], (E, H), dtype=jnp.float32) * 0.02, 'w_proj': jax.random.normal(ks[4], (E, H, C), dtype=jnp.float32) * s_hid, 'b_proj': jax.random.normal(ks[5], (E, C), dtype=jnp.float32) * 0.02}
    _L0_ffn_all = _L0_ffn_setup()
    _L0_ffn_in = {k: v for k, v in _L0_ffn_all.items() if k in ('router_w', 'w_fc', 'b_fc', 'w_proj', 'b_proj')}
    del _L0_ffn_all

    def _L1_attn_setup():
        import jax, jax.numpy as jnp
        import numpy as np
        from jax import lax
        B, L, D, K = (4, 512, 128, 3)
        H = 256

        def _layernorm(h, g, b):
            m = jnp.mean(h, axis=-1, keepdims=True)
            v = jnp.mean((h - m) ** 2, axis=-1, keepdims=True)
            return (h - m) / jnp.sqrt(v + 1e-05) * g + b
        key = jax.random.key(seed)
        ks = jax.random.split(key, 16)
        s = 0.02
        return {'x': jax.random.normal(ks[0], (B, L, D), jnp.float32), 'ln1_g': jnp.ones((D,), jnp.float32), 'ln1_b': jnp.zeros((D,), jnp.float32), 'in_W': jax.random.normal(ks[1], (D, 2 * D), jnp.float32) * s, 'in_b': jnp.zeros((2 * D,), jnp.float32), 'dw_W': jax.random.normal(ks[2], (D, 1, K), jnp.float32) * s, 'dw_b': jnp.zeros((D,), jnp.float32), 'dt_W': jax.random.normal(ks[3], (D, D), jnp.float32) * s, 'dt_b': jnp.zeros((D,), jnp.float32), 'b_W': jax.random.normal(ks[4], (D, D), jnp.float32) * s, 'b_b': jnp.zeros((D,), jnp.float32), 'c_W': jax.random.normal(ks[5], (D, D), jnp.float32) * s, 'c_b': jnp.zeros((D,), jnp.float32), 'a_log': jnp.zeros((D,), jnp.float32), 'd_skip': jnp.ones((D,), jnp.float32), 'out_W': jax.random.normal(ks[6], (D, D), jnp.float32) * s, 'out_b': jnp.zeros((D,), jnp.float32), 'ln2_g': jnp.ones((D,), jnp.float32), 'ln2_b': jnp.zeros((D,), jnp.float32), 'f1_W': jax.random.normal(ks[7], (D, H), jnp.float32) * s, 'f1_b': jnp.zeros((H,), jnp.float32), 'f2_W': jax.random.normal(ks[8], (H, D), jnp.float32) * s, 'f2_b': jnp.zeros((D,), jnp.float32)}
    _L1_attn_all = _L1_attn_setup()
    _L1_attn_in = {k: v for k, v in _L1_attn_all.items() if k in ('ln1_g', 'ln1_b', 'in_W', 'in_b', 'dw_W', 'dw_b', 'dt_W', 'dt_b', 'b_W', 'b_b', 'c_W', 'c_b', 'a_log', 'd_skip', 'out_W', 'out_b', 'ln2_g', 'ln2_b', 'f1_W', 'f1_b', 'f2_W', 'f2_b')}
    del _L1_attn_all

    def _L1_xattn_setup():
        import jax, jax.numpy as jnp
        import numpy as np
        DIM = 128
        NUM_HEADS = 16
        HEAD_DIM = DIM // NUM_HEADS
        SCALE = HEAD_DIM ** (-0.5)
        key = jax.random.key(seed)
        ks = jax.random.split(key, 8)
        B, QL, KL = (2, 256, 256)
        s = DIM ** (-0.5)
        return {'q': jax.random.normal(ks[0], (B, QL, DIM), jnp.float32), 'k': jax.random.normal(ks[1], (B, KL, DIM), jnp.float32), 'v': jax.random.normal(ks[2], (B, KL, DIM), jnp.float32), 'Wq': jax.random.normal(ks[3], (DIM, DIM), jnp.float32) * s, 'Wk': jax.random.normal(ks[4], (DIM, DIM), jnp.float32) * s, 'Wv': jax.random.normal(ks[5], (DIM, DIM), jnp.float32) * s, 'Wo': jax.random.normal(ks[6], (DIM, DIM), jnp.float32) * s, 'bo': jax.random.normal(ks[7], (DIM,), jnp.float32) * 0.02}
    _L1_xattn_all = _L1_xattn_setup()
    _L1_xattn_in = {k: v for k, v in _L1_xattn_all.items() if k in ('Wq', 'Wk', 'Wv', 'Wo', 'bo')}
    del _L1_xattn_all

    def _L1_ffn_setup():
        import jax, jax.numpy as jnp
        import numpy as np
        BLOCK = 32
        W_BITS = 4
        ACT_BITS = 16

        def act_qdq(x):
            qmax = 2.0 ** (ACT_BITS - 1) - 1.0
            scale = jnp.maximum(jnp.max(jnp.abs(x)) / qmax, 1e-12)
            return jnp.clip(jnp.round(x / scale), -qmax - 1.0, qmax) * scale

        def fixed_qdq_u16(x):
            scale = 1.0 / 65536.0
            return jnp.clip(jnp.round(x / scale), 0.0, 65535.0) * scale

        def lpbq_dequant(w):
            O, I = w.shape
            qmax = 2.0 ** (W_BITS - 1) - 1.0
            wb = w.reshape(O, I // BLOCK, BLOCK)
            s = jnp.maximum(jnp.max(jnp.abs(wb), axis=-1, keepdims=True) / qmax, 1e-12)
            wq = jnp.clip(jnp.round(wb / s), -qmax - 1.0, qmax) * s
            return wq.reshape(O, I)
        key = jax.random.key(seed)
        k1, k2, k3, k4 = jax.random.split(key, 4)
        B, S, H, I = (2, 512, 128, 384)
        x = jax.random.normal(k1, (B, S, H), jnp.float32)
        w_gate = jax.random.normal(k2, (I, H), jnp.float32) * 0.02
        w_up = jax.random.normal(k3, (I, H), jnp.float32) * 0.02
        w_down = jax.random.normal(k4, (H, I), jnp.float32) * 0.02
        return {'x': x, 'w_gate': w_gate, 'w_up': w_up, 'w_down': w_down}
    _L1_ffn_all = _L1_ffn_setup()
    _L1_ffn_in = {k: v for k, v in _L1_ffn_all.items() if k in ('w_gate', 'w_up', 'w_down')}
    del _L1_ffn_all
    return {'x': x, 'ctx_1024': ctx_1024, 'L0_attn_ln1_w': _L0_attn_in['ln1_w'], 'L0_attn_ln1_b': _L0_attn_in['ln1_b'], 'L0_attn_ln2_w': _L0_attn_in['ln2_w'], 'L0_attn_ln2_b': _L0_attn_in['ln2_b'], 'L0_attn_att_tmk': _L0_attn_in['att_tmk'], 'L0_attn_att_tmv': _L0_attn_in['att_tmv'], 'L0_attn_att_tmr': _L0_attn_in['att_tmr'], 'L0_attn_time_decay': _L0_attn_in['time_decay'], 'L0_attn_time_first': _L0_attn_in['time_first'], 'L0_attn_Wk': _L0_attn_in['Wk'], 'L0_attn_Wv': _L0_attn_in['Wv'], 'L0_attn_Wr': _L0_attn_in['Wr'], 'L0_attn_Wo': _L0_attn_in['Wo'], 'L0_attn_ffn_tmk': _L0_attn_in['ffn_tmk'], 'L0_attn_ffn_tmr': _L0_attn_in['ffn_tmr'], 'L0_attn_Wkey': _L0_attn_in['Wkey'], 'L0_attn_Wrec': _L0_attn_in['Wrec'], 'L0_attn_Wval': _L0_attn_in['Wval'], 'L0_xattn_Wq': _L0_xattn_in['Wq'], 'L0_xattn_bq': _L0_xattn_in['bq'], 'L0_xattn_Wk': _L0_xattn_in['Wk'], 'L0_xattn_bk': _L0_xattn_in['bk'], 'L0_xattn_Wv': _L0_xattn_in['Wv'], 'L0_xattn_bv': _L0_xattn_in['bv'], 'L0_xattn_Wo': _L0_xattn_in['Wo'], 'L0_xattn_bo': _L0_xattn_in['bo'], 'L0_ffn_router_w': _L0_ffn_in['router_w'], 'L0_ffn_w_fc': _L0_ffn_in['w_fc'], 'L0_ffn_b_fc': _L0_ffn_in['b_fc'], 'L0_ffn_w_proj': _L0_ffn_in['w_proj'], 'L0_ffn_b_proj': _L0_ffn_in['b_proj'], 'L1_attn_ln1_g': _L1_attn_in['ln1_g'], 'L1_attn_ln1_b': _L1_attn_in['ln1_b'], 'L1_attn_in_W': _L1_attn_in['in_W'], 'L1_attn_in_b': _L1_attn_in['in_b'], 'L1_attn_dw_W': _L1_attn_in['dw_W'], 'L1_attn_dw_b': _L1_attn_in['dw_b'], 'L1_attn_dt_W': _L1_attn_in['dt_W'], 'L1_attn_dt_b': _L1_attn_in['dt_b'], 'L1_attn_b_W': _L1_attn_in['b_W'], 'L1_attn_b_b': _L1_attn_in['b_b'], 'L1_attn_c_W': _L1_attn_in['c_W'], 'L1_attn_c_b': _L1_attn_in['c_b'], 'L1_attn_a_log': _L1_attn_in['a_log'], 'L1_attn_d_skip': _L1_attn_in['d_skip'], 'L1_attn_out_W': _L1_attn_in['out_W'], 'L1_attn_out_b': _L1_attn_in['out_b'], 'L1_attn_ln2_g': _L1_attn_in['ln2_g'], 'L1_attn_ln2_b': _L1_attn_in['ln2_b'], 'L1_attn_f1_W': _L1_attn_in['f1_W'], 'L1_attn_f1_b': _L1_attn_in['f1_b'], 'L1_attn_f2_W': _L1_attn_in['f2_W'], 'L1_attn_f2_b': _L1_attn_in['f2_b'], 'L1_xattn_Wq': _L1_xattn_in['Wq'], 'L1_xattn_Wk': _L1_xattn_in['Wk'], 'L1_xattn_Wv': _L1_xattn_in['Wv'], 'L1_xattn_Wo': _L1_xattn_in['Wo'], 'L1_xattn_bo': _L1_xattn_in['bo'], 'L1_ffn_w_gate': _L1_ffn_in['w_gate'], 'L1_ffn_w_up': _L1_ffn_in['w_up'], 'L1_ffn_w_down': _L1_ffn_in['w_down']}

def reference(x, ctx_1024, L0_attn_ln1_w, L0_attn_ln1_b, L0_attn_ln2_w, L0_attn_ln2_b, L0_attn_att_tmk, L0_attn_att_tmv, L0_attn_att_tmr, L0_attn_time_decay, L0_attn_time_first, L0_attn_Wk, L0_attn_Wv, L0_attn_Wr, L0_attn_Wo, L0_attn_ffn_tmk, L0_attn_ffn_tmr, L0_attn_Wkey, L0_attn_Wrec, L0_attn_Wval, L0_xattn_Wq, L0_xattn_bq, L0_xattn_Wk, L0_xattn_bk, L0_xattn_Wv, L0_xattn_bv, L0_xattn_Wo, L0_xattn_bo, L0_ffn_router_w, L0_ffn_w_fc, L0_ffn_b_fc, L0_ffn_w_proj, L0_ffn_b_proj, L1_attn_ln1_g, L1_attn_ln1_b, L1_attn_in_W, L1_attn_in_b, L1_attn_dw_W, L1_attn_dw_b, L1_attn_dt_W, L1_attn_dt_b, L1_attn_b_W, L1_attn_b_b, L1_attn_c_W, L1_attn_c_b, L1_attn_a_log, L1_attn_d_skip, L1_attn_out_W, L1_attn_out_b, L1_attn_ln2_g, L1_attn_ln2_b, L1_attn_f1_W, L1_attn_f1_b, L1_attn_f2_W, L1_attn_f2_b, L1_xattn_Wq, L1_xattn_Wk, L1_xattn_Wv, L1_xattn_Wo, L1_xattn_bo, L1_ffn_w_gate, L1_ffn_w_up, L1_ffn_w_down):
    import jax
    import jax.numpy as jnp

    def _L0_attn_ref(x, ln1_w, ln1_b, ln2_w, ln2_b, att_tmk, att_tmv, att_tmr, time_decay, time_first, Wk, Wv, Wr, Wo, ffn_tmk, ffn_tmr, Wkey, Wrec, Wval):
        import jax, jax.numpy as jnp
        import numpy as np
        import math
        B, T, C = (8, 256, 128)
        DIM_ATT, DIM_FFN = (128, 512)
        N_LAYER, LAYER_ID = (12, 1)
        EPS = 1e-05

        def layer_norm(x, w, b):
            mu = jnp.mean(x, axis=-1, keepdims=True)
            var = jnp.mean(jnp.square(x - mu), axis=-1, keepdims=True)
            return (x - mu) * jax.lax.rsqrt(var + EPS) * w + b

        def time_shift(x):
            return jnp.pad(x, ((0, 0), (1, 0), (0, 0)))[:, :-1, :]

        def wkv(time_decay, time_first, k, v):
            w = -jnp.exp(time_decay)
            u = time_first

            def step(carry, kv_t):
                aa, bb, pp = carry
                kt, vt = kv_t
                ww = u + kt
                qq = jnp.maximum(pp, ww)
                e1 = jnp.exp(pp - qq)
                e2 = jnp.exp(ww - qq)
                y = (e1 * aa + e2 * vt) / (e1 * bb + e2)
                ww2 = pp + w
                qq2 = jnp.maximum(ww2, kt)
                e1b = jnp.exp(ww2 - qq2)
                e2b = jnp.exp(kt - qq2)
                return ((e1b * aa + e2b * vt, e1b * bb + e2b, qq2), y)
            init = (jnp.zeros_like(k[:, 0]), jnp.zeros_like(k[:, 0]), jnp.full_like(k[:, 0], -1e+38))
            kT = jnp.swapaxes(k, 0, 1)
            vT = jnp.swapaxes(v, 0, 1)
            _, yT = jax.lax.scan(step, init, (kT, vT))
            return jnp.swapaxes(yT, 0, 1)
        h = layer_norm(x, ln1_w, ln1_b)
        hh = time_shift(h)
        xk = h * att_tmk + hh * (1 - att_tmk)
        xv = h * att_tmv + hh * (1 - att_tmv)
        xr = h * att_tmr + hh * (1 - att_tmr)
        k = xk @ Wk.T
        v = xv @ Wv.T
        sr = jax.nn.sigmoid(xr @ Wr.T)
        rwkv = sr * wkv(time_decay, time_first, k, v)
        x = x + rwkv @ Wo.T
        h = layer_norm(x, ln2_w, ln2_b)
        hh = time_shift(h)
        xk = h * ffn_tmk + hh * (1 - ffn_tmk)
        xr = h * ffn_tmr + hh * (1 - ffn_tmr)
        kk = jnp.square(jax.nn.relu(xk @ Wkey.T))
        kv = kk @ Wval.T
        x = x + jax.nn.sigmoid(xr @ Wrec.T) * kv
        return x

    def _L0_xattn_ref(queries, keys, values, Wq, bq, Wk, bk, Wv, bv, Wo, bo):
        import jax, jax.numpy as jnp
        import numpy as np
        import math
        D_MODEL = 128
        N_HEADS = 16
        N, L, _ = queries.shape
        S = keys.shape[1]
        H = N_HEADS
        q = (queries @ Wq.T + bq).reshape(N, L, H, -1)
        k = (keys @ Wk.T + bk).reshape(N, S, H, -1)
        v = (values @ Wv.T + bv).reshape(N, S, H, -1)
        D = k.shape[-1]
        sm = jnp.einsum('nlhd,nshd->nlhs', q, k) / math.sqrt(D)
        causal_mask = jnp.triu(jnp.ones((L, S), dtype=bool), k=1)
        sm = jnp.where(causal_mask[None, :, None, :], -jnp.inf, sm)
        sm = jax.nn.softmax(sm, axis=-1)
        attn = jnp.einsum('nlhs,nshd->nlhd', sm, v)
        new_values = attn.reshape(N, L, H * D)
        return new_values @ Wo.T + bo

    def _L0_ffn_ref(x, router_w, w_fc, b_fc, w_proj, b_proj):
        import math
        import jax, jax.numpy as jnp
        import numpy as np
        TOP_K = 2
        _GELU_C = math.sqrt(2.0 / math.pi)

        def gelu_new(x):
            return 0.5 * x * (1.0 + jnp.tanh(_GELU_C * (x + 0.044715 * x * x * x)))
        B, T, C = x.shape
        E = router_w.shape[0]
        N = B * T
        xf = x.reshape(N, C)
        logits = xf @ router_w.T
        probs = jax.nn.softmax(logits, axis=-1)
        topk_probs, topk_idx = jax.lax.top_k(probs, TOP_K)
        topk_probs = topk_probs / jnp.sum(topk_probs, axis=-1, keepdims=True)
        combine = jnp.zeros((N, E), dtype=x.dtype).at[jnp.arange(N)[:, None], topk_idx].add(topk_probs)
        h = gelu_new(jnp.einsum('nc,ech->neh', xf, w_fc) + b_fc)
        out = jnp.einsum('neh,ehc->nec', h, w_proj) + b_proj
        y = jnp.einsum('nec,ne->nc', out, combine)
        return y.reshape(B, T, C)

    def _L1_attn_ref(x, ln1_g, ln1_b, in_W, in_b, dw_W, dw_b, dt_W, dt_b, b_W, b_b, c_W, c_b, a_log, d_skip, out_W, out_b, ln2_g, ln2_b, f1_W, f1_b, f2_W, f2_b):
        import jax, jax.numpy as jnp
        import numpy as np
        from jax import lax
        B, L, D, K = (4, 512, 128, 3)
        H = 256

        def _layernorm(h, g, b):
            m = jnp.mean(h, axis=-1, keepdims=True)
            v = jnp.mean((h - m) ** 2, axis=-1, keepdims=True)
            return (h - m) / jnp.sqrt(v + 1e-05) * g + b
        nx = _layernorm(x, ln1_g, ln1_b)
        proj = nx @ in_W + in_b
        x_proj, gate = jnp.split(proj, 2, axis=-1)
        xt = jnp.transpose(x_proj, (0, 2, 1))
        mixed = lax.conv_general_dilated(xt, dw_W, window_strides=(1,), padding=[(K // 2, K // 2)], dimension_numbers=('NCH', 'OIH', 'NCH'), feature_group_count=D)
        mixed = jnp.transpose(mixed + dw_b[None, :, None], (0, 2, 1))
        dt = jax.nn.softplus(mixed @ dt_W + dt_b)
        bt = jnp.tanh(mixed @ b_W + b_b)
        ct = jnp.tanh(mixed @ c_W + c_b)
        a = -jnp.exp(a_log)

        def step(state, inp):
            dt_t, b_t, c_t, m_t, g_t = inp
            decay = jnp.exp(dt_t * a)
            state = decay * state + dt_t * b_t * m_t
            y_t = c_t * state + d_skip * m_t
            return (state, y_t * jax.nn.sigmoid(g_t))
        seqs = tuple((jnp.transpose(t, (1, 0, 2)) for t in (dt, bt, ct, mixed, gate)))
        state0 = jnp.zeros((x.shape[0], x.shape[2]), x.dtype)
        _, ys = lax.scan(step, state0, seqs)
        y = jnp.transpose(ys, (1, 0, 2))
        x2 = x + y @ out_W + out_b
        h = _layernorm(x2, ln2_g, ln2_b)
        ffn = jax.nn.gelu(h @ f1_W + f1_b, approximate=False) @ f2_W + f2_b
        return x2 + ffn

    def _L1_xattn_ref(q, k, v, Wq, Wk, Wv, Wo, bo):
        import jax, jax.numpy as jnp
        import numpy as np
        DIM = 128
        NUM_HEADS = 16
        HEAD_DIM = DIM // NUM_HEADS
        SCALE = HEAD_DIM ** (-0.5)
        B, QL, _ = q.shape
        KL = k.shape[1]
        qh = (q @ Wq.T).reshape(B, QL, NUM_HEADS, HEAD_DIM)
        kh = (k @ Wk.T).reshape(B, KL, NUM_HEADS, HEAD_DIM)
        vh = (v @ Wv.T).reshape(B, KL, NUM_HEADS, HEAD_DIM)
        attn = jnp.einsum('bnhc,bmhc->bhnm', qh, kh) * SCALE
        attn = jax.nn.softmax(attn, axis=-1)
        out = jnp.einsum('bhnm,bmhc->bnhc', attn, vh).reshape(B, QL, DIM)
        return out @ Wo.T + bo

    def _L1_ffn_ref(x, w_gate, w_up, w_down):
        import jax, jax.numpy as jnp
        import numpy as np
        BLOCK = 32
        W_BITS = 4
        ACT_BITS = 16

        def act_qdq(x):
            qmax = 2.0 ** (ACT_BITS - 1) - 1.0
            scale = jnp.maximum(jnp.max(jnp.abs(x)) / qmax, 1e-12)
            return jnp.clip(jnp.round(x / scale), -qmax - 1.0, qmax) * scale

        def fixed_qdq_u16(x):
            scale = 1.0 / 65536.0
            return jnp.clip(jnp.round(x / scale), 0.0, 65535.0) * scale

        def lpbq_dequant(w):
            O, I = w.shape
            qmax = 2.0 ** (W_BITS - 1) - 1.0
            wb = w.reshape(O, I // BLOCK, BLOCK)
            s = jnp.maximum(jnp.max(jnp.abs(wb), axis=-1, keepdims=True) / qmax, 1e-12)
            wq = jnp.clip(jnp.round(wb / s), -qmax - 1.0, qmax) * s
            return wq.reshape(O, I)
        x = act_qdq(x)
        up = act_qdq(x @ lpbq_dequant(w_up).T)
        gate = act_qdq(x @ lpbq_dequant(w_gate).T)
        sig = fixed_qdq_u16(jax.nn.sigmoid(gate))
        gate = act_qdq(gate * sig)
        o = act_qdq(gate * up)
        return o @ lpbq_dequant(w_down).T
    x = x + _L0_attn_ref(_layernorm(x, axis=-1), L0_attn_ln1_w, L0_attn_ln1_b, L0_attn_ln2_w, L0_attn_ln2_b, L0_attn_att_tmk, L0_attn_att_tmv, L0_attn_att_tmr, L0_attn_time_decay, L0_attn_time_first, L0_attn_Wk, L0_attn_Wv, L0_attn_Wr, L0_attn_Wo, L0_attn_ffn_tmk, L0_attn_ffn_tmr, L0_attn_Wkey, L0_attn_Wrec, L0_attn_Wval)
    x = x + _L0_xattn_ref(_layernorm(x, axis=-1), ctx_1024, ctx_1024, L0_xattn_Wq, L0_xattn_bq, L0_xattn_Wk, L0_xattn_bk, L0_xattn_Wv, L0_xattn_bv, L0_xattn_Wo, L0_xattn_bo)
    x = x + _L0_ffn_ref(_layernorm(x, axis=-1), L0_ffn_router_w, L0_ffn_w_fc, L0_ffn_b_fc, L0_ffn_w_proj, L0_ffn_b_proj)
    x = x + _L1_attn_ref(_layernorm(x, axis=-1), L1_attn_ln1_g, L1_attn_ln1_b, L1_attn_in_W, L1_attn_in_b, L1_attn_dw_W, L1_attn_dw_b, L1_attn_dt_W, L1_attn_dt_b, L1_attn_b_W, L1_attn_b_b, L1_attn_c_W, L1_attn_c_b, L1_attn_a_log, L1_attn_d_skip, L1_attn_out_W, L1_attn_out_b, L1_attn_ln2_g, L1_attn_ln2_b, L1_attn_f1_W, L1_attn_f1_b, L1_attn_f2_W, L1_attn_f2_b)
    x = x + _L1_xattn_ref(_layernorm(x, axis=-1), ctx_1024, ctx_1024, L1_xattn_Wq, L1_xattn_Wk, L1_xattn_Wv, L1_xattn_Wo, L1_xattn_bo)
    x = x + _L1_ffn_ref(_layernorm(x, axis=-1), L1_ffn_w_gate, L1_ffn_w_up, L1_ffn_w_down)
    return x

_drawn_inputs = setup_inputs


def setup_inputs(seed=0):
    import zlib

    import numpy as np

    out = dict(_drawn_inputs(seed))
    spreads = {'L0_attn_ln1_w': (1.0, 0.2),
     'L0_attn_ln1_b': (0.0, 0.1),
     'L0_attn_ln2_w': (1.0, 0.2),
     'L0_attn_ln2_b': (0.0, 0.1),
     'L1_attn_ln1_g': (1.0, 0.6),
     'L1_attn_ln1_b': (0.0, 0.8),
     'L1_attn_in_b': (0.0, 0.8),
     'L1_attn_dw_b': (0.0, 0.8),
     'L1_attn_dt_b': (0.0, 0.8),
     'L1_attn_b_b': (0.0, 0.8),
     'L1_attn_c_b': (0.0, 0.8),
     'L1_attn_a_log': (0.0, 0.8),
     'L1_attn_d_skip': (1.0, 0.6),
     'L1_attn_out_b': (0.0, 0.28),
     'L1_attn_ln2_g': (1.0, 0.6),
     'L1_attn_ln2_b': (0.0, 0.8),
     'L1_attn_f1_b': (0.0, 0.8),
     'L1_attn_f2_b': (0.0, 0.274)}
    factors = {'L0_xattn_bq': 3.235,
     'L0_xattn_bk': 8.0,
     'L0_ffn_b_fc': 8.0,
     'L0_ffn_b_proj': 8.0,
     'L1_attn_in_W': 8.0,
     'L1_attn_dw_W': 8.0,
     'L1_attn_dt_W': 8.0,
     'L1_attn_b_W': 8.0,
     'L1_attn_c_W': 8.0,
     'L1_attn_out_W': 8.0,
     'L1_attn_f1_W': 4.729,
     'L1_attn_f2_W': 4.137,
     'L1_xattn_bo': 8.0,
     'L1_ffn_w_gate': 8.0,
     'L1_ffn_w_up': 8.0,
     'L1_ffn_w_down': 8.0}
    for name, (base, spread) in spreads.items():
        noise = np.random.default_rng([zlib.crc32(name.encode()), seed]).standard_normal(out[name].shape)
        drawn = base * np.exp(spread * noise) if base else spread * noise
        out[name] = jnp.asarray(drawn.astype(out[name].dtype))
    for name, factor in factors.items():
        out[name] = (out[name] * factor).astype(out[name].dtype)
    return out
```

```python
import concourse.bass as bass
from concourse import mybir
from contextlib import ExitStack

F32 = mybir.dt.float32
BF16 = mybir.dt.bfloat16
ACT = mybir.ActivationFunctionType
ALU = mybir.AluOpType
AX = mybir.AxisListType

B, T, C = 32, 128, 128
S = 77
CH = 4
NCH = B // CH
W = CH * T
NIT = NCH // 2
H, HD = 16, 8
E, HID = 8, 512
EPS = 1e-5
ATT_SCALE = float(HD) ** -0.5
NEG = -1e38

VECTORS = ["ln1_w", "ln1_b", "ln2_w", "ln2_b", "tmk", "tmv", "tmr", "decay", "first", "ftmk", "ftmr",
           "bq", "bk", "m_ln1_g", "m_ln1_b", "in_b0", "in_b1", "dw0", "dw1", "dw2", "dw_b", "dt_b",
           "b_b", "c_b", "a_log", "d_skip", "m_ln2_g", "m_ln2_b", "f1_b0", "f1_b1"]
LAYOUT = ([(n, 1) for n in VECTORS] +
          [("b_fc", E * 4), ("head_mask", H), ("rank", E), ("ident", 128), ("causal", S),
           ("WkT", C), ("WvT", C), ("WrT", C), ("WoT", C), ("WkeyT", 512), ("WrecT", C), ("WvalT", 4 * C),
           ("qT0", C), ("kT0", C), ("vT0", C), ("oT0", C), ("qT1", C), ("kT1", C), ("vT1", C), ("oT1", C),
           ("router", E), ("in_W", 2 * C), ("dt_W", C), ("b_W", C), ("c_W", C), ("out_W", C),
           ("f1_W", 2 * C), ("f2_W", 2 * C), ("gate", 3 * C), ("up", 3 * C), ("down", 3 * C)])
AT, NPACK = {}, 0
for _n, _w in LAYOUT:
    AT[_n] = (NPACK, _w)
    NPACK += _w
ROWS = ["bv", "bo0", "m_out_b", "f2_b", "bo1"]
EXPERT_WORDS = E * HID + E * 4 * C

ARENA = 33366


class Steps:

    def __init__(self, sem, names, ahead=0):
        self.sem, self.names, self.ahead = sem, names.split(), ahead
        assert len(set(self.names)) == len(self.names)

    def done(self, turn, name):
        return turn * len(self.names) + (self.ahead * len(self.names) + self.names.index(name) + 1)

    def previous(self, turn, p, name):
        return self.done(turn, f"{name}0") if p else self.done(turn - 1, f"{name}1")

    def credit(self):
        return self.ahead * len(self.names)


class Memory:

    def __init__(self, nc, ctx):
        def sb(name, shape, dt=F32):
            return ctx.enter_context(nc.sbuf_tensor(name, shape, dt))

        self.x = sb("x_res", [128, B, C])
        self.xl = sb("x_norm", [128, B, C])
        self.hT = sb("hT", [128, B, T + 1])
        self.pack = sb("pack", [128, NPACK])
        self.rows = sb("rows", [1, len(ROWS) * C])
        self.b_proj = sb("b_proj", [E, C])
        self.ones = sb("ones", [128, 128])
        self.half = sb("half", [128, 2 * CH])
        self.hn = sb("hn", [128, 2, CH, C])
        self.bn = sb("bn", [128, 2 * CH, 6])
        self.tmp = sb("bn_sums", [128, 4, 2 * CH])
        self.mean = sb("mean", [128, 2 * CH])
        self.rs = sb("rs", [128, 7, 2 * CH])
        self.eps = sb("eps", [128, 2 * CH])
        self.arena = sb("arena", [128, ARENA])
        self.ps = ctx.enter_context(nc.psum_tensor("psum", [128, 8 * W], F32))
        self.at = 0

    def col(self, name, i=0):
        o = AT[name][0] + i
        return self.pack[:, o:o + 1]

    def mat(self, name, i=0, w=C):
        o = AT[name][0] + i * w
        return self.pack[:, o:o + w]

    def row(self, name):
        i = ROWS.index(name)
        return self.rows[0:1, i * C:(i + 1) * C]

    def bank(self, i):
        return self.ps[:, i * W:(i + 1) * W]

    def restart(self):
        self.at = 0

    def take(self, *shape):
        n = 1
        for s in shape:
            n *= s
        self.at += n
        assert self.at <= ARENA, (self.at, ARENA)
        v = self.arena[:, self.at - n:self.at]
        if len(shape) == 1:
            return v
        names = "abcde"[:len(shape)]
        return v.rearrange(f"p ({' '.join(names)}) -> p {' '.join(names)}", **dict(zip(names[:-1], shape)))


class Norm:

    def __init__(self, nc, mem, ctx, tag, src, double=False, affine=None, banks=(6, 7)):
        def sem(n):
            return ctx.enter_context(nc.semaphore(f"{tag}_{n}"))

        self.mem, self.src, self.double, self.affine, self.banks = mem, src, double, affine, banks
        self.dve = Steps(sem("dve"), "bn diff square m2 mean var veps " + "inner0 inner1 " * double + "scaled0 scaled1", 1)
        self.pool = Steps(sem("pool"), "r1" + " a b c r2 rstd" * double)
        self.pe = Steps(sem("pe"), "turned0 turned1", 1)
        self.act = Steps(sem("act"), "ready0 ready1", 1)

    def vector_turn(self, dve, it, amax=None):
        m, d, N = self.mem, self.dve, 2 * CH
        stat, tmp = m.bn, m.tmp

        def after(name):
            dve.wait_ge(d.sem, d.done(it, name))

        dve.wait_ge(d.sem, d.done(it - 1, "m2"))
        for n in range(N):
            last = dve.bn_stats(stat[:, n, :], self.src[:, it * N + n, :])
        last.then_inc(d.sem, 1)
        after("bn")
        dve.tensor_tensor(tmp[:, 0, :], stat[:, :, 1], stat[:, :, 4], ALU.subtract).then_inc(d.sem, 1)
        after("diff")
        dve.tensor_tensor(tmp[:, 1, :], tmp[:, 0, :], tmp[:, 0, :], ALU.mult).then_inc(d.sem, 1)
        dve.tensor_tensor(tmp[:, 2, :], stat[:, :, 2], stat[:, :, 5], ALU.add)
        dve.tensor_tensor(tmp[:, 3, :], stat[:, :, 1], stat[:, :, 4], ALU.add).then_inc(d.sem, 1)
        after("m2")
        dve.wait_ge(d.sem, d.done(it - 1, d.names[-1]))
        dve.tensor_scalar(m.mean[:, :], tmp[:, 3, :], 0.5, None, ALU.mult).then_inc(d.sem, 1)
        dve.scalar_tensor_tensor(m.rs[:, 4, :], tmp[:, 1, :], 32.0, tmp[:, 2, :], ALU.mult, ALU.add).then_inc(d.sem, 1)
        after("var")
        dve.tensor_scalar(m.rs[:, 5, :], m.rs[:, 4, :], 1.0 / C, None, ALU.mult)
        dve.tensor_scalar(m.rs[:, 0, :], m.rs[:, 4, :], 1.0 / C, EPS, ALU.mult, ALU.add).then_inc(d.sem, 1)
        dve.wait_ge(self.pool.sem, self.pool.done(it, "rstd" if self.double else "r1"))
        if self.double:
            for p in range(2):
                for j in range(CH):
                    n = p * CH + j
                    last = dve.tensor_scalar(m.xl[:, it * N + n, :], self.src[:, it * N + n, :], m.mean[:, n:n + 1],
                                             m.rs[:, 1, n:n + 1], ALU.subtract, ALU.mult)
                last.then_inc(d.sem, 1)
        r = m.rs[:, 3 if self.double else 1]
        if amax is not None:
            for n in range(N):
                last = dve.tensor_scalar(m.xl[:, it * N + n, :], self.src[:, it * N + n, :], m.mean[:, n:n + 1],
                                         r[:, n:n + 1], ALU.subtract, ALU.mult)
            last.then_inc(d.sem, 1)
            after("scaled0")
            dve.tensor_reduce(amax[:, bass.ds(it, 1)], m.xl[:, bass.ds(it * N, N), :], AX.XY, ALU.max,
                              apply_absolute_value=True).then_inc(d.sem, 1)
            return
        for p in range(2):
            dve.wait_ge(self.pe.sem, self.pe.done(it - 1, f"turned{p}"))
            for j in range(CH):
                n = p * CH + j
                last = dve.tensor_scalar(m.hn[:, p, j, :], self.src[:, it * N + n, :], m.mean[:, n:n + 1],
                                         r[:, n:n + 1], ALU.subtract, ALU.mult)
            last.then_inc(d.sem, 1)

    def pool_turn(self, pool, it):
        m, g = self.mem, self.pool

        def after(name):
            pool.wait_ge(g.sem, g.done(it, name))

        rs = m.rs
        pool.wait_ge(self.dve.sem, self.dve.done(it, "veps"))
        pool.tensor_tensor(rs[:, 1, :], rs[:, 0, :], m.half[:, 0:2 * CH], ALU.pow).then_inc(g.sem, 1)
        if self.double:
            after("r1")
            pool.tensor_tensor(rs[:, 2, :], rs[:, 5, :], rs[:, 1, :], ALU.mult).then_inc(g.sem, 1)
            after("a")
            pool.tensor_tensor(rs[:, 6, :], rs[:, 2, :], rs[:, 1, :], ALU.mult).then_inc(g.sem, 1)
            after("b")
            pool.tensor_tensor(rs[:, 2, :], rs[:, 6, :], m.eps[:, 0:2 * CH], ALU.add).then_inc(g.sem, 1)
            after("c")
            pool.tensor_tensor(rs[:, 6, :], rs[:, 2, :], m.half[:, 0:2 * CH], ALU.pow).then_inc(g.sem, 1)
            after("r2")
            pool.tensor_tensor(rs[:, 3, :], rs[:, 6, :], rs[:, 1, :], ALU.mult).then_inc(g.sem, 1)

    def tensor_turn(self, pe, it):
        m = self.mem
        for p in range(2):
            pe.wait_ge(self.dve.sem, self.dve.done(it, f"scaled{p}"))
            pe.wait_ge(self.act.sem, self.act.done(it - 1, f"ready{p}"))
            for j in range(CH):
                last = pe.transpose(m.bank(self.banks[p])[:, j * T:(j + 1) * T], m.hn[:, p, j, :], m.mat("ident"))
            last.then_inc(self.pe.sem, 1)

    def scalar_turn(self, act, it):
        m = self.mem
        for p in range(2):
            c = (it * 2 + p) * CH
            act.wait_ge(self.pe.sem, self.pe.done(it, f"turned{p}"))
            out = m.hT[:, bass.ds(c, CH), 1:T + 1]
            src = m.bank(self.banks[p]).rearrange("p (b t) -> p b t", b=CH)
            if self.affine:
                ins = act.activation(out, src, ACT.Identity, bias=m.col(self.affine[1]), scale=m.col(self.affine[0]))
            else:
                ins = act.activation(out, src, ACT.Copy)
            ins.then_inc(self.act.sem, 1)


def chunk(buf, it, p):
    return buf[:, bass.ds((it * 2 + p) * CH, CH), :]


def load_block(nc, mem, ctx, x, pack, rows, b_proj):
    loaded = ctx.enter_context(nc.semaphore("loaded"))
    with nc.Block() as block:
        @block.sync
        def _(sp):
            sp.dma_start(mem.x[:, :, :], x.rearrange("b t c -> t b c")).then_inc(loaded, 16)
            sp.dma_start(mem.pack[:, :], pack).then_inc(loaded, 16)
            sp.dma_start(mem.rows[:, :], rows).then_inc(loaded, 16)
            sp.dma_start(mem.b_proj[:, :], b_proj).then_inc(loaded, 16)
            sp.wait_ge(loaded, 64)

        @block.gpsimd
        def _(pool):
            pool.memset(mem.ones[:, :], 1.0)
            pool.memset(mem.half[:, :], -0.5)
            pool.memset(mem.eps[:, :], EPS)
            pool.memset(mem.hT[:, :, 0:1], 0.0)


def time_mix_block(nc, mem, ctx):
    def sem(n):
        return ctx.enter_context(nc.semaphore(n))

    mem.restart()
    PAD = T + 1
    kp = mem.take(B, PAD)
    vT = mem.take(B, T)
    sr = mem.take(B, T)
    mark = mem.at
    mixd = mem.take(W)
    mixed = mem.take(2, 3, W)
    wpad = mem.take(CH, PAD)
    wneg = mem.take(2)
    P = mem.take(2, CH, PAD)
    expo = mem.take(2, 4, CH, T)
    keep = mem.take(2, 2, CH, PAD)
    outw = mem.take(2, 2, CH, T)
    qmax = mem.take(2, CH, T)
    bv = mem.take(2, CH, PAD)
    aa = mem.take(2, CH, PAD)
    bb = mem.take(2, CH, PAD)
    num = mem.take(2, 2, CH, T)
    den = mem.take(CH, T)
    rw = mem.take(2, W)
    top = mem.at
    mem.at = mark + W + 6 * W
    relu = mem.take(CH, W)
    kk = mem.take(2, CH, W)
    gate = mem.take(2, W)
    gated = mem.take(2, W)
    mem.at = max(mem.at, top)

    n1 = Norm(nc, mem, ctx, "n1", mem.x, double=True, affine=("ln1_w", "ln1_b"))
    n2 = Norm(nc, mem, ctx, "n2", mem.xl, affine=("ln2_w", "ln2_b"))
    init = Steps(sem("tm_init_pool"), "kp keep bv wpad")
    idec = Steps(sem("tm_init_act"), "exp")
    iw = Steps(sem("tm_init_dve"), "neg wpad")
    md = Steps(sem("mix_dve"), "d0 k0 v0 r0 d1 k1 v1 r1", 1)
    mp = Steps(sem("mix_pe"), "k0 v0 r0 k1 v1 r1", 1)
    ma = Steps(sem("mix_act"), "k0 v0 r0 k1 v1 r1", 1)
    wd = Steps(sem("wkv_dve"), " ".join(f"P{p} decay{p} q{p} ww{p} aa{p} bb{p} n1{p} n2{p} d1{p} den{p} rec{p} y{p} rw{p}"
                                        for p in range(2)) + " add0 add1", 1)
    wp = Steps(sem("wkv_pool"), " ".join(f"key{p} past{p} bv{p} num{p}" for p in range(2)), 1)
    wa = Steps(sem("wkv_act"), "keep0 outw0 keep1 outw1", 1)
    we = Steps(sem("wkv_pe"), "out0 out1", 1)
    cd = Steps(sem("cm_dve"), "d0 k0 r0 d1 k1 r1 res0 gated0 add0 res1 gated1 add1", 1)
    ce = Steps(sem("cm_pe"), " ".join(f"key{p}{k}" for p in range(2) for k in range(4)) + " rec0 rec1 val0 val1", 1)
    ca = Steps(sem("cm_act"), " ".join(f"relu{p}{k}" for p in range(2) for k in range(4)) + " gate0 gate1", 1)
    cg = Steps(sem("cm_pool"), "kk0 kk1", 1)
    bank = mem.bank

    def batches(v):
        return v.rearrange("p (b t) -> p b t", b=CH)

    with nc.Block() as block:
        @block.gpsimd
        def _(pool):
            pool.memset(kp[:, :, 0:1], NEG).then_inc(init.sem, 1)
            pool.memset(keep[:, :, :, :, :], 0.0).then_inc(init.sem, 1)
            pool.memset(bv[:, :, :, :], 0.0).then_inc(init.sem, 1)
            pool.memset(wpad[:, :, :], NEG).then_inc(init.sem, 1)
            pool.sem_inc(wp.sem, wp.credit())
            pool.sem_inc(cg.sem, cg.credit())
            with pool.Fori(0, NIT) as it:
                n1.pool_turn(pool, it)
            with pool.Fori(0, NIT) as it:
                for p in range(2):
                    past, now = P[:, p, :, 0:T], P[:, p, :, 1:PAD]
                    pool.wait_ge(wd.sem, wd.done(it, f"P{p}"))
                    pool.wait_ge(wa.sem, wa.done(it - 1, f"outw{p}"))
                    pool.tensor_tensor(expo[:, p, 1], chunk(kp, it, p)[:, :, 1:PAD], now, ALU.subtract).then_inc(wp.sem, 1)
                    pool.wait_ge(wd.sem, wd.done(it, f"q{p}"))
                    pool.tensor_tensor(expo[:, p, 2], past, qmax[:, p], ALU.subtract).then_inc(wp.sem, 1)
                    pool.wait_ge(wa.sem, wa.done(it, f"keep{p}"))
                    pool.wait_ge(wd.sem, wd.done(it - 1, f"aa{p}"))
                    pool.tensor_tensor(bv[:, p, :, 1:PAD], keep[:, p, 1, :, 1:PAD], chunk(vT, it, p), ALU.mult).then_inc(wp.sem, 1)
                    pool.wait_ge(wd.sem, wd.done(it, f"n2{p}"))
                    pool.tensor_tensor(num[:, p, 0], num[:, p, 0], num[:, p, 1], ALU.add).then_inc(wp.sem, 1)
            with pool.Fori(0, NIT) as it:
                n2.pool_turn(pool, it)
            with pool.Fori(0, NIT) as it:
                for p in range(2):
                    pool.wait_ge(ca.sem, ca.done(it, f"relu{p}3"))
                    pool.wait_ge(ce.sem, ce.done(it - 1, f"val{p}"))
                    pool.tensor_tensor(kk[:, p], relu[:, :], relu[:, :], ALU.mult).then_inc(cg.sem, 1)

        @block.vector
        def _(dve):
            for s in (n1.dve, n2.dve, md, wd, cd):
                dve.sem_inc(s.sem, s.credit())
            with dve.Fori(0, NIT) as it:
                n1.vector_turn(dve, it)
            dve.wait_ge(idec.sem, 1)
            dve.tensor_scalar(wneg[:, 1:2], wneg[:, 0:1], -1.0, None, ALU.mult).then_inc(iw.sem, 1)
            dve.wait_ge(iw.sem, 1)
            dve.wait_ge(init.sem, 4)
            dve.tensor_scalar(wpad[:, :, 1:PAD],
                              mem.x[:, 0:CH, :], 0.0, wneg[:, 1:2], ALU.mult, ALU.add).then_inc(iw.sem, 1)
            with dve.Fori(0, NIT) as it:
                for p in range(2):
                    hc = chunk(mem.hT, it, p)
                    h, hh = hc[:, :, 1:T + 1], hc[:, :, 0:T]
                    dve.wait_ge(n1.act.sem, n1.act.done(it, f"ready{p}"))
                    dve.wait_ge(md.sem, md.previous(it, p, "r"))
                    dve.tensor_tensor(batches(mixd[:, :]), h, hh, ALU.subtract).then_inc(md.sem, 1)
                    dve.wait_ge(md.sem, md.done(it, f"d{p}"))
                    for i, name in enumerate("kvr"):
                        dve.wait_ge(mp.sem, mp.done(it - 1, f"{name}{p}"))
                        dve.scalar_tensor_tensor(batches(mixed[:, p, i]), batches(mixd[:, :]), mem.col(f"tm{name}"), hh,
                                                 ALU.mult, ALU.add).then_inc(md.sem, 1)
            with dve.Fori(0, NIT) as it:
                for p in range(2):
                    kc, v, past, now = chunk(kp, it, p), chunk(vT, it, p), P[:, p, :, 0:T], P[:, p, :, 1:PAD]
                    k = kc[:, :, 1:PAD]

                    def flat(v):
                        return v.rearrange("p b t -> p (b t)")

                    def after(name):
                        dve.wait_ge(wd.sem, wd.done(it, f"{name}{p}"))

                    dve.wait_ge(ma.sem, ma.done(it, f"r{p}"))
                    dve.wait_ge(iw.sem, 2)
                    dve.wait_ge(wp.sem, wp.done(it - 1, f"past{p}"))
                    dve.tensor_tensor_scan(flat(P[:, p]), flat(wpad), flat(kc), NEG, ALU.add, ALU.max).then_inc(wd.sem, 1)
                    after("P")
                    dve.wait_ge(wa.sem, wa.done(it - 1, f"outw{p}"))
                    dve.scalar_tensor_tensor(expo[:, p, 0], past, wneg[:, 1:2], now, ALU.add, ALU.subtract).then_inc(wd.sem, 1)
                    dve.scalar_tensor_tensor(qmax[:, p], k, mem.col("first"), past, ALU.add, ALU.max).then_inc(wd.sem, 1)
                    after("q")
                    dve.scalar_tensor_tensor(expo[:, p, 3], k, mem.col("first"), qmax[:, p], ALU.add, ALU.subtract).then_inc(wd.sem, 1)
                    dve.wait_ge(wa.sem, wa.done(it, f"keep{p}"))
                    dve.wait_ge(wp.sem, wp.done(it, f"bv{p}"))
                    dve.tensor_tensor_scan(flat(aa[:, p]), flat(keep[:, p, 0]), flat(bv[:, p]), 0.0, ALU.mult, ALU.add).then_inc(wd.sem, 1)
                    dve.tensor_tensor_scan(flat(bb[:, p]), flat(keep[:, p, 0]), flat(keep[:, p, 1]), 0.0, ALU.mult, ALU.add).then_inc(wd.sem, 1)
                    dve.wait_ge(wa.sem, wa.done(it, f"outw{p}"))
                    after("aa")
                    dve.tensor_tensor(num[:, p, 0], outw[:, p, 0], aa[:, p, :, 0:T], ALU.mult).then_inc(wd.sem, 1)
                    dve.tensor_tensor(num[:, p, 1], outw[:, p, 1], v, ALU.mult).then_inc(wd.sem, 1)
                    after("bb")
                    dve.tensor_tensor(den[:, :, :], outw[:, p, 0], bb[:, p, :, 0:T], ALU.mult).then_inc(wd.sem, 1)
                    after("d1")
                    dve.tensor_tensor(den[:, :, :], den[:, :, :], outw[:, p, 1], ALU.add).then_inc(wd.sem, 1)
                    after("den")
                    dve.reciprocal(den[:, :, :], den[:, :, :]).then_inc(wd.sem, 1)
                    after("rec")
                    dve.wait_ge(wp.sem, wp.done(it, f"num{p}"))
                    dve.tensor_tensor(num[:, p, 0], num[:, p, 0], den[:, :, :], ALU.mult).then_inc(wd.sem, 1)
                    after("y")
                    dve.wait_ge(we.sem, we.done(it - 1, f"out{p}"))
                    dve.tensor_tensor(batches(rw[:, p]), num[:, p, 0], chunk(sr, it, p), ALU.mult).then_inc(wd.sem, 1)
                for p in range(2):
                    xl = chunk(mem.xl, it, p)
                    dve.wait_ge(we.sem, we.done(it, f"out{p}"))
                    dve.tensor_tensor(xl, xl, bank(p)[:, :].rearrange("p (b t) -> p b t", b=CH), ALU.add).then_inc(wd.sem, 1)
            dve.wait_ge(wd.sem, wd.done(NIT - 1, "add1"))
            with dve.Fori(0, NIT) as it:
                n2.vector_turn(dve, it)
            with dve.Fori(0, NIT) as it:
                for p in range(2):
                    hc = chunk(mem.hT, it, p)
                    h, hh = hc[:, :, 1:T + 1], hc[:, :, 0:T]
                    dve.wait_ge(n2.act.sem, n2.act.done(it, f"ready{p}"))
                    dve.wait_ge(cd.sem, cd.previous(it, p, "r"))
                    dve.tensor_tensor(batches(mixd[:, :]), h, hh, ALU.subtract).then_inc(cd.sem, 1)
                    dve.wait_ge(cd.sem, cd.done(it, f"d{p}"))
                    dve.wait_ge(ce.sem, ce.done(it - 1, f"rec{p}"))
                    for i, name in enumerate("kr"):
                        dve.scalar_tensor_tensor(batches(mixed[:, p, i]), batches(mixd[:, :]), mem.col(f"ftm{name}"), hh,
                                                 ALU.mult, ALU.add).then_inc(cd.sem, 1)
                for p in range(2):
                    x = chunk(mem.x, it, p)
                    dve.tensor_tensor(x, x, chunk(mem.xl, it, p), ALU.add).then_inc(cd.sem, 1)
                    dve.wait_ge(ca.sem, ca.done(it, f"gate{p}"))
                    dve.wait_ge(ce.sem, ce.done(it, f"val{p}"))
                    dve.tensor_tensor(gated[:, p], gate[:, p], bank(5)[:, :], ALU.mult).then_inc(cd.sem, 1)
                    dve.wait_ge(cd.sem, cd.done(it, f"gated{p}"))
                    dve.tensor_tensor(x, x, batches(gated[:, p]), ALU.add).then_inc(cd.sem, 1)

        @block.scalar
        def _(act):
            for s in (n1.act, n2.act, ma, wa, ca):
                act.sem_inc(s.sem, s.credit())
            act.activation(wneg[:, 0:1], mem.col("decay"), ACT.Exp).then_inc(idec.sem, 1)
            with act.Fori(0, NIT) as it:
                n1.scalar_turn(act, it)
            with act.Fori(0, NIT) as it:
                for p in range(2):
                    act.wait_ge(mp.sem, mp.done(it, f"k{p}"))
                    act.wait_ge(init.sem, 1)
                    act.activation(chunk(kp, it, p)[:, :, 1:PAD], batches(bank(p)[:, :]), ACT.Copy).then_inc(ma.sem, 1)
                    act.wait_ge(mp.sem, mp.done(it, f"v{p}"))
                    act.activation(chunk(vT, it, p), batches(bank(2 + p)[:, :]), ACT.Copy).then_inc(ma.sem, 1)
                    act.wait_ge(mp.sem, mp.done(it, f"r{p}"))
                    act.activation(chunk(sr, it, p), batches(bank(4 + p)[:, :]), ACT.Sigmoid).then_inc(ma.sem, 1)
            with act.Fori(0, NIT) as it:
                for p in range(2):
                    act.wait_ge(init.sem, 3)
                    act.wait_ge(wd.sem, wd.done(it, f"decay{p}"))
                    act.wait_ge(wp.sem, wp.done(it, f"key{p}"))
                    act.wait_ge(wd.sem, wd.done(it - 1, f"bb{p}"))
                    act.activation(keep[:, p].rearrange("p a b t -> p (a b) t")[:, :, 1:PAD],
                                   expo[:, p, 0:2].rearrange("p a b t -> p (a b) t"), ACT.Exp).then_inc(wa.sem, 1)
                    act.wait_ge(wd.sem, wd.done(it, f"ww{p}"))
                    act.wait_ge(wp.sem, wp.done(it, f"past{p}"))
                    act.wait_ge(wd.sem, wd.done(it - 1, f"den{p}"))
                    act.activation(outw[:, p].rearrange("p a b t -> p (a b t)"),
                                   expo[:, p, 2:4].rearrange("p a b t -> p (a b t)"), ACT.Exp).then_inc(wa.sem, 1)
            with act.Fori(0, NIT) as it:
                n2.scalar_turn(act, it)
            with act.Fori(0, NIT) as it:
                for p in range(2):
                    if p == 0:
                        act.wait_ge(cg.sem, cg.done(it - 1, "kk1"))
                    else:
                        act.wait_ge(cg.sem, cg.done(it, "kk0"))
                    for k in range(4):
                        act.wait_ge(ce.sem, ce.done(it, f"key{p}{k}"))
                        act.activation(relu[:, k], bank(k)[:, :], ACT.Relu).then_inc(ca.sem, 1)
                for p in range(2):
                    act.wait_ge(ce.sem, ce.done(it, f"rec{p}"))
                    act.wait_ge(cd.sem, cd.done(it - 1, f"gated{p}"))
                    act.activation(gate[:, p], bank(4)[:, :], ACT.Sigmoid).then_inc(ca.sem, 1)

        @block.tensor
        def _(pe):
            for s in (n1.pe, n2.pe, mp, we, ce):
                pe.sem_inc(s.sem, s.credit())
            with pe.Fori(0, NIT) as it:
                n1.tensor_turn(pe, it)
            with pe.Fori(0, NIT) as it:
                for p in range(2):
                    for i, name in enumerate("kvr"):
                        pe.wait_ge(md.sem, md.done(it, f"{name}{p}"))
                        pe.wait_ge(ma.sem, ma.done(it - 1, f"{name}{p}"))
                        pe.matmul(bank(2 * i + p)[:, :], mem.mat(f"W{name}T"), mixed[:, p, i], start=True, stop=True).then_inc(mp.sem, 1)
            with pe.Fori(0, NIT) as it:
                for p in range(2):
                    pe.wait_ge(wd.sem, wd.done(it, f"rw{p}"))
                    pe.wait_ge(wd.sem, wd.done(it - 1, f"add{p}"))
                    for j in range(CH):
                        last = pe.matmul(bank(p)[:, j * T:(j + 1) * T], rw[:, p, j * T:(j + 1) * T], mem.mat("WoT"),
                                         start=True, stop=True)
                    last.then_inc(we.sem, 1)
            with pe.Fori(0, NIT) as it:
                n2.tensor_turn(pe, it)
            with pe.Fori(0, NIT) as it:
                for p in range(2):
                    pe.wait_ge(cd.sem, cd.done(it, f"k{p}"))
                    for k in range(4):
                        if p == 0:
                            pe.wait_ge(ca.sem, ca.done(it - 1, f"relu1{k}"))
                        else:
                            pe.wait_ge(ca.sem, ca.done(it, f"relu0{k}"))
                        pe.matmul(bank(k)[:, :], mem.mat("WkeyT", k), mixed[:, p, 0], start=True, stop=True).then_inc(ce.sem, 1)
                for p in range(2):
                    pe.wait_ge(cd.sem, cd.done(it, f"r{p}"))
                    if p == 0:
                        pe.wait_ge(ca.sem, ca.done(it - 1, "gate1"))
                    else:
                        pe.wait_ge(ca.sem, ca.done(it, "gate0"))
                    for j in range(CH):
                        last = pe.matmul(bank(4)[:, j * T:(j + 1) * T], mixed[:, p, 1, j * T:(j + 1) * T], mem.mat("WrecT"),
                                         start=True, stop=True)
                    last.then_inc(ce.sem, 1)
                for p in range(2):
                    pe.wait_ge(cg.sem, cg.done(it, f"kk{p}"))
                    if p == 0:
                        pe.wait_ge(cd.sem, cd.done(it - 1, "gated1"))
                    else:
                        pe.wait_ge(cd.sem, cd.done(it, "gated0"))
                    for j in range(CH):
                        for k in range(4):
                            last = pe.matmul(bank(5)[:, j * T:(j + 1) * T], kk[:, p, k, j * T:(j + 1) * T],
                                             mem.mat("WvalT", k), start=(k == 0), stop=(k == 3))
                    last.then_inc(ce.sem, 1)


KEPT_WORDS = B * S + B * C
KV_WORDS = 2 * KEPT_WORDS


def kv_views(mem):
    keys, values = [None, None], [None, None]
    for l in range(2):
        o = 0 if l == 1 else KEPT_WORDS
        keys[l] = mem.arena[:, o:o + B * S].rearrange("p (b s) -> p b s", b=B)
        values[l] = mem.arena[:, o + B * S:o + KEPT_WORDS].rearrange("p (b c) -> p b c", b=B)
    return keys, values


def context_block(nc, mem, ctx, tokens):
    def sem(n):
        return ctx.enter_context(nc.semaphore(n))

    keys, values = kv_views(mem)
    mem.at = KV_WORDS
    cn = mem.take(2, CH, C)
    cT = mem.take(2, CH * S)
    loaded = [sem("ctx_loaded0"), sem("ctx_loaded1")]
    e = Steps(sem("kv_pe"), " ".join(f"turned{p} k0{p} k1{p} v0{p} v1{p}" for p in range(2)), 1)
    a = Steps(sem("kv_act"), " ".join(f"cT{p} k0{p} v0{p}" for p in range(2)), 1)
    d = Steps(sem("kv_dve"), " ".join(f"k1{p} v1{p}" for p in range(2)), 1)
    src = tokens.rearrange("b s c -> s b c")

    with nc.Block() as block:
        @block.sync
        def _(sp):
            with sp.Fori(0, NIT) as it:
                for p in range(2):
                    sp.wait_ge(e.sem, e.done(it - 1, f"turned{p}"))
                    sp.dma_start(cn[0:S, p], src[:, bass.ds((it * 2 + p) * CH, CH), :]).then_inc(loaded[p], 16)

        @block.tensor
        def _(pe):
            pe.sem_inc(e.sem, e.credit())
            with pe.Fori(0, NIT) as it:
                for p in range(2):
                    pe.wait_ge(loaded[p], it * 16 + 16)
                    pe.wait_ge(a.sem, a.previous(it, p, "cT"))
                    for j in range(CH):
                        last = pe.transpose(mem.bank(4)[:, j * S:(j + 1) * S], cn[0:S, p, j, :], mem.mat("ident")[0:S, 0:S])
                    last.then_inc(e.sem, 1)
                    pe.wait_ge(a.sem, a.done(it, f"cT{p}"))
                    pe.wait_ge(a.sem, a.previous(it, p, "k0"))
                    pe.matmul(mem.bank(0)[:, 0:CH * S], mem.mat("kT0"), cT[:, p], start=True, stop=True).then_inc(e.sem, 1)
                    pe.wait_ge(d.sem, d.previous(it, p, "k1"))
                    pe.matmul(mem.bank(1)[:, 0:CH * S], mem.mat("kT1"), cT[:, p], start=True, stop=True).then_inc(e.sem, 1)
                    pe.wait_ge(a.sem, a.previous(it, p, "v0"))
                    for j in range(CH):
                        out = mem.bank(2)[0:S, j * C:(j + 1) * C]
                        pe.matmul(out, cT[:, p, j * S:(j + 1) * S], mem.mat("vT0"), start=True, stop=False)
                        last = pe.matmul(out, mem.ones[0:1, 0:S], mem.row("bv"), start=False, stop=True)
                    last.then_inc(e.sem, 1)
                    pe.wait_ge(d.sem, d.previous(it, p, "v1"))
                    for j in range(CH):
                        last = pe.matmul(mem.bank(3)[0:S, j * C:(j + 1) * C], cT[:, p, j * S:(j + 1) * S], mem.mat("vT1"),
                                         start=True, stop=True)
                    last.then_inc(e.sem, 1)

        @block.scalar
        def _(act):
            act.sem_inc(a.sem, a.credit())
            with act.Fori(0, NIT) as it:
                for p in range(2):
                    act.wait_ge(e.sem, e.done(it, f"turned{p}"))
                    act.wait_ge(e.sem, e.done(it - 1, f"v1{p}"))
                    act.activation(cT[:, p], mem.bank(4)[:, 0:CH * S], ACT.Copy).then_inc(a.sem, 1)
                    act.wait_ge(e.sem, e.done(it, f"k0{p}"))
                    act.activation(chunk(keys[0], it, p), mem.bank(0)[:, 0:CH * S].rearrange("p (b s) -> p b s", b=CH),
                                   ACT.Identity, bias=mem.col("bk")).then_inc(a.sem, 1)
                    act.wait_ge(e.sem, e.done(it, f"v0{p}"))
                    act.activation(chunk(values[0][0:S], it, p), mem.bank(2)[0:S, :].rearrange("p (b c) -> p b c", b=CH),
                                   ACT.Copy).then_inc(a.sem, 1)

        @block.vector
        def _(dve):
            dve.sem_inc(d.sem, d.credit())
            with dve.Fori(0, NIT) as it:
                for p in range(2):
                    dve.wait_ge(e.sem, e.done(it, f"k1{p}"))
                    dve.tensor_copy(chunk(keys[1], it, p), mem.bank(1)[:, 0:CH * S].rearrange("p (b s) -> p b s", b=CH)).then_inc(d.sem, 1)
                    dve.wait_ge(e.sem, e.done(it, f"v1{p}"))
                    dve.tensor_copy(chunk(values[1][0:S], it, p), mem.bank(3)[0:S, :].rearrange("p (b c) -> p b c", b=CH)).then_inc(d.sem, 1)


def attention_block(nc, mem, ctx, layer, v_mask_in):
    def sem(n):
        return ctx.enter_context(nc.semaphore(f"at{layer}_{n}"))

    causal = layer == 0
    keys, values = kv_views(mem)
    kT, vals = keys[layer], values[layer]
    mem.at = KV_WORDS
    NB = 2 * CH
    HS = H * S
    qT = mem.take(2, W)
    km = mem.take(2, H, S)
    vm = mem.take(2, 4, C)
    v_mask = mem.take(4, C)
    shifted = mem.take(2, H, S)
    mx = mem.take(2, H)
    prob = mem.take(2, H, S)
    pT = mem.take(2, 8, T)
    rden = mem.take(T)
    oT = mem.take(2, CH, T)
    causal_b = mem.take(4 * S // 2).bitcast(BF16)
    ident_b = mem.take(64).bitcast(BF16)
    norm = Norm(nc, mem, ctx, f"at{layer}n", mem.x)
    masks = sem("masks")
    setup = sem("setup")

    def turn(first, rest, last):
        out = []
        for n in range(NB):
            out += [s.format(n=n, p=n // CH) for s in first(n)]
            if n:
                out += [s.format(n=n - 1) for s in rest]
            if n == CH:
                out += [s.format(p=0) for s in last]
        return " ".join(out + [s.format(n=NB - 1) for s in rest] + [s.format(p=1) for s in last])

    e = Steps(sem("pe"), turn(lambda n: ["q{p}"] * (n % CH == 0) + ["S{n}"], ["Ta{n}", "Tb{n}", "O{n}"], ["out{p}"]), 1)
    d = Steps(sem("dve"), turn(lambda n: ["max{n}", "sub{n}"], ["pb{n}", "rec{n}", "o{n}"], ["add{p}"]), 1)
    a = Steps(sem("act"), " ".join([f"q{n // CH} " * (n % CH == 0) + (f"pa{n - 1} " if n else "") + f"exp{n}"
                                    for n in range(NB)] + [f"pa{NB - 1}"]), 1)
    g = Steps(sem("pool"), " ".join(f"km{n} vm{n}" for n in range(NB)), 1)
    bank = mem.bank
    scores = mem.ps[:, 0:4 * W].rearrange("p (g w) -> p g w", g=4)[:, :, 0:4 * S].rearrange("p g (j s) -> p g j s", j=4)
    turned = mem.ps[0:S, 4 * W:6 * W]

    def by_group(v):
        return v.rearrange("p (g j) s -> p g j s", g=4)

    def n_of(steps, it, name, n):
        return steps.done(it, f"{name}{n}") if n >= 0 else steps.done(it - 1, f"{name}{n + NB}")

    with nc.Block() as block:
        @block.sync
        def _(sp):
            sp.dma_start(v_mask[:, :, :], v_mask_in).then_inc(masks, 16)
            sp.wait_ge(masks, 16)

        @block.gpsimd
        def _(pool):
            pool.sem_inc(g.sem, g.credit())
            pool.wait_ge(masks, 16)
            with pool.Fori(0, NIT) as it:
                norm.pool_turn(pool, it)
            with pool.Fori(0, NIT) as it:
                for n in range(NB):
                    p, b = n // CH, n % CH
                    at = (it * 2 + p) * CH + b
                    pool.wait_ge(e.sem, n_of(e, it, "S", n - 2))
                    pool.tensor_tensor(km[:, n % 2], kT[:, bass.ds(at, 1), :].broadcast_to([128, H, S]),
                                       mem.mat("head_mask", 0, H).unsqueeze(2).broadcast_to([128, H, S]), ALU.mult).then_inc(g.sem, 1)
                    pool.wait_ge(e.sem, n_of(e, it, "O", n - 2))
                    vc = vals[0:S, bass.ds(at, 1), :]
                    pool.tensor_tensor(vm[0:S, n % 2], vc.broadcast_to([S, 4, C]), v_mask[0:S], ALU.mult).then_inc(g.sem, 1)

        @block.vector
        def _(dve):
            for s in (norm.dve, d):
                dve.sem_inc(s.sem, s.credit())
            if causal:
                dve.tensor_copy(causal_b.rearrange("p (j s) -> p j s", j=4),
                                mem.mat("causal", 0, S).unsqueeze(1).broadcast_to([128, 4, S])).then_inc(setup, 1)
                dve.tensor_copy(ident_b, mem.mat("ident")).then_inc(setup, 1)
            with dve.Fori(0, NIT) as it:
                norm.vector_turn(dve, it)
            with dve.Fori(0, NIT) as it:
                def finish(n):
                    p = n // CH
                    dve.wait_ge(e.sem, e.done(it, f"Tb{n}"))
                    dve.wait_ge(e.sem, n_of(e, it, "O", n - 1))
                    dve.tensor_copy(pT[0:S, 1].rearrange("p h t -> p (h t)"), turned).then_inc(d.sem, 1)
                    dve.wait_ge(e.sem, e.done(it, f"O{n}"))
                    dve.wait_ge(d.sem, n_of(d, it, "o", n - 1))
                    dve.reciprocal(rden[:, :], bank(7)[:, 0:T]).then_inc(d.sem, 1)
                    dve.wait_ge(d.sem, d.done(it, f"rec{n}"))
                    dve.wait_ge(e.sem, e.done(it - 1, f"out{p}"))
                    dve.tensor_tensor(oT[:, p, n % CH], bank(6)[:, 0:T], rden[:, :], ALU.mult).then_inc(d.sem, 1)

                def add(p):
                    x = chunk(mem.x, it, p)
                    dve.wait_ge(e.sem, e.done(it, f"out{p}"))
                    dve.tensor_tensor(x, x, bank(6)[:, :].rearrange("p (b c) -> p b c", b=CH), ALU.add).then_inc(d.sem, 1)

                for n in range(NB):
                    dve.wait_ge(e.sem, e.done(it, f"S{n}"))
                    dve.wait_ge(d.sem, n_of(d, it, "sub", n - 2))
                    dve.tensor_reduce(by_group(mx[:, n % 2].unsqueeze(2))[:, :, :, 0], scores, AX.X, ALU.max).then_inc(d.sem, 1)
                    dve.wait_ge(d.sem, d.done(it, f"max{n}"))
                    dve.wait_ge(a.sem, n_of(a, it, "exp", n - 2))
                    dve.tensor_tensor(by_group(shifted[:, n % 2]), scores,
                                      by_group(mx[:, n % 2].unsqueeze(2).broadcast_to([128, H, S])), ALU.subtract).then_inc(d.sem, 1)
                    if n:
                        finish(n - 1)
                    if n == CH:
                        add(0)
                finish(NB - 1)
                add(1)

        @block.scalar
        def _(act):
            for s in (norm.act, a):
                act.sem_inc(s.sem, s.credit())
            with act.Fori(0, NIT) as it:
                norm.scalar_turn(act, it)
            with act.Fori(0, NIT) as it:
                def first_half(n):
                    act.wait_ge(e.sem, e.done(it, f"Ta{n}"))
                    act.wait_ge(e.sem, n_of(e, it, "O", n - 1))
                    act.activation(pT[0:S, 0].rearrange("p h t -> p (h t)"), turned, ACT.Copy).then_inc(a.sem, 1)

                for n in range(NB):
                    p = n // CH
                    if n % CH == 0:
                        act.wait_ge(e.sem, e.done(it, f"q{p}"))
                        act.wait_ge(e.sem, e.done(it - 1, f"S{CH * p + CH - 1}"))
                        if causal:
                            ins = act.activation(qT[:, p], bank(7)[:, :], ACT.Identity, bias=mem.col("bq"))
                        else:
                            ins = act.activation(qT[:, p], bank(7)[:, :], ACT.Copy)
                        ins.then_inc(a.sem, 1)
                    if n:
                        first_half(n - 1)
                    act.wait_ge(d.sem, d.done(it, f"sub{n}"))
                    act.wait_ge(e.sem, n_of(e, it, "Tb", n - 2))
                    act.activation(prob[:, n % 2].rearrange("p h s -> p (h s)"), shifted[:, n % 2].rearrange("p h s -> p (h s)"),
                                   ACT.Exp, scale=ATT_SCALE).then_inc(a.sem, 1)
                first_half(NB - 1)

        @block.tensor
        def _(pe):
            for s in (norm.pe, e):
                pe.sem_inc(s.sem, s.credit())
            with pe.Fori(0, NIT) as it:
                norm.tensor_turn(pe, it)
            pe.wait_ge(norm.act.sem, norm.act.done(NIT - 1, "ready1"))
            if causal:
                pe.wait_ge(setup, 2)
            with pe.Fori(0, NIT) as it:
                def finish(n):
                    pe.wait_ge(a.sem, a.done(it, f"exp{n}"))
                    pe.wait_ge(d.sem, n_of(d, it, "pb", n - 1))
                    for half in range(2):
                        if half:
                            pe.wait_ge(a.sem, a.done(it, f"pa{n}"))
                        for k in range(8):
                            j, grp = 2 * half + k // 4, k % 4
                            last = pe.transpose(turned[:, k * T:(k + 1) * T], prob[:, n % 2, 4 * grp + j, :], mem.mat("ident"))
                        last.then_inc(e.sem, 1)
                    pe.wait_ge(g.sem, g.done(it, f"vm{n}"))
                    pe.wait_ge(d.sem, d.done(it, f"pb{n}"))
                    pe.wait_ge(d.sem, n_of(d, it, "o", n - 1))
                    if n % CH == 0:
                        pe.wait_ge(d.sem, d.done(it, "add0") if n else d.done(it - 1, "add1"))
                        pe.wait_ge(a.sem, a.done(it, f"q{n // CH}"))
                    for j in range(4):
                        for grp in range(4):
                            rows = slice(32 * grp, 32 * grp + 32)
                            last = pe.matmul(bank(6)[rows, 0:T], vm[0:S, n % 2, j, rows], pT[0:S, j // 2, (j % 2) * 4 + grp],
                                             start=(j == 0), stop=(j == 3))
                    for j in range(4):
                        for grp in range(4):
                            rows = slice(32 * grp, 32 * grp + 32)
                            last = pe.matmul(bank(7)[rows, 0:T], v_mask[0:S, j, 0:32], pT[0:S, j // 2, (j % 2) * 4 + grp],
                                             start=(j == 0), stop=(j == 3))
                    last.then_inc(e.sem, 1)

                def project(p):
                    pe.wait_ge(d.sem, d.done(it, f"o{CH * p + CH - 1}"))
                    for j in range(CH):
                        out = bank(6)[:, j * C:(j + 1) * C]
                        pe.matmul(out, oT[:, p, j], mem.mat(f"oT{layer}"), start=True, stop=False)
                        last = pe.matmul(out, mem.ones[0:1, :], mem.row(f"bo{layer}"), start=False, stop=True)
                    last.then_inc(e.sem, 1)

                for n in range(NB):
                    p, b = n // CH, n % CH
                    if b == 0:
                        pe.wait_ge(d.sem, n_of(d, it, "o", n - 2 if n else n - 1))
                        pe.matmul(bank(7)[:, :].rearrange("p (b t) -> p b t", b=CH), mem.mat(f"qT{layer}"),
                                  chunk(mem.hT, it, p)[:, :, 1:T + 1], start=True, stop=True).then_inc(e.sem, 1)
                        pe.wait_ge(a.sem, a.done(it, f"q{p}"))
                    pe.wait_ge(g.sem, g.done(it, f"km{n}"))
                    pe.wait_ge(d.sem, n_of(d, it, "sub", n - 1))
                    for grp in range(4):
                        out = bank(grp)[:, 0:4 * S]
                        last = pe.matmul(out, qT[:, p, b * T:(b + 1) * T],
                                         km[:, n % 2, 4 * grp:4 * grp + 4].rearrange("p j s -> p (j s)"),
                                         start=True, stop=not causal)
                        if causal:
                            last = pe.matmul(out, ident_b, causal_b, start=False, stop=True)
                    last.then_inc(e.sem, 1)
                    if n:
                        finish(n - 1)
                    if n == CH:
                        project(0)
                finish(NB - 1)
                project(1)


def experts_block(nc, mem, ctx, w_fc, w_proj):
    def sem(n):
        return ctx.enter_context(nc.semaphore(f"moe_{n}"))

    mem.at = KEPT_WORDS
    fc = mem.take(E, 4, 128)
    proj = mem.take(E, 4, C)
    hid = mem.take(2, 4, W)
    part = mem.take(2, W)
    lgT = mem.take(2, W)
    lg = mem.take(B, E)
    one1 = mem.take(B, E)
    one2 = mem.take(B, E)
    cand = mem.take(B, E)
    comb = mem.take(B, E)
    best = mem.take(6, B)
    cs = mem.take(2, CH, E)
    cT = mem.take(2, W)
    norm = Norm(nc, mem, ctx, "moen", mem.x)
    weights = sem("weights")
    re_ = Steps(sem("route_pe"), "logit0 turned0 logit1 turned1", 1)
    ra = Steps(sem("route_act"), "lgT0 lgT1", 1)
    rd = Steps(sem("route_dve"), "lg0 lg1", 1)
    top = sem("top")
    gap = sem("gap")
    XP = [f"{s}{e}" for e in range(E) for s in ("part", "add")]
    e_ = Steps(sem("pe"), "cT bias " + " ".join(" ".join(f"f{e}{k}" for k in range(4)) + (f" y{e - 1}" if e else "")
                                               for e in range(E)) + f" y{E - 1}", 1)
    a_ = Steps(sem("act"), "cT " + " ".join(f"h{e}{k}" for e in range(E) for k in range(4)), 1)
    d_ = Steps(sem("dve"), "cs bias " + " ".join(XP), 1)
    bank = mem.bank

    def wide(v):
        return v.unsqueeze(2).broadcast_to([128, B, E])

    with nc.Block() as block:
        @block.sync
        def _(sp):
            sp.dma_start(fc.rearrange("p e k h -> p (e k h)"), w_fc).then_inc(weights, 16)
            sp.dma_start(proj.rearrange("p e k c -> p (e k c)"), w_proj).then_inc(weights, 16)
            sp.wait_ge(weights, 32)

        @block.gpsimd
        def _(pool):
            with pool.Fori(0, NIT) as it:
                norm.pool_turn(pool, it)

        @block.vector
        def _(dve):
            for s in (norm.dve, rd, d_):
                dve.sem_inc(s.sem, s.credit())
            with dve.Fori(0, NIT) as it:
                norm.vector_turn(dve, it)
            with dve.Fori(0, NIT) as it:
                for p in range(2):
                    dve.wait_ge(re_.sem, re_.done(it, f"turned{p}"))
                    dve.tensor_copy(chunk(lg, it, p), bank(2 + p)[:, 0:CH * E].rearrange("p (b e) -> p b e", b=CH)).then_inc(rd.sem, 1)
            rank = mem.mat("rank", 0, E).unsqueeze(1).broadcast_to([128, B, E])
            dve.wait_ge(rd.sem, rd.done(NIT - 1, "lg1"))
            n = 0
            for k, one in enumerate((one1, one2)):
                src = lg if k == 0 else cand
                dve.tensor_reduce(best[:, 3 * k, :], src[:, :, :], AX.X, ALU.max).then_inc(top, 1)
                n += 1
                dve.wait_ge(top, n)
                dve.tensor_tensor(one, src, wide(best[:, 3 * k, :]), ALU.is_equal).then_inc(top, 1)
                n += 1
                dve.wait_ge(top, n)
                dve.tensor_tensor(one, one, rank, ALU.mult).then_inc(top, 1)
                n += 1
                dve.wait_ge(top, n)
                dve.tensor_reduce(best[:, 3 * k + 1, :], one[:, :, :], AX.X, ALU.max).then_inc(top, 1)
                n += 1
                dve.wait_ge(top, n)
                dve.tensor_tensor(one, rank, wide(best[:, 3 * k + 1, :]), ALU.is_equal).then_inc(top, 1)
                n += 1
                dve.wait_ge(top, n)
                if k == 0:
                    dve.scalar_tensor_tensor(cand, one, -1e30, lg, ALU.mult, ALU.add).then_inc(top, 1)
                    n += 1
                    dve.wait_ge(top, n)
            dve.tensor_tensor(best[:, 2, :], best[:, 3, :], best[:, 0, :], ALU.subtract).then_inc(top, 1)
            n += 1
            dve.wait_ge(gap, 1)
            dve.tensor_scalar(best[:, 4, :], best[:, 5, :], 1.0, None, ALU.add).then_inc(top, 1)
            n += 1
            dve.wait_ge(top, n)
            dve.reciprocal(best[:, 1, :], best[:, 4, :]).then_inc(top, 1)
            n += 1
            dve.wait_ge(top, n)
            dve.tensor_tensor(best[:, 2, :], best[:, 5, :], best[:, 1, :], ALU.mult).then_inc(top, 1)
            dve.tensor_tensor(one1, one1, wide(best[:, 1, :]), ALU.mult).then_inc(top, 1)
            n += 2
            dve.wait_ge(top, n)
            dve.tensor_tensor(one2, one2, wide(best[:, 2, :]), ALU.mult).then_inc(top, 1)
            n += 1
            dve.wait_ge(top, n)
            dve.tensor_tensor(comb, one1, one2, ALU.add).then_inc(top, 1)
            n += 1
            dve.wait_ge(top, n)
            with dve.Fori(0, NCH) as it:
                dve.wait_ge(e_.sem, e_.done(it - 1, "cT"))
                dve.tensor_copy(cs[:, 0], comb[:, bass.ds(it * CH, CH), :]).then_inc(d_.sem, 1)
                x = mem.x[:, bass.ds(it * CH, CH), :]
                dve.wait_ge(e_.sem, e_.done(it, "bias"))
                dve.tensor_tensor(x, x, bank(7).rearrange("p (b c) -> p b c", b=CH), ALU.add).then_inc(d_.sem, 1)
                for e in range(E):
                    dve.wait_ge(e_.sem, e_.done(it, f"y{e}"))
                    dve.wait_ge(d_.sem, d_.done(it, f"add{e - 2}") if e > 1 else d_.done(it - 1, f"add{e + E - 2}"))
                    dve.tensor_tensor(part[:, e % 2].rearrange("p (b c) -> p b c", b=CH),
                                      bank(4 + e % 2).rearrange("p (b c) -> p b c", b=CH),
                                      cs[:, 0, :, e:e + 1].broadcast_to([128, CH, C]), ALU.mult).then_inc(d_.sem, 1)
                    dve.wait_ge(d_.sem, d_.done(it, f"part{e}"))
                    dve.tensor_tensor(x, x, part[:, e % 2].rearrange("p (b c) -> p b c", b=CH), ALU.add).then_inc(d_.sem, 1)

        @block.scalar
        def _(act):
            for s in (norm.act, ra, a_):
                act.sem_inc(s.sem, s.credit())
            with act.Fori(0, NIT) as it:
                norm.scalar_turn(act, it)
            with act.Fori(0, NIT) as it:
                for p in range(2):
                    act.wait_ge(re_.sem, re_.done(it, f"logit{p}"))
                    act.wait_ge(re_.sem, re_.done(it - 1, f"turned{p}"))
                    act.activation(lgT[0:E, p], bank(p)[0:E, :], ACT.Copy).then_inc(ra.sem, 1)
            act.wait_ge(top, 12)
            act.activation(best[:, 5, :], best[:, 2, :], ACT.Exp).then_inc(gap, 1)
            with act.Fori(0, NCH) as it:
                act.wait_ge(e_.sem, e_.done(it, "cT"))
                act.wait_ge(e_.sem, e_.done(it - 1, "bias"))
                act.activation(cT[0:E, 0], bank(6)[0:E, :], ACT.Copy).then_inc(a_.sem, 1)
                for e in range(E):
                    for k in range(4):
                        act.wait_ge(e_.sem, e_.done(it, f"f{e}{k}"))
                        if k == 0:
                            act.wait_ge(e_.sem, e_.done(it, f"y{e - 2}") if e > 1 else e_.done(it - 1, f"y{e + E - 2}"))
                        act.activation(hid[:, e % 2, k], bank(k), ACT.Gelu_apprx_tanh, bias=mem.col("b_fc", e * 4 + k)).then_inc(a_.sem, 1)

        @block.tensor
        def _(pe):
            for s in (norm.pe, re_, e_):
                pe.sem_inc(s.sem, s.credit())
            with pe.Fori(0, NIT) as it:
                norm.tensor_turn(pe, it)
            with pe.Fori(0, NIT) as it:
                for p in range(2):
                    pe.wait_ge(norm.act.sem, norm.act.done(it, f"ready{p}"))
                    pe.wait_ge(ra.sem, ra.done(it - 1, f"lgT{p}"))
                    pe.matmul(bank(p)[0:E, :].rearrange("p (b t) -> p b t", b=CH), mem.mat("router", 0, E),
                              chunk(mem.hT, it, p)[:, :, 1:T + 1], start=True, stop=True).then_inc(re_.sem, 1)
                    pe.wait_ge(ra.sem, ra.done(it, f"lgT{p}"))
                    pe.wait_ge(rd.sem, rd.done(it - 1, f"lg{p}"))
                    for j in range(CH):
                        last = pe.matmul(bank(2 + p)[:, j * E:(j + 1) * E], lgT[0:E, p, j * T:(j + 1) * T],
                                         mem.mat("ident")[0:E, 0:E], start=True, stop=True)
                    last.then_inc(re_.sem, 1)
            pe.wait_ge(weights, 32)
            with pe.Fori(0, NCH) as it:
                def outputs(e):
                    pe.wait_ge(a_.sem, a_.done(it, f"h{e}3"))
                    pe.wait_ge(d_.sem, d_.done(it, f"part{e - 2}") if e > 1 else d_.done(it - 1, f"part{e + E - 2}"))
                    for j in range(CH):
                        for k in range(4):
                            last = pe.matmul(bank(4 + e % 2)[:, j * C:(j + 1) * C], hid[:, e % 2, k, j * T:(j + 1) * T], proj[:, e, k],
                                             start=(k == 0), stop=(k == 3))
                    last.then_inc(e_.sem, 1)

                pe.wait_ge(d_.sem, d_.done(it, "cs"))
                pe.wait_ge(a_.sem, a_.done(it - 1, "cT"))
                for j in range(CH):
                    last = pe.transpose(bank(6)[0:E, j * T:(j + 1) * T], cs[:, 0, j, :], mem.mat("ident"))
                last.then_inc(e_.sem, 1)
                pe.wait_ge(a_.sem, a_.done(it, "cT"))
                pe.wait_ge(d_.sem, d_.done(it - 1, "bias"))
                for j in range(CH):
                    last = pe.matmul(bank(7)[:, j * C:(j + 1) * C], cT[0:E, 0, j * T:(j + 1) * T], mem.b_proj[:, :], start=True, stop=True)
                last.then_inc(e_.sem, 1)
                for e in range(E):
                    for k in range(4):
                        pe.wait_ge(a_.sem, a_.done(it, f"h{e - 1}{k}") if e else a_.done(it - 1, f"h{E - 1}{k}"))
                        pe.matmul(bank(k).rearrange("p (b t) -> p b t", b=CH), fc[:, e, k],
                                  mem.hT[:, bass.ds(it * CH, CH), 1:T + 1], start=True, stop=True).then_inc(e_.sem, 1)
                    if e:
                        outputs(e - 1)
                outputs(E - 1)


def state_space_block(nc, mem, ctx):
    def sem(n):
        return ctx.enter_context(nc.semaphore(f"ssm_{n}"))

    mem.at = KEPT_WORDS
    xp = mem.take(B, T + 2)
    gt = mem.take(B, T)
    mix = mem.take(B, T)
    dz = mem.take(B, T)
    bm = mem.take(B, T)
    ct = mem.take(B, T)
    neg_a = mem.take(2)
    tb = mem.take(2, CH, T)
    top = mem.at
    mem.at = KEPT_WORDS
    soft = mem.take(2, 2, CH, T)
    mem.at = top
    decay, u = tb[:, 0], tb[:, 1]
    state = mem.take(CH, T)
    yT = mem.hn[:, :, :, :].rearrange("p a b c -> p a (b c)")
    mem.at = KEPT_WORDS
    act1 = mem.take(2, 2, W)
    n4 = Norm(nc, mem, ctx, "ssmn", mem.x, double=True, affine=("m_ln1_g", "m_ln1_b"))
    n5 = Norm(nc, mem, ctx, "ffn", mem.xl, affine=("m_ln2_g", "m_ln2_b"))
    init = sem("init")
    ie = Steps(sem("in_pe"), "x0 g0 x1 g1", 1)
    ia = Steps(sem("in_act"), "x0 g0 x1 g1", 1)
    cd = Steps(sem("conv_dve"), "a0 b0 c0 a1 b1 c1")
    ce = Steps(sem("conv_pe"), "dt0 b0 c0 dt1 b1 c1", 1)
    ca = Steps(sem("conv_act"), "dt0 b0 c0 dt1 b1 c1", 1)
    cg = Steps(sem("conv_pool"), "bm0 bm1", 1)
    sa = Steps(sem("scan_act"), "neg0 exp0 ln0 decay0 neg1 exp1 ln1 decay1", 1)
    sd = Steps(sem("scan_dve"), " ".join(f"dt{p} start{p} state{p} cs{p} skip{p} y{p} add{p}" for p in range(2)), 1)
    sg = Steps(sem("scan_pool"), "u0 u1", 1)
    se = Steps(sem("scan_pe"), "out0 out1", 1)
    fe = Steps(sem("ff_pe"), "h00 h01 out0 h10 h11 out1", 1)
    fa = Steps(sem("ff_act"), "g00 g01 g10 g11", 1)
    fd = Steps(sem("ff_dve"), "res0 add0 res1 add1", 1)
    bank = mem.bank

    def bt(v):
        return v.rearrange("p (b t) -> p b t", b=CH)

    def flat(v):
        return v.rearrange("p b t -> p (b t)")

    with nc.Block() as block:
        @block.gpsimd
        def _(pool):
            pool.sem_inc(cg.sem, cg.credit())
            pool.sem_inc(sg.sem, sg.credit())
            pool.memset(xp[:, :, 0:1], 0.0).then_inc(init, 1)
            pool.memset(xp[:, :, T + 1:T + 2], 0.0).then_inc(init, 1)
            with pool.Fori(0, NIT) as it:
                n4.pool_turn(pool, it)
            with pool.Fori(0, NIT) as it:
                for p in range(2):
                    pool.wait_ge(ca.sem, ca.done(it, f"b{p}"))
                    pool.tensor_tensor(chunk(bm, it, p), tb[:, p], chunk(mix, it, p), ALU.mult).then_inc(cg.sem, 1)
            with pool.Fori(0, NIT) as it:
                for p in range(2):
                    pool.wait_ge(sd.sem, sd.done(it, f"dt{p}"))
                    pool.wait_ge(sd.sem, sd.previous(it, p, "state"))
                    pool.tensor_tensor(u[:, :, :], soft[:, p, 0], chunk(bm, it, p), ALU.mult).then_inc(sg.sem, 1)
            with pool.Fori(0, NIT) as it:
                n5.pool_turn(pool, it)

        @block.vector
        def _(dve):
            for s in (n4.dve, n5.dve, sd, fd):
                dve.sem_inc(s.sem, s.credit())
            dve.wait_ge(init, 3)
            dve.tensor_scalar(neg_a[:, 1:2], neg_a[:, 0:1], -1.0, None, ALU.mult).then_inc(init, 1)
            with dve.Fori(0, NIT) as it:
                n4.vector_turn(dve, it)
            with dve.Fori(0, NIT) as it:
                for p in range(2):
                    m = chunk(mix, it, p)
                    dve.wait_ge(ia.sem, ia.done(it, f"x{p}"))
                    dve.tensor_scalar(m, chunk(xp, it, p)[:, :, 1:T + 1], mem.col("dw1"), mem.col("dw_b"), ALU.mult, ALU.add).then_inc(cd.sem, 1)
                    dve.wait_ge(cd.sem, cd.done(it, f"a{p}"))
                    dve.scalar_tensor_tensor(m, chunk(xp, it, p)[:, :, 0:T], mem.col("dw0"), m, ALU.mult, ALU.add).then_inc(cd.sem, 1)
                    dve.wait_ge(cd.sem, cd.done(it, f"b{p}"))
                    dve.scalar_tensor_tensor(m, chunk(xp, it, p)[:, :, 2:T + 2], mem.col("dw2"), m, ALU.mult, ALU.add).then_inc(cd.sem, 1)
            with dve.Fori(0, NIT) as it:
                for p in range(2):
                    dve.wait_ge(sa.sem, sa.done(it, f"ln{p}"))
                    dve.scalar_tensor_tensor(soft[:, p, 0], chunk(dz, it, p), 0.0, soft[:, p, 1], ALU.max, ALU.add).then_inc(sd.sem, 1)
                    dve.wait_ge(sa.sem, sa.done(it, f"decay{p}"))
                    dve.memset(decay[:, :, 0:1], 0.0).then_inc(sd.sem, 1)
                    dve.wait_ge(sd.sem, sd.done(it, f"start{p}"))
                    dve.wait_ge(sg.sem, sg.done(it, f"u{p}"))
                    dve.tensor_tensor_scan(flat(state), flat(decay), flat(u), 0.0, ALU.mult, ALU.add).then_inc(sd.sem, 1)
                    dve.wait_ge(sd.sem, sd.done(it, f"state{p}"))
                    dve.tensor_tensor(state, state, chunk(ct, it, p), ALU.mult).then_inc(sd.sem, 1)
                    dve.wait_ge(sd.sem, sd.done(it, f"cs{p}"))
                    dve.scalar_tensor_tensor(state, chunk(mix, it, p), mem.col("d_skip"), state, ALU.mult, ALU.add).then_inc(sd.sem, 1)
                    dve.wait_ge(sd.sem, sd.done(it, f"skip{p}"))
                    dve.wait_ge(se.sem, se.done(it - 1, f"out{p}"))
                    dve.tensor_tensor(bt(yT[:, p]), state, chunk(gt, it, p), ALU.mult).then_inc(sd.sem, 1)
                    xl = chunk(mem.xl, it, p)
                    dve.wait_ge(se.sem, se.done(it, f"out{p}"))
                    dve.tensor_tensor(xl, xl, bt(bank(p)), ALU.add).then_inc(sd.sem, 1)
            dve.wait_ge(sd.sem, sd.done(NIT - 1, "add1"))
            with dve.Fori(0, NIT) as it:
                n5.vector_turn(dve, it)
            with dve.Fori(0, NIT) as it:
                for p in range(2):
                    x = chunk(mem.x, it, p)
                    dve.tensor_tensor(x, x, chunk(mem.xl, it, p), ALU.add).then_inc(fd.sem, 1)
                    dve.wait_ge(fd.sem, fd.done(it, f"res{p}"))
                    dve.wait_ge(fe.sem, fe.done(it, f"out{p}"))
                    dve.tensor_tensor(x, x, bt(bank(4 + p)), ALU.add).then_inc(fd.sem, 1)

        @block.scalar
        def _(act):
            for s in (n4.act, n5.act, ia, ca, sa, fa):
                act.sem_inc(s.sem, s.credit())
            act.activation(neg_a[:, 0:1], mem.col("a_log"), ACT.Exp).then_inc(init, 1)
            with act.Fori(0, NIT) as it:
                n4.scalar_turn(act, it)
            act.wait_ge(init, 2)
            with act.Fori(0, NIT) as it:
                for p in range(2):
                    act.wait_ge(ie.sem, ie.done(it, f"x{p}"))
                    act.activation(chunk(xp, it, p)[:, :, 1:T + 1], bt(bank(p)), ACT.Identity, bias=mem.col("in_b0")).then_inc(ia.sem, 1)
                    act.wait_ge(ie.sem, ie.done(it, f"g{p}"))
                    act.activation(chunk(gt, it, p), bt(bank(2 + p)), ACT.Sigmoid, bias=mem.col("in_b1")).then_inc(ia.sem, 1)
            with act.Fori(0, NIT) as it:
                for p in range(2):
                    act.wait_ge(ce.sem, ce.done(it, f"dt{p}"))
                    act.activation(chunk(dz, it, p), bt(bank(4)), ACT.Identity, bias=mem.col("dt_b")).then_inc(ca.sem, 1)
                    act.wait_ge(ce.sem, ce.done(it, f"b{p}"))
                    act.wait_ge(cg.sem, cg.done(it - 1, f"bm{p}"))
                    act.activation(tb[:, p], bt(bank(5)), ACT.Tanh, bias=mem.col("b_b")).then_inc(ca.sem, 1)
                    act.wait_ge(ce.sem, ce.done(it, f"c{p}"))
                    act.activation(chunk(ct, it, p), bt(bank(6 + p)), ACT.Tanh, bias=mem.col("c_b")).then_inc(ca.sem, 1)
            act.wait_ge(ca.sem, ca.done(NIT - 1, "c1"))
            act.wait_ge(cd.sem, cd.done(NIT - 1, "c1"))
            act.wait_ge(cg.sem, cg.done(NIT - 1, "bm1"))
            act.wait_ge(init, 4)
            with act.Fori(0, NIT) as it:
                for p in range(2):
                    act.wait_ge(sd.sem, sd.done(it - 1, f"state{p}"))
                    act.activation(soft[:, p, 0], chunk(dz, it, p), ACT.Abs).then_inc(sa.sem, 1)
                    act.wait_ge(sa.sem, sa.done(it, f"neg{p}"))
                    act.activation(soft[:, p, 1], soft[:, p, 0], ACT.Exp, scale=-1.0).then_inc(sa.sem, 1)
                    act.wait_ge(sa.sem, sa.done(it, f"exp{p}"))
                    act.activation(soft[:, p, 1], soft[:, p, 1], ACT.Ln, bias=1.0).then_inc(sa.sem, 1)
                    act.wait_ge(sd.sem, sd.done(it, f"dt{p}"))
                    act.wait_ge(sd.sem, sd.previous(it, p, "state"))
                    act.activation(decay[:, :, :], soft[:, p, 0], ACT.Exp, scale=neg_a[:, 1:2]).then_inc(sa.sem, 1)
            with act.Fori(0, NIT) as it:
                n5.scalar_turn(act, it)
            with act.Fori(0, NIT) as it:
                for p in range(2):
                    for k in range(2):
                        act.wait_ge(fe.sem, fe.done(it, f"h{p}{k}"))
                        if k == 0:
                            act.wait_ge(fe.sem, fe.done(it - 1, f"out{p}"))
                        act.activation(act1[:, p, k], bank(2 * p + k), ACT.Gelu, bias=mem.col(f"f1_b{k}")).then_inc(fa.sem, 1)

        @block.tensor
        def _(pe):
            for s in (n4.pe, n5.pe, ie, ce, se, fe):
                pe.sem_inc(s.sem, s.credit())
            with pe.Fori(0, NIT) as it:
                n4.tensor_turn(pe, it)
            with pe.Fori(0, NIT) as it:
                for p in range(2):
                    h = chunk(mem.hT, it, p)[:, :, 1:T + 1]
                    pe.wait_ge(n4.act.sem, n4.act.done(it, f"ready{p}"))
                    for k, name in enumerate("xg"):
                        pe.wait_ge(ia.sem, ia.done(it - 1, f"{name}{p}"))
                        pe.matmul(bt(bank(2 * k + p)), mem.mat("in_W", k), h, start=True, stop=True).then_inc(ie.sem, 1)
            with pe.Fori(0, NIT) as it:
                for p in range(2):
                    m = chunk(mix, it, p)
                    pe.wait_ge(cd.sem, cd.done(it, f"c{p}"))
                    for name, i in (("dt", 4), ("b", 5), ("c", 6 + p)):
                        pe.wait_ge(ca.sem, ca.done(it - 1, f"c{p}") if name == "c" else ca.previous(it, p, name))
                        pe.matmul(bt(bank(i)), mem.mat(f"{name}_W"), m, start=True, stop=True).then_inc(ce.sem, 1)
            with pe.Fori(0, NIT) as it:
                for p in range(2):
                    pe.wait_ge(sd.sem, sd.done(it, f"y{p}"))
                    for j in range(CH):
                        out = bank(p)[:, j * C:(j + 1) * C]
                        pe.matmul(out, yT[:, p, j * T:(j + 1) * T], mem.mat("out_W"), start=True, stop=False)
                        last = pe.matmul(out, mem.ones[0:1, :], mem.row("m_out_b"), start=False, stop=True)
                    last.then_inc(se.sem, 1)
            with pe.Fori(0, NIT) as it:
                n5.tensor_turn(pe, it)
            with pe.Fori(0, NIT) as it:
                for p in range(2):
                    h = chunk(mem.hT, it, p)[:, :, 1:T + 1]
                    pe.wait_ge(n5.act.sem, n5.act.done(it, f"ready{p}"))
                    for k in range(2):
                        pe.wait_ge(fa.sem, fa.done(it - 1, f"g{p}{k}"))
                        pe.matmul(bt(bank(2 * p + k)), mem.mat("f1_W", k), h, start=True, stop=True).then_inc(fe.sem, 1)
                    pe.wait_ge(fa.sem, fa.done(it, f"g{p}1"))
                    pe.wait_ge(fd.sem, fd.done(it - 1, f"add{p}"))
                    for j in range(CH):
                        out = bank(4 + p)[:, j * C:(j + 1) * C]
                        for k in range(2):
                            pe.matmul(out, act1[:, p, k, j * T:(j + 1) * T], mem.mat("f2_W", k), start=(k == 0), stop=False)
                        last = pe.matmul(out, mem.ones[0:1, :], mem.row("f2_b"), start=False, stop=True)
                    last.then_inc(fe.sem, 1)


MAGIC = 12582912.0
Q16 = 32767.0
NG = 12
GW = 3 * B * T // NG


def quantised_ffn_block(nc, mem, ctx, out):
    def sem(n):
        return ctx.enter_context(nc.semaphore(f"q_{n}"))

    mem.restart()
    up = mem.take(3, B * T)
    gate = mem.take(3, B * T)
    wT = mem.take(3, 3 * C)
    qx = mem.take(2, CH, C)
    qxT = mem.take(2, W)
    top = mem.at
    mem.at = 0
    wq = mem.take(36, 32)
    ws = mem.take(3, 36)
    mem.at = top
    amax = mem.take(16)
    amax_u = mem.take(16)
    glob = mem.take(16)
    row = mem.take(128)
    t1 = mem.take(2, GW)
    t2 = mem.take(2, GW)
    oq = mem.hn
    n = Norm(nc, mem, ctx, "qn", mem.x)
    n.dve.names[-2:] = ["scaled0", "amax"]
    wd = sem("weights_dve")
    we = Steps(sem("weights_pe"), "0 1 2")
    wa = Steps(sem("weights_act"), "0 1 2")
    gd, ge = sem("max_dve"), sem("max_pe")
    pd = Steps(sem("proj_dve"), " ".join(f"a{p} b{p} q{p} " + " ".join(f"mu{p}{k} mg{p}{k}" for k in range(3)) for p in range(2)), 1)
    pe_ = Steps(sem("proj_pe"), " ".join(f"turned{p} " + " ".join(f"u{p}{k} g{p}{k}" for k in range(3)) for p in range(2)), 1)
    pa = Steps(sem("proj_act"), " ".join(f"xT{p} " + " ".join(f"u{p}{k} g{p}{k}" for k in range(3)) for p in range(2)), 1)
    sd = Steps(sem("sig_dve"), " ".join(f"a{p} b{p} q{p} s{p} r{p} g{p} m{p}" for p in range(2)), 1)
    sa = Steps(sem("sig_act"), "sig0 sig1", 1)
    od = Steps(sem("prod_dve"), " ".join(f"ga{p} gb{p} gq{p} ua{p} ub{p} uq{p} o{p} m{p}" for p in range(2)), 1)
    dd = Steps(sem("down_dve"), "a0 b0 q0 a1 b1 q1 add0 add1", 1)
    de = Steps(sem("down_pe"), "out0 out1", 1)
    stored = sem("stored")
    bank = mem.bank
    used = [0]

    def bt(v):
        return v.rearrange("p (b t) -> p b t", b=CH)

    X, U, G, G2, O = range(5)

    def scale(i):
        return glob[:, 2 * i:2 * i + 1]

    def inverse(i):
        return glob[:, 2 * i + 1:2 * i + 2]

    def find_scale_vector(dve, i, src, unit=1.0):
        def step(ins):
            used[0] += 1
            ins.then_inc(gd, 1)
            dve.wait_ge(gd, used[0])

        step(dve.tensor_reduce(row[:, 0:1], src, AX.X, ALU.max))
        dve.wait_ge(ge, 2 * i + 1)
        step(dve.tensor_reduce(row[0:1, 1:2], bank(7)[0:1, 0:128], AX.X, ALU.max))
        dve.wait_ge(ge, 2 * i + 2)
        step(dve.tensor_scalar(row[:, 2:3], bank(7)[:, 128:129], unit / Q16, 1e-12, ALU.mult, ALU.max))
        if unit == 1.0:
            step(dve.tensor_copy(scale(i), row[:, 2:3]))
        else:
            step(dve.tensor_scalar(scale(i), row[:, 2:3], 1.0 / unit, None, ALU.mult))
        step(dve.reciprocal(inverse(i), scale(i)))

    def find_scale_tensor(pe, i):
        pe.wait_ge(gd, 5 * i + 1)
        pe.transpose(bank(7)[0:1, 0:128], row[:, 0:1], mem.mat("ident")).then_inc(ge, 1)
        pe.wait_ge(gd, 5 * i + 2)
        pe.matmul(bank(7)[:, 128:129], mem.ones[0:1, :], row[0:1, 1:2], start=True, stop=True).then_inc(ge, 1)

    def ready(eng, i):
        eng.wait_ge(gd, 5 * i + 5)

    with nc.Block() as block:
        @block.gpsimd
        def _(pool):
            with pool.Fori(0, NIT) as it:
                n.pool_turn(pool, it)

        @block.vector
        def _(dve):
            for s in (n.dve, pd, sd, od, dd):
                dve.sem_inc(s.sem, s.credit())
            k = 0

            def step(ins):
                nonlocal k
                k += 1
                ins.then_inc(wd, 1)
                dve.wait_ge(wd, k)

            w = mem.mat("gate", 0, 9 * C).rearrange("p (n k) -> p n k", k=32)
            step(dve.tensor_reduce(ws[:, 0, :], w, AX.X, ALU.max, apply_absolute_value=True))
            step(dve.tensor_scalar(ws[:, 1, :], ws[:, 0, :], 1.0 / 7.0, 1e-12, ALU.mult, ALU.max))
            step(dve.reciprocal(ws[:, 2, :], ws[:, 1, :]))
            step(dve.tensor_tensor(wq[:, :, :], w, ws[:, 2, :].unsqueeze(2).broadcast_to([128, 36, 32]), ALU.mult))
            step(dve.tensor_scalar(wq[:, :, :], wq[:, :, :], MAGIC, MAGIC, ALU.add, ALU.subtract))
            step(dve.tensor_scalar(wq[:, :, :], wq[:, :, :], 7.0, -8.0, ALU.min, ALU.max))
            step(dve.tensor_tensor(wq[:, :, :], wq[:, :, :], ws[:, 1, :].unsqueeze(2).broadcast_to([128, 36, 32]), ALU.mult))
            with dve.Fori(0, NIT) as it:
                n.vector_turn(dve, it, amax)
            dve.wait_ge(n.dve.sem, n.dve.done(NIT - 1, "amax"))
            find_scale_vector(dve, X, amax[:, 0:NIT])

            def round_to(eng_sem, steps, it, names, dst, src, i, tmp):
                dve.tensor_scalar(tmp, src, inverse(i), Q16, ALU.mult, ALU.min).then_inc(steps.sem, 1)
                dve.wait_ge(steps.sem, steps.done(it, names[0]))
                dve.tensor_scalar(tmp, tmp, -Q16 - 1.0, MAGIC, ALU.max, ALU.add).then_inc(steps.sem, 1)
                dve.wait_ge(steps.sem, steps.done(it, names[1]))
                dve.tensor_scalar(dst, tmp, MAGIC, scale(i), ALU.subtract, ALU.mult).then_inc(steps.sem, 1)

            with dve.Fori(0, NIT) as it:
                for p in range(2):
                    tmp = t1[:, p, 0:W].rearrange("p (b c) -> p b c", b=CH)
                    dve.wait_ge(pd.sem, pd.done(it - 1, f"q{p}"))
                    dve.wait_ge(pe_.sem, pe_.done(it - 1, f"turned{p}"))
                    round_to(None, pd, it, (f"a{p}", f"b{p}"), qx[:, p], chunk(mem.xl, it, p), X, tmp)
                    for j in range(3):
                        for name, kk, arr in (("u", 0, amax_u), ("g", 1, amax)):
                            dve.wait_ge(pe_.sem, pe_.done(it, f"{name}{p}{j}"))
                            if name == "u":
                                dst = t2[:, 0, 0:24]
                            else:
                                dst = t2[:, 1, 0:24]
                            dst = dst.rearrange("p (c k) -> p c k", k=3)[:, bass.ds(it * 2 + p, 1), j]
                            dve.tensor_reduce(dst, bank(2 * j + kk), AX.X, ALU.max, apply_absolute_value=True).then_inc(pd.sem, 1)
            dve.wait_ge(pd.sem, pd.done(NIT - 1, "mg12"))
            find_scale_vector(dve, U, t2[:, 0, 0:24])
            find_scale_vector(dve, G, t2[:, 1, 0:24])
            dve.wait_ge(pa.sem, pa.done(NIT - 1, "g12"))
            gflat, uflat = gate.rearrange("p k t -> p (k t)"), up.rearrange("p k t -> p (k t)")
            with dve.Fori(0, NG // 2) as it:
                for p in range(2):
                    g = gflat[:, bass.ds((it * 2 + p) * GW, GW)]
                    dve.wait_ge(sd.sem, sd.done(it - 1, f"g{p}"))
                    round_to(None, sd, it, (f"a{p}", f"b{p}"), t1[:, p, :], g, G, t1[:, p, :])
                    dve.wait_ge(sa.sem, sa.done(it, f"sig{p}"))
                    dve.tensor_scalar(t2[:, p, :], t2[:, p, :], 65536.0, 65535.0, ALU.mult, ALU.min).then_inc(sd.sem, 1)
                    dve.wait_ge(sd.sem, sd.done(it, f"s{p}"))
                    dve.tensor_scalar(t2[:, p, :], t2[:, p, :], 0.0, MAGIC, ALU.max, ALU.add).then_inc(sd.sem, 1)
                    dve.wait_ge(sd.sem, sd.done(it, f"r{p}"))
                    dve.scalar_tensor_tensor(g, t2[:, p, :], MAGIC, t1[:, p, :], ALU.subtract, ALU.mult).then_inc(sd.sem, 1)
                    dve.wait_ge(sd.sem, sd.done(it, f"g{p}"))
                    dve.tensor_reduce(amax[:, bass.ds(it * 2 + p, 1)], gflat[:, bass.ds((it * 2 + p) * GW, GW)], AX.X, ALU.max,
                                      apply_absolute_value=True).then_inc(sd.sem, 1)
            dve.wait_ge(sd.sem, sd.done(NG // 2 - 1, "m1"))
            find_scale_vector(dve, G2, amax[:, 0:NG], unit=2.0 ** -16)
            with dve.Fori(0, NG // 2) as it:
                for p in range(2):
                    g, u = gflat[:, bass.ds((it * 2 + p) * GW, GW)], uflat[:, bass.ds((it * 2 + p) * GW, GW)]
                    dve.wait_ge(od.sem, od.done(it - 1, f"o{p}"))
                    round_to(None, od, it, (f"ga{p}", f"gb{p}"), t1[:, p, :], g, G2, t1[:, p, :])
                    round_to(None, od, it, (f"ua{p}", f"ub{p}"), t2[:, p, :], u, U, t2[:, p, :])
                    dve.wait_ge(od.sem, od.done(it, f"uq{p}"))
                    dve.tensor_tensor(g, t1[:, p, :], t2[:, p, :], ALU.mult).then_inc(od.sem, 1)
                    dve.wait_ge(od.sem, od.done(it, f"o{p}"))
                    dve.tensor_reduce(amax_u[:, bass.ds(it * 2 + p, 1)], gflat[:, bass.ds((it * 2 + p) * GW, GW)], AX.X, ALU.max,
                                      apply_absolute_value=True).then_inc(od.sem, 1)
            dve.wait_ge(od.sem, od.done(NG // 2 - 1, "m1"))
            find_scale_vector(dve, O, amax_u[:, 0:NG], unit=2.0 ** -16)
            dve.tensor_scalar(row[:, 3:4], scale(O), 2.0 ** -16, None, ALU.mult).then_inc(wd, 1)
            dve.wait_ge(wd, k + 1)
            prod = uflat[:, 0:2 * 3 * W].rearrange("p (q k t) -> p q k t", q=2, k=3)
            tmp = uflat[:, 2 * 3 * W:4 * 3 * W].rearrange("p (q k t) -> p q k t", q=2, k=3)
            with dve.Fori(0, NIT) as it:
                for p in range(2):
                    dve.wait_ge(dd.sem, dd.done(it - 1, f"q{p}"))
                    dve.wait_ge(de.sem, de.done(it - 1, f"out{p}"))
                    src = gate[:, :, bass.ds((it * 2 + p) * W, W)]
                    dve.tensor_scalar(tmp[:, p], src, inverse(O), Q16, ALU.mult, ALU.min).then_inc(dd.sem, 1)
                    dve.wait_ge(dd.sem, dd.done(it, f"a{p}"))
                    dve.tensor_scalar(tmp[:, p], tmp[:, p], -Q16 - 1.0, MAGIC, ALU.max, ALU.add).then_inc(dd.sem, 1)
                    dve.wait_ge(dd.sem, dd.done(it, f"b{p}"))
                    dve.tensor_scalar(prod[:, p], tmp[:, p], MAGIC, row[:, 3:4], ALU.subtract, ALU.mult).then_inc(dd.sem, 1)
                for p in range(2):
                    x = chunk(mem.x, it, p)
                    dve.wait_ge(de.sem, de.done(it, f"out{p}"))
                    dve.tensor_tensor(x, x, bt(bank(p)), ALU.add).then_inc(dd.sem, 1)

        @block.scalar
        def _(act):
            for s in (pa, sa):
                act.sem_inc(s.sem, s.credit())
            for i in range(3):
                act.wait_ge(we.sem, i + 1)
                act.activation(wT[:, i, :], bank(i)[:, 0:3 * C], ACT.Copy).then_inc(wa.sem, 1)
            act.wait_ge(wd, 7)
            with act.Fori(0, NIT) as it:
                for p in range(2):
                    act.wait_ge(pe_.sem, pe_.done(it, f"turned{p}"))
                    act.wait_ge(pe_.sem, pe_.done(it - 1, f"g{p}2"))
                    act.activation(qxT[:, p], bank(6), ACT.Copy).then_inc(pa.sem, 1)
                    for j in range(3):
                        for name, kk, dst in (("u", 0, up), ("g", 1, gate)):
                            act.wait_ge(pd.sem, pd.done(it, f"m{name}{p}{j}"))
                            act.activation(dst[:, j, bass.ds((it * 2 + p) * W, W)], bank(2 * j + kk), ACT.Copy).then_inc(pa.sem, 1)
            with act.Fori(0, NG // 2) as it:
                for p in range(2):
                    act.wait_ge(sd.sem, sd.done(it, f"q{p}"))
                    act.wait_ge(sd.sem, sd.done(it - 1, f"g{p}"))
                    act.activation(t2[:, p, :], t1[:, p, :], ACT.Sigmoid).then_inc(sa.sem, 1)

        @block.tensor
        def _(pe):
            for s in (pe_, de):
                pe.sem_inc(s.sem, s.credit())
            pe.wait_ge(wd, 7)
            wflat = wq.rearrange("p n k -> p (n k)")
            for i in range(3):
                for j in range(3):
                    last = pe.transpose(bank(i)[:, j * C:(j + 1) * C], wflat[:, (3 * i + j) * C:(3 * i + j + 1) * C], mem.mat("ident"))
                last.then_inc(we.sem, 1)
            find_scale_tensor(pe, X)
            pe.wait_ge(wa.sem, 3)
            with pe.Fori(0, NIT) as it:
                for p in range(2):
                    pe.wait_ge(pd.sem, pd.done(it, f"q{p}"))
                    pe.wait_ge(pa.sem, pa.previous(it, p, "xT"))
                    for j in range(CH):
                        last = pe.transpose(bank(6)[:, j * T:(j + 1) * T], qx[:, p, j, :], mem.mat("ident"))
                    last.then_inc(pe_.sem, 1)
                    pe.wait_ge(pa.sem, pa.done(it, f"xT{p}"))
                    for j in range(3):
                        for name, kk, w in (("u", 0, 1), ("g", 1, 0)):
                            pe.wait_ge(pa.sem, pa.done(it, f"{name}0{j}") if p else pa.done(it - 1, f"{name}1{j}"))
                            pe.matmul(bank(2 * j + kk), wT[:, w, j * C:(j + 1) * C], qxT[:, p], start=True, stop=True).then_inc(pe_.sem, 1)
            for i in (U, G, G2, O):
                find_scale_tensor(pe, i)
            prod = up.rearrange("p k t -> p (k t)")[:, 0:2 * 3 * W].rearrange("p (q k t) -> p q k t", q=2, k=3)
            with pe.Fori(0, NIT) as it:
                for p in range(2):
                    pe.wait_ge(dd.sem, dd.done(it, f"q{p}"))
                    pe.wait_ge(dd.sem, dd.done(it - 1, f"add{p}"))
                    for j in range(CH):
                        for k in range(3):
                            last = pe.matmul(bank(p)[:, j * C:(j + 1) * C], prod[:, p, k, j * T:(j + 1) * T],
                                             wT[:, 2, k * C:(k + 1) * C], start=(k == 0), stop=(k == 2))
                    last.then_inc(de.sem, 1)

        @block.sync
        def _(sp):
            dst = out.rearrange("b t c -> t b c")
            with sp.Fori(0, NIT) as it:
                for p in range(2):
                    sp.wait_ge(dd.sem, dd.done(it, f"add{p}"))
                    at = bass.ds((it * 2 + p) * CH, CH)
                    sp.dma_start(dst[:, at, :], mem.x[:, at, :]).then_inc(stored, 16)
            sp.wait_ge(stored, 16 * NCH)


def build(nc, x, ctx_tokens, pack, rows, b_proj, w_fc, w_proj, v_mask, out):
    with ExitStack() as ctx:
        mem = Memory(nc, ctx)
        load_block(nc, mem, ctx, x, pack, rows, b_proj)
        time_mix_block(nc, mem, ctx)
        context_block(nc, mem, ctx, ctx_tokens)
        attention_block(nc, mem, ctx, 0, v_mask)
        experts_block(nc, mem, ctx, w_fc, w_proj)
        state_space_block(nc, mem, ctx)
        attention_block(nc, mem, ctx, 1, v_mask)
        quantised_ffn_block(nc, mem, ctx, out)


def lay_out(inp):
    import numpy as np

    f = {k: np.asarray(v) for k, v in inp.items()}
    a, x0, m, x1, g = "L0_attn_", "L0_xattn_", "L1_attn_", "L1_xattn_", "L1_ffn_"

    def blocks(w):
        return w.reshape(-1, 128, w.shape[1]).transpose(1, 0, 2).reshape(128, -1)

    parts = {
        "ln1_w": f[a + "ln1_w"], "ln1_b": f[a + "ln1_b"], "ln2_w": f[a + "ln2_w"], "ln2_b": f[a + "ln2_b"],
        "tmk": f[a + "att_tmk"], "tmv": f[a + "att_tmv"], "tmr": f[a + "att_tmr"],
        "decay": f[a + "time_decay"], "first": f[a + "time_first"],
        "ftmk": f[a + "ffn_tmk"], "ftmr": f[a + "ffn_tmr"], "bq": f[x0 + "bq"], "bk": f[x0 + "bk"],
        "m_ln1_g": f[m + "ln1_g"], "m_ln1_b": f[m + "ln1_b"], "in_b0": f[m + "in_b"][:C], "in_b1": f[m + "in_b"][C:],
        "dw0": f[m + "dw_W"][:, 0, 0], "dw1": f[m + "dw_W"][:, 0, 1], "dw2": f[m + "dw_W"][:, 0, 2],
        "dw_b": f[m + "dw_b"], "dt_b": f[m + "dt_b"], "b_b": f[m + "b_b"], "c_b": f[m + "c_b"],
        "a_log": f[m + "a_log"], "d_skip": f[m + "d_skip"], "m_ln2_g": f[m + "ln2_g"], "m_ln2_b": f[m + "ln2_b"],
        "f1_b0": f[m + "f1_b"][:C], "f1_b1": f[m + "f1_b"][C:],
        "b_fc": f["L0_ffn_b_fc"].reshape(E, 4, 128).transpose(2, 0, 1),
        "WkT": f[a + "Wk"].T, "WvT": f[a + "Wv"].T, "WrT": f[a + "Wr"].T, "WoT": f[a + "Wo"].T,
        "WkeyT": f[a + "Wkey"].T, "WrecT": f[a + "Wrec"].T, "WvalT": blocks(f[a + "Wval"].T),
        "qT0": f[x0 + "Wq"].T, "kT0": f[x0 + "Wk"].T, "vT0": f[x0 + "Wv"].T, "oT0": f[x0 + "Wo"].T,
        "qT1": f[x1 + "Wq"].T, "kT1": f[x1 + "Wk"].T, "vT1": f[x1 + "Wv"].T, "oT1": f[x1 + "Wo"].T,
        "router": f["L0_ffn_router_w"].T, "in_W": f[m + "in_W"], "dt_W": f[m + "dt_W"], "b_W": f[m + "b_W"],
        "c_W": f[m + "c_W"], "out_W": f[m + "out_W"], "f1_W": f[m + "f1_W"], "f2_W": blocks(f[m + "f2_W"]),
        "gate": blocks(f[g + "w_gate"]), "up": blocks(f[g + "w_up"]), "down": f[g + "w_down"],
    }
    head_of = np.arange(128) % 32 // HD
    parts["head_mask"] = (np.arange(128)[:, None] // HD == np.arange(H)[None, :]).astype(np.float32)
    parts["rank"] = np.broadcast_to(np.arange(E, 0, -1, dtype=np.float32), (128, E))
    parts["ident"] = np.eye(128, dtype=np.float32)
    parts["causal"] = np.where(np.arange(S)[None, :] > np.arange(128)[:, None], np.float32(-1e30), np.float32(0))
    v_mask = np.broadcast_to(head_of[None, :] == np.arange(4)[:, None], (128, 4, C)).astype(np.float32)
    pack = np.concatenate([np.asarray(parts[n]).reshape(128, w) for n, w in LAYOUT], axis=1)
    rows = np.concatenate([f[x0 + "bv"], f[x0 + "bo"], f[m + "out_b"], f[m + "f2_b"], f[x1 + "bo"]])[None, :]
    return {
        "x": f["x"], "ctx_tokens": f["ctx_1024"], "pack": pack, "rows": rows, "b_proj": f["L0_ffn_b_proj"],
        "w_fc": f["L0_ffn_w_fc"].transpose(1, 0, 2).reshape(128, E * HID),
        "w_proj": f["L0_ffn_w_proj"].reshape(E, 4, 128, C).transpose(2, 0, 1, 3).reshape(128, E * 4 * C),
        "v_mask": v_mask,
    }


def kernel(**inputs):
    import numpy as np
    import concourse.bacc as bacc
    from concourse.bass_utils import run_bass_kernel_spmd

    arrays = {f"in_{k}": np.ascontiguousarray(v) for k, v in lay_out(inputs).items()}
    nc = bacc.Bacc("TRN2", target_bir_lowering=False, num_devices=1)
    args = [nc.dram_tensor(k, v.shape, F32, kind="ExternalInput").ap() for k, v in arrays.items()]
    out = nc.dram_tensor("out", (B, T, C), F32, kind="ExternalOutput").ap()
    build(nc, *args, out)
    r = run_bass_kernel_spmd(nc, [arrays], core_ids=[0])
    return r.results[0]["out"]
```

```python
import concourse.bass as bass
from concourse import mybir
from contextlib import ExitStack

F32 = mybir.dt.float32
BF16 = mybir.dt.bfloat16
ACT = mybir.ActivationFunctionType
ALU = mybir.AluOpType
AX = mybir.AxisListType

B, T, C = 32, 128, 128
S = 77
CH = 4
NCH = B // CH
W = CH * T
NIT = NCH // 2
H, HD = 16, 8
E, HID = 8, 512
EPS = 1e-5
ATT_SCALE = float(HD) ** -0.5
NEG = -1e38

VECTORS = ["ln1_w", "ln1_b", "ln2_w", "ln2_b", "tmk", "tmv", "tmr", "decay", "first", "ftmk", "ftmr",
           "bq", "bk", "bv", "m_ln1_g", "m_ln1_b", "in_b0", "in_b1", "dw0", "dw1", "dw2", "dw_b", "dt_b",
           "b_b", "c_b", "a_log", "d_skip", "m_ln2_g", "m_ln2_b", "f1_b0", "f1_b1"]
LAYOUT = ([(n, 1) for n in VECTORS] +
          [("b_fc", E * 4), ("head_mask", H), ("rank", E), ("ident", 128), ("causal", S),
           ("WkT", C), ("WvT", C), ("WrT", C), ("WoT", C), ("WkeyT", 512), ("WrecT", C), ("WvalT", 4 * C),
           ("qT0", C), ("kT0", C), ("vT0", C), ("oT0", C), ("qT1", C), ("kT1", C), ("vT1", C), ("oT1", C),
           ("router", E), ("in_W", 2 * C), ("dt_W", C), ("b_W", C), ("c_W", C), ("out_W", C),
           ("f1_W", 2 * C), ("f2_W", 2 * C), ("gate", 3 * C), ("up", 3 * C), ("down", 3 * C)])
AT, NPACK = {}, 0
for _n, _w in LAYOUT:
    AT[_n] = (NPACK, _w)
    NPACK += _w
ROWS = ["bo0", "m_out_b", "f2_b", "bo1"]
EXPERT_WORDS = E * HID + E * 4 * C

ARENA = 33160


class Steps:

    def __init__(self, sem, names, ahead=0):
        self.sem, self.names, self.ahead = sem, names.split(), ahead
        assert len(set(self.names)) == len(self.names)

    def done(self, turn, name):
        return turn * len(self.names) + (self.ahead * len(self.names) + self.names.index(name) + 1)

    def previous(self, turn, p, name):
        return self.done(turn, f"{name}0") if p else self.done(turn - 1, f"{name}1")

    def credit(self):
        return self.ahead * len(self.names)


class Memory:

    def __init__(self, nc, ctx):
        def sb(name, shape, dt=F32):
            return ctx.enter_context(nc.sbuf_tensor(name, shape, dt))

        self.x = sb("x_res", [128, B, C])
        self.xl = sb("x_norm", [128, B, C])
        self.hT = sb("hT", [128, B, T + 1])
        self.pack = sb("pack", [128, NPACK])
        self.rows = sb("rows", [1, len(ROWS) * C])
        self.b_proj = sb("b_proj", [E, C])
        self.ones = sb("ones", [128, 128])
        self.half = sb("half", [128, 2 * CH])
        self.hn = sb("hn", [128, 2, CH, C])
        self.bn = sb("bn", [128, 2 * CH, 6])
        self.tmp = sb("bn_sums", [128, 5, 2 * CH])
        self.ve = sb("ve", [128, 6, 2 * CH])
        self.mean = sb("mean", [128, B])
        self.rs = sb("rs", [128, 6, B])
        self.eps = sb("eps", [128, 2 * CH])
        self.arena = sb("arena", [128, ARENA])
        self.ps = ctx.enter_context(nc.psum_tensor("psum", [128, 8 * W], F32))
        self.at = 0

    def col(self, name, i=0):
        o = AT[name][0] + i
        return self.pack[:, o:o + 1]

    def mat(self, name, i=0, w=C):
        o = AT[name][0] + i * w
        return self.pack[:, o:o + w]

    def row(self, name):
        i = ROWS.index(name)
        return self.rows[0:1, i * C:(i + 1) * C]

    def bank(self, i):
        return self.ps[:, i * W:(i + 1) * W]

    def restart(self):
        self.at = 0

    def take(self, *shape):
        n = 1
        for s in shape:
            n *= s
        self.at += n
        assert self.at <= ARENA, (self.at, ARENA)
        v = self.arena[:, self.at - n:self.at]
        if len(shape) == 1:
            return v
        names = "abcde"[:len(shape)]
        return v.rearrange(f"p ({' '.join(names)}) -> p {' '.join(names)}", **dict(zip(names[:-1], shape)))


class Norm:

    def __init__(self, nc, mem, ctx, tag, src, double=False, affine=None, whole=False, banks=(6, 7)):
        def sem(n):
            return ctx.enter_context(nc.semaphore(f"{tag}_{n}"))

        self.mem, self.src, self.double, self.affine, self.banks = mem, src, double, affine, banks
        self.stats = Steps(sem("stats"), "bn diff square m2 mean var veps", 1)
        self.dve = Steps(sem("dve"), "inner amax" if whole else "inner " * double + "scaled0 scaled1")
        self.pool = Steps(sem("pool"), "veps var pow r1 a b c r2 r12 rstd" if double else "veps pow r1", 0)
        self.pe = Steps(sem("pe"), "turned0 turned1", 1)
        self.act = Steps(sem("act"), "ready0 ready1", 1)

    def vector_stats(self, dve, it):
        m, d, N = self.mem, self.stats, 2 * CH
        stat, tmp = m.bn, m.tmp
        at = bass.ds(it * N, N)

        def after(name):
            dve.wait_ge(d.sem, d.done(it, name))

        dve.wait_ge(d.sem, d.done(it - 1, "m2"))
        for n in range(N):
            last = dve.bn_stats(stat[:, n, :], self.src[:, it * N + n, :])
        last.then_inc(d.sem, 1)
        after("bn")
        dve.tensor_tensor(tmp[:, 0, :], stat[:, :, 1], stat[:, :, 4], ALU.subtract).then_inc(d.sem, 1)
        after("diff")
        dve.tensor_tensor(tmp[:, 1, :], tmp[:, 0, :], tmp[:, 0, :], ALU.mult).then_inc(d.sem, 1)
        dve.tensor_tensor(tmp[:, 2, :], stat[:, :, 2], stat[:, :, 5], ALU.add)
        dve.tensor_tensor(tmp[:, 3, :], stat[:, :, 1], stat[:, :, 4], ALU.add).then_inc(d.sem, 1)
        after("m2")
        dve.tensor_scalar(m.mean[:, at], tmp[:, 3, :], 0.5, None, ALU.mult).then_inc(d.sem, 1)
        dve.wait_ge(d.sem, d.done(it - 1, "veps"))
        dve.scalar_tensor_tensor(tmp[:, 4, :], tmp[:, 1, :], 32.0, tmp[:, 2, :], ALU.mult, ALU.add).then_inc(d.sem, 1)
        after("var")
        dve.tensor_scalar(m.rs[:, 5, at], tmp[:, 4, :], 1.0 / C, None, ALU.mult)
        dve.tensor_scalar(m.rs[:, 0, at], tmp[:, 4, :], 1.0 / C, EPS, ALU.mult, ALU.add).then_inc(d.sem, 1)

    def scaled(self, dve, out, it, n, row):
        m, at = self.mem, it * 2 * CH + n
        return dve.tensor_scalar(out, self.src[:, at, :], m.mean[:, bass.ds(at, 1)], m.rs[:, row, bass.ds(at, 1)],
                                 ALU.subtract, ALU.mult)

    def vector_scale(self, dve, it, amax=None):
        m, d, N = self.mem, self.dve, 2 * CH
        dve.wait_ge(self.pool.sem, self.pool.done(it, "rstd" if self.double else "r1"))
        if self.double or amax is not None:
            for n in range(N):
                last = self.scaled(dve, m.xl[:, it * N + n, :], it, n, 1)
            last.then_inc(d.sem, 1)
        if amax is not None:
            dve.wait_ge(d.sem, d.done(it, "inner"))
            dve.tensor_reduce(amax[:, bass.ds(it, 1)], m.xl[:, bass.ds(it * N, N), :], AX.XY, ALU.max,
                              apply_absolute_value=True).then_inc(d.sem, 1)
            return
        for p in range(2):
            dve.wait_ge(self.pe.sem, self.pe.done(it - 1, f"turned{p}"))
            for j in range(CH):
                last = self.scaled(dve, m.hn[:, p, j, :], it, p * CH + j, 3 if self.double else 1)
            last.then_inc(d.sem, 1)

    def vector_pass(self, dve, amax=None):
        with dve.Fori(0, NIT) as it:
            self.vector_stats(dve, it)
        with dve.Fori(0, NIT) as it:
            self.vector_scale(dve, it, amax)

    def pool_turn(self, pool, it):
        m, g = self.mem, self.pool
        at = bass.ds(it * 2 * CH, 2 * CH)

        def after(name):
            pool.wait_ge(g.sem, g.done(it, name))

        rs = m.rs
        pool.wait_ge(self.stats.sem, self.stats.done(it, "veps"))
        pool.tensor_copy(m.ve[:, 0, :], rs[:, 0, at]).then_inc(g.sem, 1)
        if self.double:
            pool.tensor_copy(m.ve[:, 1, :], rs[:, 5, at]).then_inc(g.sem, 1)
        after("var" if self.double else "veps")
        ve = m.ve
        pool.tensor_tensor(ve[:, 2, :], ve[:, 0, :], m.half[:, 0:2 * CH], ALU.pow).then_inc(g.sem, 1)
        after("pow")
        pool.tensor_copy(rs[:, 1, at], ve[:, 2, :]).then_inc(g.sem, 1)
        if self.double:
            pool.tensor_tensor(ve[:, 3, :], ve[:, 1, :], ve[:, 2, :], ALU.mult).then_inc(g.sem, 1)
            after("a")
            pool.tensor_tensor(ve[:, 4, :], ve[:, 3, :], ve[:, 2, :], ALU.mult).then_inc(g.sem, 1)
            after("b")
            pool.tensor_tensor(ve[:, 3, :], ve[:, 4, :], m.eps[:, 0:2 * CH], ALU.add).then_inc(g.sem, 1)
            after("c")
            pool.tensor_tensor(ve[:, 4, :], ve[:, 3, :], m.half[:, 0:2 * CH], ALU.pow).then_inc(g.sem, 1)
            after("r2")
            pool.tensor_tensor(ve[:, 5, :], ve[:, 4, :], ve[:, 2, :], ALU.mult).then_inc(g.sem, 1)
            after("r12")
            pool.tensor_copy(rs[:, 3, at], ve[:, 5, :]).then_inc(g.sem, 1)

    def tensor_turn(self, pe, it):
        m = self.mem
        for p in range(2):
            pe.wait_ge(self.dve.sem, self.dve.done(it, f"scaled{p}"))
            pe.wait_ge(self.act.sem, self.act.done(it - 1, f"ready{p}"))
            for j in range(CH):
                last = pe.transpose(m.bank(self.banks[p])[:, j * T:(j + 1) * T], m.hn[:, p, j, :], m.mat("ident"))
            last.then_inc(self.pe.sem, 1)

    def scalar_turn(self, act, it):
        m = self.mem
        for p in range(2):
            c = (it * 2 + p) * CH
            act.wait_ge(self.pe.sem, self.pe.done(it, f"turned{p}"))
            out = m.hT[:, bass.ds(c, CH), 1:T + 1]
            src = m.bank(self.banks[p]).rearrange("p (b t) -> p b t", b=CH)
            if self.affine:
                ins = act.activation(out, src, ACT.Identity, bias=m.col(self.affine[1]), scale=m.col(self.affine[0]))
            else:
                ins = act.activation(out, src, ACT.Copy)
            ins.then_inc(self.act.sem, 1)


def chunk(buf, it, p):
    return buf[:, bass.ds((it * 2 + p) * CH, CH), :]


def load_block(nc, mem, ctx, x, pack, rows, b_proj):
    loaded = ctx.enter_context(nc.semaphore("loaded"))
    with nc.Block() as block:
        @block.sync
        def _(sp):
            sp.dma_start(mem.x[:, :, :], x.rearrange("b t c -> t b c")).then_inc(loaded, 16)
            sp.dma_start(mem.pack[:, :], pack).then_inc(loaded, 16)
            sp.dma_start(mem.rows[:, :], rows).then_inc(loaded, 16)
            sp.dma_start(mem.b_proj[:, :], b_proj).then_inc(loaded, 16)
            sp.wait_ge(loaded, 64)

        @block.gpsimd
        def _(pool):
            pool.memset(mem.ones[:, :], 1.0)
            pool.memset(mem.half[:, :], -0.5)
            pool.memset(mem.eps[:, :], EPS)
            pool.memset(mem.hT[:, :, 0:1], 0.0)


def time_mix_block(nc, mem, ctx):
    def sem(n):
        return ctx.enter_context(nc.semaphore(n))

    mem.restart()
    PAD = T + 1
    kp = mem.take(B, PAD)
    vT = mem.take(B, T)
    sr = mem.take(B, T)
    mark = mem.at
    mixd = mem.take(W)
    mixed = mem.take(2, 3, W)
    wpad = mem.take(CH, PAD)
    wneg = mem.take(2)
    P = mem.take(2, CH, PAD)
    expo = mem.take(2, 4, CH, T)
    keep = mem.take(2, 2, CH, PAD)
    outw = mem.take(2, 2, CH, T)
    qmax = mem.take(2, CH, T)
    bv = mem.take(2, CH, PAD)
    aa = mem.take(2, CH, PAD)
    bb = mem.take(2, CH, PAD)
    num = mem.take(2, 2, CH, T)
    rw = mixed[:, :, 0]
    den = [mixed[:, p, 1].rearrange("p (b t) -> p b t", b=CH) for p in range(2)]
    inv = [mixed[:, p, 2].rearrange("p (b t) -> p b t", b=CH) for p in range(2)]
    top = mem.at
    mem.at = mark + W + 6 * W
    relu = mem.take(4, W)
    kk = mem.take(2, CH, W)
    gate = mem.take(2, W)
    gated = mem.take(2, W)
    mem.at = max(mem.at, top)

    n1 = Norm(nc, mem, ctx, "n1", mem.x, double=True, affine=("ln1_w", "ln1_b"))
    n2 = Norm(nc, mem, ctx, "n2", mem.xl, affine=("ln2_w", "ln2_b"))
    init = Steps(sem("tm_init_pool"), "kp keep bv wpad")
    idec = Steps(sem("tm_init_act"), "exp")
    iw = Steps(sem("tm_init_dve"), "neg wpad")
    md = Steps(sem("mix_dve"), "d0 k0 v0 r0 d1 k1 v1 r1", 1)
    mp = Steps(sem("mix_pe"), "k0 v0 r0 k1 v1 r1", 1)
    ma = Steps(sem("mix_act"), "k0 v0 r0 k1 v1 r1", 1)
    wd = Steps(sem("wkv_dve"), "P0 P1 decay0 q0 decay1 q1 ww0 ww1 bb0 aa0 bb1 aa1 d10 d11 den0 n10 den1 n11 "
               "num0 num1 y0 y1 rw0 rw1", 1)
    wo = Steps(sem("wkv_add"), "add0 add1")
    wp = Steps(sem("wkv_pool"), "key0 key1 past0 past1 bv0 bv1 n20 n21", 1)
    wa = Steps(sem("wkv_act"), "keep0 keep1 outw0 outw1 ln0 inv0 ln1 inv1", 1)
    we = Steps(sem("wkv_pe"), "out0 out1", 1)
    cx = Steps(sem("cm_mix"), "d0 k0 r0 d1 k1 r1", 1)
    cs = Steps(sem("cm_square"), "sq00 sq02 sq10 sq12", 1)
    cd = Steps(sem("cm_add"), "res0 res1 gated0 add0 gated1 add1", 1)
    ce = Steps(sem("cm_pe"), "key00 key01 key02 key03 rec0 key10 key11 key12 key13 rec1 val0 val1", 1)
    ca = Steps(sem("cm_act"), "relu00 relu01 sq01 relu02 relu03 sq03 gate0 relu10 relu11 sq11 relu12 relu13 sq13 gate1", 1)
    bank = mem.bank

    def batches(v):
        return v.rearrange("p (b t) -> p b t", b=CH)

    with nc.Block() as block:
        @block.gpsimd
        def _(pool):
            pool.memset(kp[:, :, 0:1], NEG).then_inc(init.sem, 1)
            pool.memset(keep[:, :, :, :, :], 0.0).then_inc(init.sem, 1)
            pool.memset(bv[:, :, :, :], 0.0).then_inc(init.sem, 1)
            pool.memset(wpad[:, :, :], NEG).then_inc(init.sem, 1)
            pool.sem_inc(wp.sem, wp.credit())
            with pool.Fori(0, NIT) as it:
                n1.pool_turn(pool, it)
            with pool.Fori(0, NIT) as it:
                for p in range(2):
                    pool.wait_ge(wd.sem, wd.done(it, f"P{p}"))
                    pool.wait_ge(wa.sem, wa.done(it - 1, f"outw{p}"))
                    pool.tensor_tensor(expo[:, p, 1], chunk(kp, it, p)[:, :, 1:PAD], P[:, p, :, 1:PAD],
                                       ALU.subtract).then_inc(wp.sem, 1)
                for p in range(2):
                    pool.wait_ge(wd.sem, wd.done(it, f"q{p}"))
                    pool.tensor_tensor(expo[:, p, 2], P[:, p, :, 0:T], qmax[:, p], ALU.subtract).then_inc(wp.sem, 1)
                for p in range(2):
                    pool.wait_ge(wa.sem, wa.done(it, f"keep{p}"))
                    pool.wait_ge(wd.sem, wd.done(it - 1, f"aa{p}"))
                    pool.tensor_tensor(bv[:, p, :, 1:PAD], keep[:, p, 1, :, 1:PAD], chunk(vT, it, p), ALU.mult).then_inc(wp.sem, 1)
                for p in range(2):
                    pool.wait_ge(wa.sem, wa.done(it, f"outw{p}"))
                    pool.wait_ge(wd.sem, wd.done(it, f"aa{p}"))
                    pool.wait_ge(wd.sem, wd.done(it - 1, f"num{p}"))
                    pool.tensor_tensor(num[:, p, 1], outw[:, p, 0], aa[:, p, :, 0:T], ALU.mult).then_inc(wp.sem, 1)
            with pool.Fori(0, NIT) as it:
                n2.pool_turn(pool, it)

        @block.vector
        def _(dve):
            for s in (n1.stats, n2.stats, md, wd, cx, cs, cd):
                dve.sem_inc(s.sem, s.credit())
            n1.vector_pass(dve)
            dve.wait_ge(idec.sem, 1)
            dve.tensor_scalar(wneg[:, 1:2], wneg[:, 0:1], -1.0, None, ALU.mult).then_inc(iw.sem, 1)
            dve.wait_ge(iw.sem, 1)
            dve.wait_ge(init.sem, 4)
            dve.tensor_scalar(wpad[:, :, 1:PAD],
                              mem.x[:, 0:CH, :], 0.0, wneg[:, 1:2], ALU.mult, ALU.add).then_inc(iw.sem, 1)
            with dve.Fori(0, NIT) as it:
                for p in range(2):
                    hc = chunk(mem.hT, it, p)
                    h, hh = hc[:, :, 1:T + 1], hc[:, :, 0:T]
                    dve.wait_ge(n1.act.sem, n1.act.done(it, f"ready{p}"))
                    dve.wait_ge(md.sem, md.previous(it, p, "r"))
                    dve.tensor_tensor(batches(mixd[:, :]), h, hh, ALU.subtract).then_inc(md.sem, 1)
                    dve.wait_ge(md.sem, md.done(it, f"d{p}"))
                    for i, name in enumerate("kvr"):
                        dve.wait_ge(mp.sem, mp.done(it - 1, f"{name}{p}"))
                        dve.scalar_tensor_tensor(batches(mixed[:, p, i]), batches(mixd[:, :]), mem.col(f"tm{name}"), hh,
                                                 ALU.mult, ALU.add).then_inc(md.sem, 1)
            with dve.Fori(0, NIT) as it:
                k = [chunk(kp, it, p)[:, :, 1:PAD] for p in range(2)]
                past, now = [P[:, p, :, 0:T] for p in range(2)], [P[:, p, :, 1:PAD] for p in range(2)]

                def flat(v):
                    return v.rearrange("p b t -> p (b t)")

                def after(name):
                    dve.wait_ge(wd.sem, wd.done(it, name))

                for p in range(2):
                    dve.wait_ge(ma.sem, ma.done(it, f"r{p}"))
                    dve.wait_ge(iw.sem, 2)
                    dve.wait_ge(wp.sem, wp.done(it - 1, f"past{p}"))
                    dve.tensor_tensor_scan(flat(P[:, p]), flat(wpad), flat(chunk(kp, it, p)), NEG,
                                           ALU.add, ALU.max).then_inc(wd.sem, 1)
                for p in range(2):
                    after(f"P{p}")
                    dve.wait_ge(wa.sem, wa.done(it - 1, f"outw{p}"))
                    dve.scalar_tensor_tensor(expo[:, p, 0], past[p], wneg[:, 1:2], now[p],
                                             ALU.add, ALU.subtract).then_inc(wd.sem, 1)
                    dve.scalar_tensor_tensor(qmax[:, p], k[p], mem.col("first"), past[p],
                                             ALU.add, ALU.max).then_inc(wd.sem, 1)
                for p in range(2):
                    after(f"q{p}")
                    dve.scalar_tensor_tensor(expo[:, p, 3], k[p], mem.col("first"), qmax[:, p],
                                             ALU.add, ALU.subtract).then_inc(wd.sem, 1)
                for p in range(2):
                    dve.wait_ge(wa.sem, wa.done(it, f"keep{p}"))
                    dve.tensor_tensor_scan(flat(bb[:, p]), flat(keep[:, p, 0]), flat(keep[:, p, 1]), 0.0,
                                           ALU.mult, ALU.add).then_inc(wd.sem, 1)
                    dve.wait_ge(wp.sem, wp.done(it, f"bv{p}"))
                    dve.tensor_tensor_scan(flat(aa[:, p]), flat(keep[:, p, 0]), flat(bv[:, p]), 0.0,
                                           ALU.mult, ALU.add).then_inc(wd.sem, 1)
                dve.wait_ge(mp.sem, mp.done(NIT - 1, "r1"))
                for p in range(2):
                    after(f"bb{p}")
                    dve.wait_ge(wa.sem, wa.done(it, f"outw{p}"))
                    dve.tensor_tensor(den[p], outw[:, p, 0], bb[:, p, :, 0:T], ALU.mult).then_inc(wd.sem, 1)
                for p in range(2):
                    after(f"d1{p}")
                    dve.tensor_tensor(den[p], den[p], outw[:, p, 1], ALU.add).then_inc(wd.sem, 1)
                    dve.tensor_tensor(num[:, p, 0], outw[:, p, 1], chunk(vT, it, p), ALU.mult).then_inc(wd.sem, 1)
                for p in range(2):
                    after(f"n1{p}")
                    dve.wait_ge(wp.sem, wp.done(it, f"n2{p}"))
                    dve.tensor_tensor(num[:, p, 0], num[:, p, 0], num[:, p, 1], ALU.add).then_inc(wd.sem, 1)
                for p in range(2):
                    after(f"num{p}")
                    dve.wait_ge(wa.sem, wa.done(it, f"inv{p}"))
                    dve.tensor_tensor(num[:, p, 0], num[:, p, 0], inv[p], ALU.mult).then_inc(wd.sem, 1)
                for p in range(2):
                    after(f"y{p}")
                    dve.wait_ge(we.sem, we.done(it - 1, f"out{p}"))
                    dve.tensor_tensor(batches(rw[:, p]), num[:, p, 0], chunk(sr, it, p), ALU.mult).then_inc(wd.sem, 1)
            with dve.Fori(0, NIT) as it:
                for p in range(2):
                    xl = chunk(mem.xl, it, p)
                    dve.wait_ge(we.sem, we.done(it, f"out{p}"))
                    dve.tensor_tensor(xl, xl, batches(mem.ps[:, bass.ds((it * 2 + p) * W, W)]), ALU.add).then_inc(wo.sem, 1)
            dve.wait_ge(wo.sem, wo.done(NIT - 1, "add1"))
            n2.vector_pass(dve)

            def mix(it):
                for p in range(2):
                    hc = chunk(mem.hT, it, p)
                    h, hh = hc[:, :, 1:T + 1], hc[:, :, 0:T]
                    dve.wait_ge(n2.act.sem, n2.act.done(it, f"ready{p}"))
                    dve.wait_ge(cx.sem, cx.previous(it, p, "r"))
                    dve.tensor_tensor(batches(mixd[:, :]), h, hh, ALU.subtract).then_inc(cx.sem, 1)
                    dve.wait_ge(cx.sem, cx.done(it, f"d{p}"))
                    dve.wait_ge(ce.sem, ce.done(it - 1, f"rec{p}"))
                    for i, name in enumerate("kr"):
                        dve.scalar_tensor_tensor(batches(mixed[:, p, i]), batches(mixd[:, :]), mem.col(f"ftm{name}"), hh,
                                                 ALU.mult, ALU.add).then_inc(cx.sem, 1)

            def squares(it):
                for p in range(2):
                    for k in (0, 2):
                        dve.wait_ge(ca.sem, ca.done(it, f"relu{p}{k}"))
                        dve.wait_ge(ce.sem, ce.done(it - 1, f"val{p}"))
                        dve.tensor_tensor(kk[:, p, k], relu[:, k], relu[:, k], ALU.mult).then_inc(cs.sem, 1)

            def add(it):
                for p in range(2):
                    x = chunk(mem.x, it, p)
                    dve.tensor_tensor(x, x, chunk(mem.xl, it, p), ALU.add).then_inc(cd.sem, 1)
                for p in range(2):
                    x = chunk(mem.x, it, p)
                    dve.wait_ge(ca.sem, ca.done(it, f"gate{p}"))
                    dve.wait_ge(ce.sem, ce.done(it, f"val{p}"))
                    dve.tensor_tensor(gated[:, p], gate[:, p], bank(6 + p)[:, :], ALU.mult).then_inc(cd.sem, 1)
                    dve.wait_ge(cd.sem, cd.done(it, f"gated{p}"))
                    dve.tensor_tensor(x, x, batches(gated[:, p]), ALU.add).then_inc(cd.sem, 1)

            mix(0)
            with dve.Fori(0, NIT - 1) as it:
                squares(it)
                mix(it + 1)
                add(it)
            squares(NIT - 1)
            add(NIT - 1)

        @block.scalar
        def _(act):
            for s in (n1.act, n2.act, ma, wa, ca):
                act.sem_inc(s.sem, s.credit())
            act.activation(wneg[:, 0:1], mem.col("decay"), ACT.Exp).then_inc(idec.sem, 1)
            with act.Fori(0, NIT) as it:
                n1.scalar_turn(act, it)
            act.preload_act_table(ACT.Sigmoid)
            with act.Fori(0, NIT) as it:
                for p in range(2):
                    act.wait_ge(mp.sem, mp.done(it, f"k{p}"))
                    act.wait_ge(init.sem, 1)
                    act.activation(chunk(kp, it, p)[:, :, 1:PAD], batches(bank(p)[:, :]), ACT.Copy).then_inc(ma.sem, 1)
                    act.wait_ge(mp.sem, mp.done(it, f"v{p}"))
                    act.activation(chunk(vT, it, p), batches(bank(2 + p)[:, :]), ACT.Copy).then_inc(ma.sem, 1)
                    act.wait_ge(mp.sem, mp.done(it, f"r{p}"))
                    act.activation(chunk(sr, it, p), batches(bank(4 + p)[:, :]), ACT.Sigmoid).then_inc(ma.sem, 1)
            act.preload_act_table_set("natural_log_exp_and_others")
            act.wait_ge(init.sem, 3)
            with act.Fori(0, NIT) as it:
                for p in range(2):
                    act.wait_ge(wd.sem, wd.done(it, f"decay{p}"))
                    act.wait_ge(wp.sem, wp.done(it, f"key{p}"))
                    act.wait_ge(wd.sem, wd.done(it - 1, f"bb{p}"))
                    act.wait_ge(wd.sem, wd.done(it - 1, f"aa{p}"))
                    act.activation(keep[:, p].rearrange("p a b t -> p (a b) t")[:, :, 1:PAD],
                                   expo[:, p, 0:2].rearrange("p a b t -> p (a b) t"), ACT.Exp).then_inc(wa.sem, 1)
                for p in range(2):
                    act.wait_ge(wd.sem, wd.done(it, f"ww{p}"))
                    act.wait_ge(wp.sem, wp.done(it, f"past{p}"))
                    act.wait_ge(wd.sem, wd.done(it - 1, f"n1{p}"))
                    act.wait_ge(wp.sem, wp.done(it - 1, f"n2{p}"))
                    act.activation(outw[:, p].rearrange("p a b t -> p (a b t)"),
                                   expo[:, p, 2:4].rearrange("p a b t -> p (a b t)"), ACT.Exp).then_inc(wa.sem, 1)
                for p in range(2):
                    act.wait_ge(wd.sem, wd.done(it, f"den{p}"))
                    act.wait_ge(wd.sem, wd.done(it - 1, f"y{p}"))
                    act.activation(inv[p], den[p], ACT.Ln).then_inc(wa.sem, 1)
                    act.wait_ge(wa.sem, wa.done(it, f"ln{p}"))
                    act.activation(inv[p], inv[p], ACT.Exp, scale=-1.0).then_inc(wa.sem, 1)
            with act.Fori(0, NIT) as it:
                n2.scalar_turn(act, it)
            act.preload_act_table(ACT.Sigmoid)
            with act.Fori(0, NIT) as it:
                for p in range(2):
                    for k in range(4):
                        act.wait_ge(ce.sem, ce.done(it, f"key{p}{k}"))
                        turn, before = (it, 0) if p else (it - 1, 1)
                        squared = cs if k % 2 == 0 else ca
                        act.wait_ge(squared.sem, squared.done(turn, f"sq{before}{k}"))
                        act.activation(relu[:, k], bank(k)[:, :], ACT.Relu).then_inc(ca.sem, 1)
                        if k % 2 == 1:
                            act.wait_ge(ca.sem, ca.done(it, f"relu{p}{k}"))
                            act.wait_ge(ce.sem, ce.done(it - 1, f"val{p}"))
                            act.activation(kk[:, p, k], relu[:, k], ACT.Square).then_inc(ca.sem, 1)
                    act.wait_ge(ce.sem, ce.done(it, f"rec{p}"))
                    act.wait_ge(cd.sem, cd.done(it - 1, f"gated{p}"))
                    act.activation(gate[:, p], bank(4 + p)[:, :], ACT.Sigmoid).then_inc(ca.sem, 1)

        @block.tensor
        def _(pe):
            for s in (n1.pe, n2.pe, mp, we, ce):
                pe.sem_inc(s.sem, s.credit())
            with pe.Fori(0, NIT) as it:
                n1.tensor_turn(pe, it)
            with pe.Fori(0, NIT) as it:
                for p in range(2):
                    for i, name in enumerate("kvr"):
                        pe.wait_ge(md.sem, md.done(it, f"{name}{p}"))
                        pe.wait_ge(ma.sem, ma.done(it - 1, f"{name}{p}"))
                        pe.matmul(bank(2 * i + p)[:, :], mem.mat(f"W{name}T"), mixed[:, p, i], start=True, stop=True).then_inc(mp.sem, 1)
            with pe.Fori(0, NIT) as it:
                for p in range(2):
                    pe.wait_ge(wd.sem, wd.done(it, f"rw{p}"))
                    for j in range(CH):
                        out = mem.ps[:, bass.ds((it * 2 + p) * W + j * T, T)]
                        last = pe.matmul(out, rw[:, p, j * T:(j + 1) * T], mem.mat("WoT"),
                                         start=True, stop=True)
                    last.then_inc(we.sem, 1)
            with pe.Fori(0, NIT) as it:
                n2.tensor_turn(pe, it)
            with pe.Fori(0, NIT) as it:
                for p in range(2):
                    pe.wait_ge(cx.sem, cx.done(it, f"k{p}"))
                    for k in range(4):
                        pe.wait_ge(ca.sem, ca.done(it, f"relu0{k}") if p else ca.done(it - 1, f"relu1{k}"))
                        pe.matmul(bank(k)[:, :], mem.mat("WkeyT", k), mixed[:, p, 0], start=True, stop=True).then_inc(ce.sem, 1)
                    pe.wait_ge(cx.sem, cx.done(it, f"r{p}"))
                    pe.wait_ge(ca.sem, ca.done(it - 1, f"gate{p}"))
                    for j in range(CH):
                        last = pe.matmul(bank(4 + p)[:, j * T:(j + 1) * T], mixed[:, p, 1, j * T:(j + 1) * T], mem.mat("WrecT"),
                                         start=True, stop=True)
                    last.then_inc(ce.sem, 1)
                for p in range(2):
                    pe.wait_ge(cs.sem, cs.done(it, f"sq{p}2"))
                    pe.wait_ge(ca.sem, ca.done(it, f"sq{p}3"))
                    pe.wait_ge(cd.sem, cd.done(it - 1, f"gated{p}"))
                    for j in range(CH):
                        for k in range(4):
                            last = pe.matmul(bank(6 + p)[:, j * T:(j + 1) * T], kk[:, p, k, j * T:(j + 1) * T],
                                             mem.mat("WvalT", k), start=(k == 0), stop=(k == 3))
                    last.then_inc(ce.sem, 1)


KEPT_WORDS = B * S + B * C
KV_WORDS = 2 * KEPT_WORDS


def kv_views(mem):
    keys, values = [None, None], [None, None]
    for l in range(2):
        o = 0 if l == 1 else KEPT_WORDS
        keys[l] = mem.arena[:, o:o + B * S].rearrange("p (b s) -> p b s", b=B)
        values[l] = mem.arena[:, o + B * S:o + KEPT_WORDS].rearrange("p (b c) -> p b c", b=B)
    return keys, values


class Context:

    def __init__(self, nc, mem, ctx, tokens):
        def sem(n):
            return ctx.enter_context(nc.semaphore(n))

        self.mem = mem
        self.keys, self.values = kv_views(mem)
        self.cn = mem.take(2, CH, C)
        self.cT = mem.take(2, CH * S)
        self.loaded = [sem("ctx_loaded0"), sem("ctx_loaded1")]
        self.pe = Steps(sem("ctx_pe"), "turned0 turned1 k00 k10 v00 v10 k01 k11 v01 v11", 1)
        self.act = Steps(sem("ctx_act"), "cT0 cT1 k00 k10 v00 v10 k01 k11 v01 v11", 1)
        self.src = tokens.rearrange("b s c -> s b c")

    def load_turn(self, sp, it):
        for p in range(2):
            sp.wait_ge(self.pe.sem, self.pe.done(it - 1, f"turned{p}"))
            sp.dma_start(self.cn[0:S, p], self.src[:, bass.ds((it * 2 + p) * CH, CH), :]).then_inc(self.loaded[p], 16)

    def tensor_turn(self, pe, it):
        mem, e, a = self.mem, self.pe, self.act
        for p in range(2):
            pe.wait_ge(self.loaded[p], it * 16 + 16)
            pe.wait_ge(a.sem, a.done(it - 1, f"cT{p}"))
            for j in range(CH):
                last = pe.transpose(mem.bank(4 + p)[:, j * S:(j + 1) * S], self.cn[0:S, p, j, :], mem.mat("ident")[0:S, 0:S])
            last.then_inc(e.sem, 1)
        for p in range(2):
            pe.wait_ge(a.sem, a.done(it, f"cT{p}"))
            for l in range(2):
                pe.wait_ge(a.sem, a.previous(it, p, f"k{l}"))
                pe.matmul(mem.bank(l)[:, 0:CH * S], mem.mat(f"kT{l}"), self.cT[:, p], start=True, stop=True).then_inc(e.sem, 1)
            for l in range(2):
                pe.wait_ge(a.sem, a.previous(it, p, f"v{l}"))
                for j in range(CH):
                    last = pe.matmul(mem.bank(2 + l)[0:S, j * C:(j + 1) * C], self.cT[:, p, j * S:(j + 1) * S],
                                     mem.mat(f"vT{l}"), start=True, stop=True)
                last.then_inc(e.sem, 1)

    def scalar_turn(self, act, it):
        mem, e, a = self.mem, self.pe, self.act
        for p in range(2):
            act.wait_ge(e.sem, e.done(it, f"turned{p}"))
            act.wait_ge(e.sem, e.done(it - 1, f"v1{p}"))
            act.activation(self.cT[:, p], mem.bank(4 + p)[:, 0:CH * S], ACT.Copy).then_inc(a.sem, 1)
        for p in range(2):
            for l in range(2):
                act.wait_ge(e.sem, e.done(it, f"k{l}{p}"))
                out, src = chunk(self.keys[l], it, p), mem.bank(l)[:, 0:CH * S].rearrange("p (b s) -> p b s", b=CH)
                if l == 0:
                    ins = act.activation(out, src, ACT.Identity, bias=mem.col("bk"))
                else:
                    ins = act.activation(out, src, ACT.Copy)
                ins.then_inc(a.sem, 1)
            for l in range(2):
                act.wait_ge(e.sem, e.done(it, f"v{l}{p}"))
                act.activation(chunk(self.values[l][0:S], it, p), mem.bank(2 + l)[0:S, :].rearrange("p (b c) -> p b c", b=CH),
                               ACT.Copy).then_inc(a.sem, 1)


def attention_block(nc, mem, ctx, layer, v_mask_in, tokens):
    def sem(n):
        return ctx.enter_context(nc.semaphore(f"at{layer}_{n}"))

    causal = layer == 0
    keys, values = kv_views(mem)
    kT, vals = keys[layer], values[layer]
    mem.at = KV_WORDS
    NB = 2 * CH
    qT = mem.take(2, W)
    km = mem.take(2, H, S)
    vm = mem.take(2, 4, C)
    v_mask = mem.take(4, C)
    shifted = mem.take(2, H, S)
    mx = mem.take(2, H)
    prob = mem.take(2, H, S)
    pT = mem.take(4, 4 * T)
    rden = mem.take(T)
    oT = mem.take(2, CH, T)
    bias = mem.take(C)
    bias_row = mem.take(C)
    causal_b = mem.take(4 * S // 2).bitcast(BF16)
    ident_b = mem.take(64).bitcast(BF16)
    context = Context(nc, mem, ctx, tokens) if causal else None
    norm = Norm(nc, mem, ctx, f"at{layer}n", mem.x)
    masks = sem("masks")
    setup, padded = sem("setup"), sem("padded")
    bias_pe, bias_dve = sem("bias_pe"), sem("bias_dve")

    e = Steps(sem("pe_scores"), "q0 S0 S1 S2 q1 S3 S4 S5 S6 S7", 1)
    d = Steps(sem("dve_scores"), " ".join(f"max{n} sub{n}" for n in range(NB)), 1)
    a = Steps(sem("act_scores"), "q0 exp0 exp1 exp2 q1 exp3 exp4 exp5 exp6 exp7", 1)
    ef = Steps(sem("pe_out"), " ".join(f"T{n}0 T{n}1 T{n}2 T{n}3 O{n}" + f" out{n // CH}" * (n % CH == CH - 1)
                                       for n in range(NB)), 1)
    df = Steps(sem("dve_out"), " ".join(f"rec{n} o{n}" + f" add{n // CH}" * (n % CH == CH - 1) for n in range(NB)), 1)
    af = Steps(sem("act_out"), " ".join(f"p{n}0 p{n}1 p{n}2 p{n}3" for n in range(NB)), 1)
    g = Steps(sem("pool"), " ".join(f"km{n} vm{n}" for n in range(NB)), 1)
    gb = Steps(sem("pool_bias"), "bias0 bias1")
    bank = mem.bank
    scores = mem.ps[:, 0:4 * W].rearrange("p (g w) -> p g w", g=4)[:, :, 0:4 * S].rearrange("p g (j s) -> p g j s", j=4)

    def by_group(v):
        return v.rearrange("p (g j) s -> p g j s", g=4)

    def n_of(steps, it, name, n, more=""):
        return steps.done(it, f"{name}{n}{more}") if n >= 0 else steps.done(it - 1, f"{name}{n + NB}{more}")

    def turns(eng, first, second, late=None):
        def turn(it, more):
            for n in range(NB):
                ahead = (it, n + 1) if n + 1 < NB else (it + 1, 0)
                if n + 1 < NB or more:
                    first(*ahead)
                second(it, n)
                if late and (n + 1 < NB or more):
                    late(*ahead)

        first(0, 0)
        if late:
            late(0, 0)
        with eng.Fori(0, NIT - 1) as it:
            turn(it, True)
        turn(NIT - 1, False)

    with nc.Block() as block:
        @block.sync
        def _(sp):
            sp.dma_start(v_mask[:, :, :], v_mask_in).then_inc(masks, 16)
            if context:
                with sp.Fori(0, NIT) as it:
                    context.load_turn(sp, it)
            sp.wait_ge(masks, 16)

        @block.gpsimd
        def _(pool):
            pool.sem_inc(g.sem, g.credit())
            pool.memset(pT[64:128, :, :], 0.0).then_inc(padded, 1)
            pool.memset(vm[64:128, :, :, :], 0.0).then_inc(padded, 1)
            pool.wait_ge(padded, 2)
            pool.wait_ge(masks, 16)
            with pool.Fori(0, NIT) as it:
                norm.pool_turn(pool, it)
            if context:
                pool.wait_ge(context.act.sem, context.act.done(NIT - 1, "v11"))
            pool.wait_ge(norm.dve.sem, norm.dve.done(NIT - 1, "scaled1"))
            pool.wait_ge(bias_dve, 2)
            with pool.Fori(0, NIT) as it:
                for n in range(NB):
                    p, b = n // CH, n % CH
                    at = (it * 2 + p) * CH + b
                    pool.wait_ge(e.sem, n_of(e, it, "S", n - 2))
                    pool.tensor_tensor(km[:, n % 2], kT[:, bass.ds(at, 1), :].broadcast_to([128, H, S]),
                                       mem.mat("head_mask", 0, H).unsqueeze(2).broadcast_to([128, H, S]), ALU.mult).then_inc(g.sem, 1)
                    pool.wait_ge(ef.sem, n_of(ef, it, "O", n - 2))
                    vc = vals[0:S, bass.ds(at, 1), :]
                    pool.tensor_tensor(vm[0:S, n % 2], vc.broadcast_to([S, 4, C]), v_mask[0:S], ALU.mult).then_inc(g.sem, 1)
                    if b == 1:
                        x = chunk(mem.x, it, p)
                        pool.tensor_tensor(x, x, bias.unsqueeze(1).broadcast_to([128, CH, C]), ALU.add).then_inc(gb.sem, 1)

        @block.vector
        def _(dve):
            for s in (norm.stats, d, df):
                dve.sem_inc(s.sem, s.credit())
            if causal:
                dve.tensor_copy(causal_b.rearrange("p (j s) -> p j s", j=4),
                                mem.mat("causal", 0, S).unsqueeze(1).broadcast_to([128, 4, S])).then_inc(setup, 1)
                dve.tensor_copy(ident_b, mem.mat("ident")).then_inc(setup, 1)
            norm.vector_pass(dve)
            if causal:
                dve.wait_ge(bias_pe, 1)
                dve.tensor_tensor(bias_row[0:1, :], mem.row("bo0"), bank(5)[0:1, 0:C], ALU.add).then_inc(bias_dve, 1)
            else:
                dve.tensor_copy(bias_row[0:1, :], mem.row("bo1")).then_inc(bias_dve, 1)
            dve.wait_ge(bias_pe, 2)
            dve.tensor_copy(bias[:, :], bank(5)[:, C:2 * C]).then_inc(bias_dve, 1)

            def first(it, n):
                dve.wait_ge(e.sem, e.done(it, f"S{n}"))
                dve.wait_ge(d.sem, n_of(d, it, "sub", n - 2))
                dve.tensor_reduce(by_group(mx[:, n % 2].unsqueeze(2))[:, :, :, 0], scores, AX.X, ALU.max).then_inc(d.sem, 1)
                dve.wait_ge(d.sem, d.done(it, f"max{n}"))
                dve.wait_ge(a.sem, n_of(a, it, "exp", n - 2))
                dve.tensor_tensor(by_group(shifted[:, n % 2]), scores,
                                  by_group(mx[:, n % 2].unsqueeze(2).broadcast_to([128, H, S])), ALU.subtract).then_inc(d.sem, 1)

            def second(it, n):
                p = n // CH
                dve.wait_ge(ef.sem, ef.done(it, f"O{n}"))
                dve.wait_ge(df.sem, n_of(df, it, "o", n - 1))
                dve.reciprocal(rden[:, :], bank(7)[:, 0:T]).then_inc(df.sem, 1)
                dve.wait_ge(df.sem, df.done(it, f"rec{n}"))
                dve.wait_ge(ef.sem, ef.done(it - 1, f"out{p}"))
                dve.tensor_tensor(oT[:, p, n % CH], bank(6)[:, 0:T], rden[:, :], ALU.mult).then_inc(df.sem, 1)
                if n % CH == CH - 1:
                    x = chunk(mem.x, it, p)
                    dve.wait_ge(ef.sem, ef.done(it, f"out{p}"))
                    dve.wait_ge(gb.sem, gb.done(it, f"bias{p}"))
                    dve.tensor_tensor(x, x, bank(6)[:, :].rearrange("p (b c) -> p b c", b=CH), ALU.add).then_inc(df.sem, 1)

            turns(dve, first, second)

        @block.scalar
        def _(act):
            for s in (norm.act, a, af) + ((context.act,) if context else ()):
                act.sem_inc(s.sem, s.credit())
            act.preload_act_table(ACT.Exp)
            if context:
                with act.Fori(0, NIT) as it:
                    context.scalar_turn(act, it)
            with act.Fori(0, NIT) as it:
                norm.scalar_turn(act, it)

            act.wait_ge(padded, 2)

            def queries(it, n):
                for q in range(2):
                    if n == (0, CH - 1)[q]:
                        act.wait_ge(e.sem, e.done(it, f"q{q}"))
                        act.wait_ge(e.sem, e.done(it - 1, f"S{CH * q + CH - 1}"))
                        if causal:
                            ins = act.activation(qT[:, q], bank(5)[:, :], ACT.Identity, bias=mem.col("bq"))
                        else:
                            ins = act.activation(qT[:, q], bank(5)[:, :], ACT.Copy)
                        ins.then_inc(a.sem, 1)

            def exponentials(it, n):
                act.wait_ge(d.sem, d.done(it, f"sub{n}"))
                act.wait_ge(ef.sem, n_of(ef, it, "T", n - 2, "3"))
                act.activation(prob[:, n % 2].rearrange("p h s -> p (h s)"), shifted[:, n % 2].rearrange("p h s -> p (h s)"),
                               ACT.Exp, scale=ATT_SCALE).then_inc(a.sem, 1)

            def second(it, n):
                for j in range(4):
                    act.wait_ge(ef.sem, ef.done(it, f"T{n}{j}"))
                    act.wait_ge(ef.sem, n_of(ef, it, "O", n - 1))
                    act.activation(pT[0:S, j], bank(4 + j % 2)[0:S, :], ACT.Copy).then_inc(af.sem, 1)

            turns(act, queries, second, exponentials)

        @block.tensor
        def _(pe):
            for s in (norm.pe, e, ef) + ((context.pe,) if context else ()):
                pe.sem_inc(s.sem, s.credit())
            if context:
                with pe.Fori(0, NIT) as it:
                    context.tensor_turn(pe, it)
                pe.wait_ge(context.act.sem, context.act.done(NIT - 1, "v11"))
                pe.matmul(bank(5)[0:1, 0:C], mem.col("bv"), mem.mat("oT0"), start=True, stop=True).then_inc(bias_pe, 1)
            else:
                pe.sem_inc(bias_pe, 1)
            with pe.Fori(0, NIT) as it:
                norm.tensor_turn(pe, it)
            pe.wait_ge(bias_dve, 1)
            pe.matmul(bank(5)[:, C:2 * C], mem.ones[0:1, :], bias_row[0:1, :], start=True, stop=True).then_inc(bias_pe, 1)
            pe.wait_ge(bias_dve, 2)
            pe.wait_ge(norm.act.sem, norm.act.done(NIT - 1, "ready1"))
            if causal:
                pe.wait_ge(setup, 2)

            pe.wait_ge(padded, 2)
            pe.wait_ge(masks, 16)

            def first(it, n):
                p, b = n // CH, n % CH
                for q in range(2):
                    if n == (0, CH - 1)[q]:
                        pe.wait_ge(af.sem, n_of(af, it, "p", n - 2, "3"))
                        pe.matmul(bank(5)[:, :].rearrange("p (b t) -> p b t", b=CH), mem.mat(f"qT{layer}"),
                                  chunk(mem.hT, it, q)[:, :, 1:T + 1], start=True, stop=True).then_inc(e.sem, 1)
                pe.wait_ge(a.sem, a.done(it, f"q{p}"))
                pe.wait_ge(g.sem, g.done(it, f"km{n}"))
                pe.wait_ge(d.sem, n_of(d, it, "sub", n - 1))
                for grp in range(4):
                    out = bank(grp)[:, 0:4 * S]
                    last = pe.matmul(out, qT[:, p, b * T:(b + 1) * T],
                                     km[:, n % 2, 4 * grp:4 * grp + 4].rearrange("p j s -> p (j s)"),
                                     start=True, stop=not causal)
                    if causal:
                        last = pe.matmul(out, ident_b, causal_b, start=False, stop=True)
                last.then_inc(e.sem, 1)

            def second(it, n):
                p = n // CH

                def turn(j):
                    pe.wait_ge(af.sem, af.done(it, f"p{n}{j - 2}") if j >= 2 else n_of(af, it, "p", n - 1, f"{j + 2}"))
                    if n == CH - 2 and j == 1:
                        pe.wait_ge(a.sem, a.done(it, "q1"))
                    for grp in range(4):
                        last = pe.transpose(bank(4 + j % 2)[0:S, grp * T:(grp + 1) * T], prob[:, n % 2, 4 * grp + j, :],
                                            mem.mat("ident"))
                    last.then_inc(ef.sem, 1)

                def weigh(j):
                    pe.wait_ge(af.sem, af.done(it, f"p{n}{j}"))
                    for out, lhs in ((bank(6), vm[:, n % 2, j]), (bank(7), v_mask[:, j])):
                        for grp in range(4):
                            rows = slice(32 * grp, 32 * grp + 32)
                            last = pe.matmul(out[rows, 0:T], lhs[:, rows],
                                             pT[:, j, grp * T:(grp + 1) * T], start=(j == 0), stop=(j == 3))
                    return last

                pe.wait_ge(a.sem, a.done(it, f"exp{n}"))
                turn(0)
                turn(1)
                turn(2)
                pe.wait_ge(g.sem, g.done(it, f"vm{n}"))
                pe.wait_ge(df.sem, n_of(df, it, "o", n - 1))
                if n % CH == 0:
                    pe.wait_ge(df.sem, df.done(it, "add0") if n else df.done(it - 1, "add1"))
                weigh(0)
                turn(3)
                weigh(1)
                weigh(2)
                weigh(3).then_inc(ef.sem, 1)
                if n % CH == CH - 1:
                    pe.wait_ge(df.sem, df.done(it, f"o{n}"))
                    for j in range(CH):
                        last = pe.matmul(bank(6)[:, j * C:(j + 1) * C], oT[:, p, j], mem.mat(f"oT{layer}"),
                                         start=True, stop=True)
                    last.then_inc(ef.sem, 1)

            turns(pe, first, second)


def experts_block(nc, mem, ctx, w_fc, w_proj):
    def sem(n):
        return ctx.enter_context(nc.semaphore(f"moe_{n}"))

    mem.at = KEPT_WORDS
    fc = mem.take(E, 4, 128)
    proj = mem.take(E, 4, C)
    hid = mem.take(2, 4, W)
    part = mem.take(2, W)
    lgT = mem.take(2, W)
    lg = mem.take(B, E)
    one1 = mem.take(B, E)
    one2 = mem.take(B, E)
    cand = mem.take(B, E)
    comb = mem.take(B, E)
    best = mem.take(6, B)
    cs = mem.take(2, CH, E)
    cT = mem.take(2, W)
    norm = Norm(nc, mem, ctx, "moen", mem.x)
    weights = sem("weights")
    re_ = Steps(sem("route_pe"), "logit0 turned0 logit1 turned1", 1)
    ra = Steps(sem("route_act"), "lgT0 lgT1", 1)
    rd = Steps(sem("route_dve"), "lg0 lg1", 1)
    top = sem("top")
    gap = sem("gap")
    XP = [f"{s}{e}" for e in range(E) for s in ("part", "add")]
    e_ = Steps(sem("pe"), "cT bias " + " ".join(" ".join(f"f{e}{k}" for k in range(4)) + (f" y{e - 1}" if e else "")
                                               for e in range(E)) + f" y{E - 1}", 1)
    a_ = Steps(sem("act"), "cT " + " ".join(f"h{e}{k}" for e in range(E) for k in range(4)), 1)
    d_ = Steps(sem("dve"), "cs bias " + " ".join(XP), 1)
    bank = mem.bank

    def wide(v):
        return v.unsqueeze(2).broadcast_to([128, B, E])

    with nc.Block() as block:
        @block.sync
        def _(sp):
            sp.dma_start(fc.rearrange("p e k h -> p (e k h)"), w_fc).then_inc(weights, 16)
            sp.dma_start(proj.rearrange("p e k c -> p (e k c)"), w_proj).then_inc(weights, 16)
            sp.wait_ge(weights, 32)

        @block.gpsimd
        def _(pool):
            with pool.Fori(0, NIT) as it:
                norm.pool_turn(pool, it)

        @block.vector
        def _(dve):
            for s in (norm.stats, rd, d_):
                dve.sem_inc(s.sem, s.credit())
            norm.vector_pass(dve)
            with dve.Fori(0, NIT) as it:
                for p in range(2):
                    dve.wait_ge(re_.sem, re_.done(it, f"turned{p}"))
                    dve.tensor_copy(chunk(lg, it, p), bank(2 + p)[:, 0:CH * E].rearrange("p (b e) -> p b e", b=CH)).then_inc(rd.sem, 1)
            rank = mem.mat("rank", 0, E).unsqueeze(1).broadcast_to([128, B, E])
            dve.wait_ge(rd.sem, rd.done(NIT - 1, "lg1"))
            n = 0
            for k, one in enumerate((one1, one2)):
                src = lg if k == 0 else cand
                dve.tensor_reduce(best[:, 3 * k, :], src[:, :, :], AX.X, ALU.max).then_inc(top, 1)
                n += 1
                dve.wait_ge(top, n)
                dve.tensor_tensor(one, src, wide(best[:, 3 * k, :]), ALU.is_equal).then_inc(top, 1)
                n += 1
                dve.wait_ge(top, n)
                dve.tensor_tensor(one, one, rank, ALU.mult).then_inc(top, 1)
                n += 1
                dve.wait_ge(top, n)
                dve.tensor_reduce(best[:, 3 * k + 1, :], one[:, :, :], AX.X, ALU.max).then_inc(top, 1)
                n += 1
                dve.wait_ge(top, n)
                dve.tensor_tensor(one, rank, wide(best[:, 3 * k + 1, :]), ALU.is_equal).then_inc(top, 1)
                n += 1
                dve.wait_ge(top, n)
                if k == 0:
                    dve.scalar_tensor_tensor(cand, one, -1e30, lg, ALU.mult, ALU.add).then_inc(top, 1)
                    n += 1
                    dve.wait_ge(top, n)
            dve.tensor_tensor(best[:, 2, :], best[:, 3, :], best[:, 0, :], ALU.subtract).then_inc(top, 1)
            n += 1
            dve.wait_ge(gap, 1)
            dve.tensor_scalar(best[:, 4, :], best[:, 5, :], 1.0, None, ALU.add).then_inc(top, 1)
            n += 1
            dve.wait_ge(top, n)
            dve.reciprocal(best[:, 1, :], best[:, 4, :]).then_inc(top, 1)
            n += 1
            dve.wait_ge(top, n)
            dve.tensor_tensor(best[:, 2, :], best[:, 5, :], best[:, 1, :], ALU.mult).then_inc(top, 1)
            dve.tensor_tensor(one1, one1, wide(best[:, 1, :]), ALU.mult).then_inc(top, 1)
            n += 2
            dve.wait_ge(top, n)
            dve.tensor_tensor(one2, one2, wide(best[:, 2, :]), ALU.mult).then_inc(top, 1)
            n += 1
            dve.wait_ge(top, n)
            dve.tensor_tensor(comb, one1, one2, ALU.add).then_inc(top, 1)
            n += 1
            dve.wait_ge(top, n)
            with dve.Fori(0, NCH) as it:
                dve.wait_ge(e_.sem, e_.done(it - 1, "cT"))
                dve.tensor_copy(cs[:, 0], comb[:, bass.ds(it * CH, CH), :]).then_inc(d_.sem, 1)
                x = mem.x[:, bass.ds(it * CH, CH), :]
                dve.wait_ge(e_.sem, e_.done(it, "bias"))
                dve.tensor_tensor(x, x, bank(7).rearrange("p (b c) -> p b c", b=CH), ALU.add).then_inc(d_.sem, 1)
                for e in range(E):
                    dve.wait_ge(e_.sem, e_.done(it, f"y{e}"))
                    dve.wait_ge(d_.sem, d_.done(it, f"add{e - 2}") if e > 1 else d_.done(it - 1, f"add{e + E - 2}"))
                    dve.tensor_tensor(part[:, e % 2].rearrange("p (b c) -> p b c", b=CH),
                                      bank(4 + e % 2).rearrange("p (b c) -> p b c", b=CH),
                                      cs[:, 0, :, e:e + 1].broadcast_to([128, CH, C]), ALU.mult).then_inc(d_.sem, 1)
                    dve.wait_ge(d_.sem, d_.done(it, f"part{e}"))
                    dve.tensor_tensor(x, x, part[:, e % 2].rearrange("p (b c) -> p b c", b=CH), ALU.add).then_inc(d_.sem, 1)

        @block.scalar
        def _(act):
            for s in (norm.act, ra, a_):
                act.sem_inc(s.sem, s.credit())
            with act.Fori(0, NIT) as it:
                norm.scalar_turn(act, it)
            with act.Fori(0, NIT) as it:
                for p in range(2):
                    act.wait_ge(re_.sem, re_.done(it, f"logit{p}"))
                    act.wait_ge(re_.sem, re_.done(it - 1, f"turned{p}"))
                    act.activation(lgT[0:E, p], bank(p)[0:E, :], ACT.Copy).then_inc(ra.sem, 1)
            act.wait_ge(top, 12)
            act.activation(best[:, 5, :], best[:, 2, :], ACT.Exp).then_inc(gap, 1)
            with act.Fori(0, NCH) as it:
                act.wait_ge(e_.sem, e_.done(it, "cT"))
                act.wait_ge(e_.sem, e_.done(it - 1, "bias"))
                act.activation(cT[0:E, 0], bank(6)[0:E, :], ACT.Copy).then_inc(a_.sem, 1)
                for e in range(E):
                    for k in range(4):
                        act.wait_ge(e_.sem, e_.done(it, f"f{e}{k}"))
                        if k == 0:
                            act.wait_ge(e_.sem, e_.done(it, f"y{e - 2}") if e > 1 else e_.done(it - 1, f"y{e + E - 2}"))
                        act.activation(hid[:, e % 2, k], bank(k), ACT.Gelu_apprx_tanh, bias=mem.col("b_fc", e * 4 + k)).then_inc(a_.sem, 1)

        @block.tensor
        def _(pe):
            for s in (norm.pe, re_, e_):
                pe.sem_inc(s.sem, s.credit())
            with pe.Fori(0, NIT) as it:
                norm.tensor_turn(pe, it)
            with pe.Fori(0, NIT) as it:
                for p in range(2):
                    pe.wait_ge(norm.act.sem, norm.act.done(it, f"ready{p}"))
                    pe.wait_ge(ra.sem, ra.done(it - 1, f"lgT{p}"))
                    pe.matmul(bank(p)[0:E, :].rearrange("p (b t) -> p b t", b=CH), mem.mat("router", 0, E),
                              chunk(mem.hT, it, p)[:, :, 1:T + 1], start=True, stop=True).then_inc(re_.sem, 1)
                    pe.wait_ge(ra.sem, ra.done(it, f"lgT{p}"))
                    pe.wait_ge(rd.sem, rd.done(it - 1, f"lg{p}"))
                    for j in range(CH):
                        last = pe.matmul(bank(2 + p)[:, j * E:(j + 1) * E], lgT[0:E, p, j * T:(j + 1) * T],
                                         mem.mat("ident")[0:E, 0:E], start=True, stop=True)
                    last.then_inc(re_.sem, 1)
            pe.wait_ge(weights, 32)
            with pe.Fori(0, NCH) as it:
                def outputs(e):
                    pe.wait_ge(a_.sem, a_.done(it, f"h{e}3"))
                    pe.wait_ge(d_.sem, d_.done(it, f"part{e - 2}") if e > 1 else d_.done(it - 1, f"part{e + E - 2}"))
                    for j in range(CH):
                        for k in range(4):
                            last = pe.matmul(bank(4 + e % 2)[:, j * C:(j + 1) * C], hid[:, e % 2, k, j * T:(j + 1) * T], proj[:, e, k],
                                             start=(k == 0), stop=(k == 3))
                    last.then_inc(e_.sem, 1)

                pe.wait_ge(d_.sem, d_.done(it, "cs"))
                pe.wait_ge(a_.sem, a_.done(it - 1, "cT"))
                for j in range(CH):
                    last = pe.transpose(bank(6)[0:E, j * T:(j + 1) * T], cs[:, 0, j, :], mem.mat("ident"))
                last.then_inc(e_.sem, 1)
                pe.wait_ge(a_.sem, a_.done(it, "cT"))
                pe.wait_ge(d_.sem, d_.done(it - 1, "bias"))
                for j in range(CH):
                    last = pe.matmul(bank(7)[:, j * C:(j + 1) * C], cT[0:E, 0, j * T:(j + 1) * T], mem.b_proj[:, :], start=True, stop=True)
                last.then_inc(e_.sem, 1)
                for e in range(E):
                    for k in range(4):
                        pe.wait_ge(a_.sem, a_.done(it, f"h{e - 1}{k}") if e else a_.done(it - 1, f"h{E - 1}{k}"))
                        pe.matmul(bank(k).rearrange("p (b t) -> p b t", b=CH), fc[:, e, k],
                                  mem.hT[:, bass.ds(it * CH, CH), 1:T + 1], start=True, stop=True).then_inc(e_.sem, 1)
                    if e:
                        outputs(e - 1)
                outputs(E - 1)


def state_space_block(nc, mem, ctx):
    def sem(n):
        return ctx.enter_context(nc.semaphore(f"ssm_{n}"))

    mem.at = KEPT_WORDS
    xp = mem.take(B, T + 2)
    gt = mem.take(B, T)
    mix = mem.take(B, T)
    dz = mem.take(B, T)
    bm = mem.take(B, T)
    ct = mem.take(B, T)
    neg_a = mem.take(2)
    tb = mem.take(2, CH, T)
    top = mem.at
    mem.at = KEPT_WORDS
    soft = mem.take(2, 2, CH, T)
    mem.at = top
    decay, u = tb[:, 0], tb[:, 1]
    state = mem.take(CH, T)
    yT = mem.hn[:, :, :, :].rearrange("p a b c -> p a (b c)")
    mem.at = KEPT_WORDS
    act1 = mem.take(2, 2, W)
    n4 = Norm(nc, mem, ctx, "ssmn", mem.x, double=True, affine=("m_ln1_g", "m_ln1_b"))
    n5 = Norm(nc, mem, ctx, "ffn", mem.xl, affine=("m_ln2_g", "m_ln2_b"))
    init = sem("init")
    ie = Steps(sem("in_pe"), "x0 g0 x1 g1", 1)
    ia = Steps(sem("in_act"), "x0 g0 x1 g1", 1)
    cd = Steps(sem("conv_dve"), "a0 b0 c0 a1 b1 c1")
    ce = Steps(sem("conv_pe"), "dt0 b0 c0 dt1 b1 c1", 1)
    ca = Steps(sem("conv_act"), "dt0 b0 c0 dt1 b1 c1", 1)
    cg = Steps(sem("conv_pool"), "bm0 bm1", 1)
    sa = Steps(sem("scan_act"), "neg0 exp0 ln0 decay0 neg1 exp1 ln1 decay1", 1)
    sd = Steps(sem("scan_dve"), " ".join(f"dt{p} start{p} state{p} cs{p} skip{p} y{p} add{p}" for p in range(2)), 1)
    sg = Steps(sem("scan_pool"), "u0 u1", 1)
    se = Steps(sem("scan_pe"), "out0 out1", 1)
    fe = Steps(sem("ff_pe"), "h00 h01 out0 h10 h11 out1", 1)
    fa = Steps(sem("ff_act"), "g00 g01 g10 g11", 1)
    fd = Steps(sem("ff_dve"), "res0 add0 res1 add1", 1)
    bank = mem.bank

    def bt(v):
        return v.rearrange("p (b t) -> p b t", b=CH)

    def flat(v):
        return v.rearrange("p b t -> p (b t)")

    with nc.Block() as block:
        @block.gpsimd
        def _(pool):
            pool.sem_inc(cg.sem, cg.credit())
            pool.sem_inc(sg.sem, sg.credit())
            pool.memset(xp[:, :, 0:1], 0.0).then_inc(init, 1)
            pool.memset(xp[:, :, T + 1:T + 2], 0.0).then_inc(init, 1)
            with pool.Fori(0, NIT) as it:
                n4.pool_turn(pool, it)
            with pool.Fori(0, NIT) as it:
                for p in range(2):
                    pool.wait_ge(ca.sem, ca.done(it, f"b{p}"))
                    pool.tensor_tensor(chunk(bm, it, p), tb[:, p], chunk(mix, it, p), ALU.mult).then_inc(cg.sem, 1)
            with pool.Fori(0, NIT) as it:
                for p in range(2):
                    pool.wait_ge(sd.sem, sd.done(it, f"dt{p}"))
                    pool.wait_ge(sd.sem, sd.previous(it, p, "state"))
                    pool.tensor_tensor(u[:, :, :], soft[:, p, 0], chunk(bm, it, p), ALU.mult).then_inc(sg.sem, 1)
            with pool.Fori(0, NIT) as it:
                n5.pool_turn(pool, it)

        @block.vector
        def _(dve):
            for s in (n4.stats, n5.stats, sd, fd):
                dve.sem_inc(s.sem, s.credit())
            dve.wait_ge(init, 3)
            dve.tensor_scalar(neg_a[:, 1:2], neg_a[:, 0:1], -1.0, None, ALU.mult).then_inc(init, 1)
            n4.vector_pass(dve)
            with dve.Fori(0, NIT) as it:
                for p in range(2):
                    m = chunk(mix, it, p)
                    dve.wait_ge(ia.sem, ia.done(it, f"x{p}"))
                    dve.tensor_scalar(m, chunk(xp, it, p)[:, :, 1:T + 1], mem.col("dw1"), mem.col("dw_b"), ALU.mult, ALU.add).then_inc(cd.sem, 1)
                    dve.wait_ge(cd.sem, cd.done(it, f"a{p}"))
                    dve.scalar_tensor_tensor(m, chunk(xp, it, p)[:, :, 0:T], mem.col("dw0"), m, ALU.mult, ALU.add).then_inc(cd.sem, 1)
                    dve.wait_ge(cd.sem, cd.done(it, f"b{p}"))
                    dve.scalar_tensor_tensor(m, chunk(xp, it, p)[:, :, 2:T + 2], mem.col("dw2"), m, ALU.mult, ALU.add).then_inc(cd.sem, 1)
            with dve.Fori(0, NIT) as it:
                for p in range(2):
                    dve.wait_ge(sa.sem, sa.done(it, f"ln{p}"))
                    dve.scalar_tensor_tensor(soft[:, p, 0], chunk(dz, it, p), 0.0, soft[:, p, 1], ALU.max, ALU.add).then_inc(sd.sem, 1)
                    dve.wait_ge(sa.sem, sa.done(it, f"decay{p}"))
                    dve.memset(decay[:, :, 0:1], 0.0).then_inc(sd.sem, 1)
                    dve.wait_ge(sd.sem, sd.done(it, f"start{p}"))
                    dve.wait_ge(sg.sem, sg.done(it, f"u{p}"))
                    dve.tensor_tensor_scan(flat(state), flat(decay), flat(u), 0.0, ALU.mult, ALU.add).then_inc(sd.sem, 1)
                    dve.wait_ge(sd.sem, sd.done(it, f"state{p}"))
                    dve.tensor_tensor(state, state, chunk(ct, it, p), ALU.mult).then_inc(sd.sem, 1)
                    dve.wait_ge(sd.sem, sd.done(it, f"cs{p}"))
                    dve.scalar_tensor_tensor(state, chunk(mix, it, p), mem.col("d_skip"), state, ALU.mult, ALU.add).then_inc(sd.sem, 1)
                    dve.wait_ge(sd.sem, sd.done(it, f"skip{p}"))
                    dve.wait_ge(se.sem, se.done(it - 1, f"out{p}"))
                    dve.tensor_tensor(bt(yT[:, p]), state, chunk(gt, it, p), ALU.mult).then_inc(sd.sem, 1)
                    xl = chunk(mem.xl, it, p)
                    dve.wait_ge(se.sem, se.done(it, f"out{p}"))
                    dve.tensor_tensor(xl, xl, bt(bank(p)), ALU.add).then_inc(sd.sem, 1)
            dve.wait_ge(sd.sem, sd.done(NIT - 1, "add1"))
            n5.vector_pass(dve)
            with dve.Fori(0, NIT) as it:
                for p in range(2):
                    x = chunk(mem.x, it, p)
                    dve.tensor_tensor(x, x, chunk(mem.xl, it, p), ALU.add).then_inc(fd.sem, 1)
                    dve.wait_ge(fd.sem, fd.done(it, f"res{p}"))
                    dve.wait_ge(fe.sem, fe.done(it, f"out{p}"))
                    dve.tensor_tensor(x, x, bt(bank(4 + p)), ALU.add).then_inc(fd.sem, 1)

        @block.scalar
        def _(act):
            for s in (n4.act, n5.act, ia, ca, sa, fa):
                act.sem_inc(s.sem, s.credit())
            act.activation(neg_a[:, 0:1], mem.col("a_log"), ACT.Exp).then_inc(init, 1)
            with act.Fori(0, NIT) as it:
                n4.scalar_turn(act, it)
            act.wait_ge(init, 2)
            with act.Fori(0, NIT) as it:
                for p in range(2):
                    act.wait_ge(ie.sem, ie.done(it, f"x{p}"))
                    act.activation(chunk(xp, it, p)[:, :, 1:T + 1], bt(bank(p)), ACT.Identity, bias=mem.col("in_b0")).then_inc(ia.sem, 1)
                    act.wait_ge(ie.sem, ie.done(it, f"g{p}"))
                    act.activation(chunk(gt, it, p), bt(bank(2 + p)), ACT.Sigmoid, bias=mem.col("in_b1")).then_inc(ia.sem, 1)
            with act.Fori(0, NIT) as it:
                for p in range(2):
                    act.wait_ge(ce.sem, ce.done(it, f"dt{p}"))
                    act.activation(chunk(dz, it, p), bt(bank(4)), ACT.Identity, bias=mem.col("dt_b")).then_inc(ca.sem, 1)
                    act.wait_ge(ce.sem, ce.done(it, f"b{p}"))
                    act.wait_ge(cg.sem, cg.done(it - 1, f"bm{p}"))
                    act.activation(tb[:, p], bt(bank(5)), ACT.Tanh, bias=mem.col("b_b")).then_inc(ca.sem, 1)
                    act.wait_ge(ce.sem, ce.done(it, f"c{p}"))
                    act.activation(chunk(ct, it, p), bt(bank(6 + p)), ACT.Tanh, bias=mem.col("c_b")).then_inc(ca.sem, 1)
            act.wait_ge(ca.sem, ca.done(NIT - 1, "c1"))
            act.wait_ge(cd.sem, cd.done(NIT - 1, "c1"))
            act.wait_ge(cg.sem, cg.done(NIT - 1, "bm1"))
            act.wait_ge(init, 4)
            with act.Fori(0, NIT) as it:
                for p in range(2):
                    act.wait_ge(sd.sem, sd.done(it - 1, f"state{p}"))
                    act.activation(soft[:, p, 0], chunk(dz, it, p), ACT.Abs).then_inc(sa.sem, 1)
                    act.wait_ge(sa.sem, sa.done(it, f"neg{p}"))
                    act.activation(soft[:, p, 1], soft[:, p, 0], ACT.Exp, scale=-1.0).then_inc(sa.sem, 1)
                    act.wait_ge(sa.sem, sa.done(it, f"exp{p}"))
                    act.activation(soft[:, p, 1], soft[:, p, 1], ACT.Ln, bias=1.0).then_inc(sa.sem, 1)
                    act.wait_ge(sd.sem, sd.done(it, f"dt{p}"))
                    act.wait_ge(sd.sem, sd.previous(it, p, "state"))
                    act.activation(decay[:, :, :], soft[:, p, 0], ACT.Exp, scale=neg_a[:, 1:2]).then_inc(sa.sem, 1)
            with act.Fori(0, NIT) as it:
                n5.scalar_turn(act, it)
            with act.Fori(0, NIT) as it:
                for p in range(2):
                    for k in range(2):
                        act.wait_ge(fe.sem, fe.done(it, f"h{p}{k}"))
                        if k == 0:
                            act.wait_ge(fe.sem, fe.done(it - 1, f"out{p}"))
                        act.activation(act1[:, p, k], bank(2 * p + k), ACT.Gelu, bias=mem.col(f"f1_b{k}")).then_inc(fa.sem, 1)

        @block.tensor
        def _(pe):
            for s in (n4.pe, n5.pe, ie, ce, se, fe):
                pe.sem_inc(s.sem, s.credit())
            with pe.Fori(0, NIT) as it:
                n4.tensor_turn(pe, it)
            with pe.Fori(0, NIT) as it:
                for p in range(2):
                    h = chunk(mem.hT, it, p)[:, :, 1:T + 1]
                    pe.wait_ge(n4.act.sem, n4.act.done(it, f"ready{p}"))
                    for k, name in enumerate("xg"):
                        pe.wait_ge(ia.sem, ia.done(it - 1, f"{name}{p}"))
                        pe.matmul(bt(bank(2 * k + p)), mem.mat("in_W", k), h, start=True, stop=True).then_inc(ie.sem, 1)
            with pe.Fori(0, NIT) as it:
                for p in range(2):
                    m = chunk(mix, it, p)
                    pe.wait_ge(cd.sem, cd.done(it, f"c{p}"))
                    for name, i in (("dt", 4), ("b", 5), ("c", 6 + p)):
                        pe.wait_ge(ca.sem, ca.done(it - 1, f"c{p}") if name == "c" else ca.previous(it, p, name))
                        pe.matmul(bt(bank(i)), mem.mat(f"{name}_W"), m, start=True, stop=True).then_inc(ce.sem, 1)
            with pe.Fori(0, NIT) as it:
                for p in range(2):
                    pe.wait_ge(sd.sem, sd.done(it, f"y{p}"))
                    for j in range(CH):
                        out = bank(p)[:, j * C:(j + 1) * C]
                        pe.matmul(out, yT[:, p, j * T:(j + 1) * T], mem.mat("out_W"), start=True, stop=False)
                        last = pe.matmul(out, mem.ones[0:1, :], mem.row("m_out_b"), start=False, stop=True)
                    last.then_inc(se.sem, 1)
            with pe.Fori(0, NIT) as it:
                n5.tensor_turn(pe, it)
            with pe.Fori(0, NIT) as it:
                for p in range(2):
                    h = chunk(mem.hT, it, p)[:, :, 1:T + 1]
                    pe.wait_ge(n5.act.sem, n5.act.done(it, f"ready{p}"))
                    for k in range(2):
                        pe.wait_ge(fa.sem, fa.done(it - 1, f"g{p}{k}"))
                        pe.matmul(bt(bank(2 * p + k)), mem.mat("f1_W", k), h, start=True, stop=True).then_inc(fe.sem, 1)
                    pe.wait_ge(fa.sem, fa.done(it, f"g{p}1"))
                    pe.wait_ge(fd.sem, fd.done(it - 1, f"add{p}"))
                    for j in range(CH):
                        out = bank(4 + p)[:, j * C:(j + 1) * C]
                        for k in range(2):
                            pe.matmul(out, act1[:, p, k, j * T:(j + 1) * T], mem.mat("f2_W", k), start=(k == 0), stop=False)
                        last = pe.matmul(out, mem.ones[0:1, :], mem.row("f2_b"), start=False, stop=True)
                    last.then_inc(fe.sem, 1)


MAGIC = 12582912.0
Q16 = 32767.0
NG = 12
GW = 3 * B * T // NG


def quantised_ffn_block(nc, mem, ctx, out):
    def sem(n):
        return ctx.enter_context(nc.semaphore(f"q_{n}"))

    mem.restart()
    up = mem.take(3, B * T)
    gate = mem.take(3, B * T)
    wT = mem.take(3, 3 * C)
    qx = mem.take(2, CH, C)
    qxT = mem.take(2, W)
    top = mem.at
    mem.at = 0
    wq = mem.take(36, 32)
    ws = mem.take(3, 36)
    mem.at = top
    amax = mem.take(16)
    amax_u = mem.take(16)
    glob = mem.take(16)
    row = mem.take(128)
    t1 = mem.take(2, GW)
    t2 = mem.take(2, GW)
    oq = mem.hn
    n = Norm(nc, mem, ctx, "qn", mem.x, whole=True)
    wd = sem("weights_dve")
    we = Steps(sem("weights_pe"), "0 1 2")
    wa = Steps(sem("weights_act"), "0 1 2")
    gd, ge = sem("max_dve"), sem("max_pe")
    pd = Steps(sem("proj_dve"), " ".join(f"a{p} b{p} q{p} " + " ".join(f"mu{p}{k} mg{p}{k}" for k in range(3)) for p in range(2)), 1)
    pe_ = Steps(sem("proj_pe"), " ".join(f"turned{p} " + " ".join(f"u{p}{k} g{p}{k}" for k in range(3)) for p in range(2)), 1)
    pa = Steps(sem("proj_act"), " ".join(f"xT{p} " + " ".join(f"u{p}{k} g{p}{k}" for k in range(3)) for p in range(2)), 1)
    sd = Steps(sem("sig_dve"), " ".join(f"a{p} b{p} q{p} s{p} r{p} g{p} m{p}" for p in range(2)), 1)
    sa = Steps(sem("sig_act"), "sig0 sig1", 1)
    od = Steps(sem("prod_dve"), " ".join(f"ga{p} gb{p} gq{p} ua{p} ub{p} uq{p} o{p} m{p}" for p in range(2)), 1)
    dd = Steps(sem("down_dve"), "a0 b0 q0 a1 b1 q1 add0 add1", 1)
    de = Steps(sem("down_pe"), "out0 out1", 1)
    stored = sem("stored")
    bank = mem.bank
    used = [0]

    def bt(v):
        return v.rearrange("p (b t) -> p b t", b=CH)

    X, U, G, G2, O = range(5)

    def scale(i):
        return glob[:, 2 * i:2 * i + 1]

    def inverse(i):
        return glob[:, 2 * i + 1:2 * i + 2]

    def find_scale_vector(dve, i, src, unit=1.0):
        def step(ins):
            used[0] += 1
            ins.then_inc(gd, 1)
            dve.wait_ge(gd, used[0])

        step(dve.tensor_reduce(row[:, 0:1], src, AX.X, ALU.max))
        dve.wait_ge(ge, 2 * i + 1)
        step(dve.tensor_reduce(row[0:1, 1:2], bank(7)[0:1, 0:128], AX.X, ALU.max))
        dve.wait_ge(ge, 2 * i + 2)
        step(dve.tensor_scalar(row[:, 2:3], bank(7)[:, 128:129], unit / Q16, 1e-12, ALU.mult, ALU.max))
        if unit == 1.0:
            step(dve.tensor_copy(scale(i), row[:, 2:3]))
        else:
            step(dve.tensor_scalar(scale(i), row[:, 2:3], 1.0 / unit, None, ALU.mult))
        step(dve.reciprocal(inverse(i), scale(i)))

    def find_scale_tensor(pe, i):
        pe.wait_ge(gd, 5 * i + 1)
        pe.transpose(bank(7)[0:1, 0:128], row[:, 0:1], mem.mat("ident")).then_inc(ge, 1)
        pe.wait_ge(gd, 5 * i + 2)
        pe.matmul(bank(7)[:, 128:129], mem.ones[0:1, :], row[0:1, 1:2], start=True, stop=True).then_inc(ge, 1)

    def ready(eng, i):
        eng.wait_ge(gd, 5 * i + 5)

    with nc.Block() as block:
        @block.gpsimd
        def _(pool):
            with pool.Fori(0, NIT) as it:
                n.pool_turn(pool, it)

        @block.vector
        def _(dve):
            for s in (n.stats, pd, sd, od, dd):
                dve.sem_inc(s.sem, s.credit())
            k = 0

            def step(ins):
                nonlocal k
                k += 1
                ins.then_inc(wd, 1)
                dve.wait_ge(wd, k)

            w = mem.mat("gate", 0, 9 * C).rearrange("p (n k) -> p n k", k=32)
            step(dve.tensor_reduce(ws[:, 0, :], w, AX.X, ALU.max, apply_absolute_value=True))
            step(dve.tensor_scalar(ws[:, 1, :], ws[:, 0, :], 1.0 / 7.0, 1e-12, ALU.mult, ALU.max))
            step(dve.reciprocal(ws[:, 2, :], ws[:, 1, :]))
            step(dve.tensor_tensor(wq[:, :, :], w, ws[:, 2, :].unsqueeze(2).broadcast_to([128, 36, 32]), ALU.mult))
            step(dve.tensor_scalar(wq[:, :, :], wq[:, :, :], MAGIC, MAGIC, ALU.add, ALU.subtract))
            step(dve.tensor_scalar(wq[:, :, :], wq[:, :, :], 7.0, -8.0, ALU.min, ALU.max))
            step(dve.tensor_tensor(wq[:, :, :], wq[:, :, :], ws[:, 1, :].unsqueeze(2).broadcast_to([128, 36, 32]), ALU.mult))
            n.vector_pass(dve, amax)
            dve.wait_ge(n.dve.sem, n.dve.done(NIT - 1, "amax"))
            find_scale_vector(dve, X, amax[:, 0:NIT])

            def round_to(eng_sem, steps, it, names, dst, src, i, tmp):
                dve.tensor_scalar(tmp, src, inverse(i), Q16, ALU.mult, ALU.min).then_inc(steps.sem, 1)
                dve.wait_ge(steps.sem, steps.done(it, names[0]))
                dve.tensor_scalar(tmp, tmp, -Q16 - 1.0, MAGIC, ALU.max, ALU.add).then_inc(steps.sem, 1)
                dve.wait_ge(steps.sem, steps.done(it, names[1]))
                dve.tensor_scalar(dst, tmp, MAGIC, scale(i), ALU.subtract, ALU.mult).then_inc(steps.sem, 1)

            with dve.Fori(0, NIT) as it:
                for p in range(2):
                    tmp = t1[:, p, 0:W].rearrange("p (b c) -> p b c", b=CH)
                    dve.wait_ge(pd.sem, pd.done(it - 1, f"q{p}"))
                    dve.wait_ge(pe_.sem, pe_.done(it - 1, f"turned{p}"))
                    round_to(None, pd, it, (f"a{p}", f"b{p}"), qx[:, p], chunk(mem.xl, it, p), X, tmp)
                    for j in range(3):
                        for name, kk, arr in (("u", 0, amax_u), ("g", 1, amax)):
                            dve.wait_ge(pe_.sem, pe_.done(it, f"{name}{p}{j}"))
                            if name == "u":
                                dst = t2[:, 0, 0:24]
                            else:
                                dst = t2[:, 1, 0:24]
                            dst = dst.rearrange("p (c k) -> p c k", k=3)[:, bass.ds(it * 2 + p, 1), j]
                            dve.tensor_reduce(dst, bank(2 * j + kk), AX.X, ALU.max, apply_absolute_value=True).then_inc(pd.sem, 1)
            dve.wait_ge(pd.sem, pd.done(NIT - 1, "mg12"))
            find_scale_vector(dve, U, t2[:, 0, 0:24])
            find_scale_vector(dve, G, t2[:, 1, 0:24])
            dve.wait_ge(pa.sem, pa.done(NIT - 1, "g12"))
            gflat, uflat = gate.rearrange("p k t -> p (k t)"), up.rearrange("p k t -> p (k t)")
            with dve.Fori(0, NG // 2) as it:
                for p in range(2):
                    g = gflat[:, bass.ds((it * 2 + p) * GW, GW)]
                    dve.wait_ge(sd.sem, sd.done(it - 1, f"g{p}"))
                    round_to(None, sd, it, (f"a{p}", f"b{p}"), t1[:, p, :], g, G, t1[:, p, :])
                    dve.wait_ge(sa.sem, sa.done(it, f"sig{p}"))
                    dve.tensor_scalar(t2[:, p, :], t2[:, p, :], 65536.0, 65535.0, ALU.mult, ALU.min).then_inc(sd.sem, 1)
                    dve.wait_ge(sd.sem, sd.done(it, f"s{p}"))
                    dve.tensor_scalar(t2[:, p, :], t2[:, p, :], 0.0, MAGIC, ALU.max, ALU.add).then_inc(sd.sem, 1)
                    dve.wait_ge(sd.sem, sd.done(it, f"r{p}"))
                    dve.scalar_tensor_tensor(g, t2[:, p, :], MAGIC, t1[:, p, :], ALU.subtract, ALU.mult).then_inc(sd.sem, 1)
                    dve.wait_ge(sd.sem, sd.done(it, f"g{p}"))
                    dve.tensor_reduce(amax[:, bass.ds(it * 2 + p, 1)], gflat[:, bass.ds((it * 2 + p) * GW, GW)], AX.X, ALU.max,
                                      apply_absolute_value=True).then_inc(sd.sem, 1)
            dve.wait_ge(sd.sem, sd.done(NG // 2 - 1, "m1"))
            find_scale_vector(dve, G2, amax[:, 0:NG], unit=2.0 ** -16)
            with dve.Fori(0, NG // 2) as it:
                for p in range(2):
                    g, u = gflat[:, bass.ds((it * 2 + p) * GW, GW)], uflat[:, bass.ds((it * 2 + p) * GW, GW)]
                    dve.wait_ge(od.sem, od.done(it - 1, f"o{p}"))
                    round_to(None, od, it, (f"ga{p}", f"gb{p}"), t1[:, p, :], g, G2, t1[:, p, :])
                    round_to(None, od, it, (f"ua{p}", f"ub{p}"), t2[:, p, :], u, U, t2[:, p, :])
                    dve.wait_ge(od.sem, od.done(it, f"uq{p}"))
                    dve.tensor_tensor(g, t1[:, p, :], t2[:, p, :], ALU.mult).then_inc(od.sem, 1)
                    dve.wait_ge(od.sem, od.done(it, f"o{p}"))
                    dve.tensor_reduce(amax_u[:, bass.ds(it * 2 + p, 1)], gflat[:, bass.ds((it * 2 + p) * GW, GW)], AX.X, ALU.max,
                                      apply_absolute_value=True).then_inc(od.sem, 1)
            dve.wait_ge(od.sem, od.done(NG // 2 - 1, "m1"))
            find_scale_vector(dve, O, amax_u[:, 0:NG], unit=2.0 ** -16)
            dve.tensor_scalar(row[:, 3:4], scale(O), 2.0 ** -16, None, ALU.mult).then_inc(wd, 1)
            dve.wait_ge(wd, k + 1)
            prod = uflat[:, 0:2 * 3 * W].rearrange("p (q k t) -> p q k t", q=2, k=3)
            tmp = uflat[:, 2 * 3 * W:4 * 3 * W].rearrange("p (q k t) -> p q k t", q=2, k=3)
            with dve.Fori(0, NIT) as it:
                for p in range(2):
                    dve.wait_ge(dd.sem, dd.done(it - 1, f"q{p}"))
                    dve.wait_ge(de.sem, de.done(it - 1, f"out{p}"))
                    src = gate[:, :, bass.ds((it * 2 + p) * W, W)]
                    dve.tensor_scalar(tmp[:, p], src, inverse(O), Q16, ALU.mult, ALU.min).then_inc(dd.sem, 1)
                    dve.wait_ge(dd.sem, dd.done(it, f"a{p}"))
                    dve.tensor_scalar(tmp[:, p], tmp[:, p], -Q16 - 1.0, MAGIC, ALU.max, ALU.add).then_inc(dd.sem, 1)
                    dve.wait_ge(dd.sem, dd.done(it, f"b{p}"))
                    dve.tensor_scalar(prod[:, p], tmp[:, p], MAGIC, row[:, 3:4], ALU.subtract, ALU.mult).then_inc(dd.sem, 1)
                for p in range(2):
                    x = chunk(mem.x, it, p)
                    dve.wait_ge(de.sem, de.done(it, f"out{p}"))
                    dve.tensor_tensor(x, x, bt(bank(p)), ALU.add).then_inc(dd.sem, 1)

        @block.scalar
        def _(act):
            for s in (pa, sa):
                act.sem_inc(s.sem, s.credit())
            for i in range(3):
                act.wait_ge(we.sem, i + 1)
                act.activation(wT[:, i, :], bank(i)[:, 0:3 * C], ACT.Copy).then_inc(wa.sem, 1)
            act.wait_ge(wd, 7)
            with act.Fori(0, NIT) as it:
                for p in range(2):
                    act.wait_ge(pe_.sem, pe_.done(it, f"turned{p}"))
                    act.wait_ge(pe_.sem, pe_.done(it - 1, f"g{p}2"))
                    act.activation(qxT[:, p], bank(6), ACT.Copy).then_inc(pa.sem, 1)
                    for j in range(3):
                        for name, kk, dst in (("u", 0, up), ("g", 1, gate)):
                            act.wait_ge(pd.sem, pd.done(it, f"m{name}{p}{j}"))
                            act.activation(dst[:, j, bass.ds((it * 2 + p) * W, W)], bank(2 * j + kk), ACT.Copy).then_inc(pa.sem, 1)
            with act.Fori(0, NG // 2) as it:
                for p in range(2):
                    act.wait_ge(sd.sem, sd.done(it, f"q{p}"))
                    act.wait_ge(sd.sem, sd.done(it - 1, f"g{p}"))
                    act.activation(t2[:, p, :], t1[:, p, :], ACT.Sigmoid).then_inc(sa.sem, 1)

        @block.tensor
        def _(pe):
            for s in (pe_, de):
                pe.sem_inc(s.sem, s.credit())
            pe.wait_ge(wd, 7)
            wflat = wq.rearrange("p n k -> p (n k)")
            for i in range(3):
                for j in range(3):
                    last = pe.transpose(bank(i)[:, j * C:(j + 1) * C], wflat[:, (3 * i + j) * C:(3 * i + j + 1) * C], mem.mat("ident"))
                last.then_inc(we.sem, 1)
            find_scale_tensor(pe, X)
            pe.wait_ge(wa.sem, 3)
            with pe.Fori(0, NIT) as it:
                for p in range(2):
                    pe.wait_ge(pd.sem, pd.done(it, f"q{p}"))
                    pe.wait_ge(pa.sem, pa.previous(it, p, "xT"))
                    for j in range(CH):
                        last = pe.transpose(bank(6)[:, j * T:(j + 1) * T], qx[:, p, j, :], mem.mat("ident"))
                    last.then_inc(pe_.sem, 1)
                    pe.wait_ge(pa.sem, pa.done(it, f"xT{p}"))
                    for j in range(3):
                        for name, kk, w in (("u", 0, 1), ("g", 1, 0)):
                            pe.wait_ge(pa.sem, pa.done(it, f"{name}0{j}") if p else pa.done(it - 1, f"{name}1{j}"))
                            pe.matmul(bank(2 * j + kk), wT[:, w, j * C:(j + 1) * C], qxT[:, p], start=True, stop=True).then_inc(pe_.sem, 1)
            for i in (U, G, G2, O):
                find_scale_tensor(pe, i)
            prod = up.rearrange("p k t -> p (k t)")[:, 0:2 * 3 * W].rearrange("p (q k t) -> p q k t", q=2, k=3)
            with pe.Fori(0, NIT) as it:
                for p in range(2):
                    pe.wait_ge(dd.sem, dd.done(it, f"q{p}"))
                    pe.wait_ge(dd.sem, dd.done(it - 1, f"add{p}"))
                    for j in range(CH):
                        for k in range(3):
                            last = pe.matmul(bank(p)[:, j * C:(j + 1) * C], prod[:, p, k, j * T:(j + 1) * T],
                                             wT[:, 2, k * C:(k + 1) * C], start=(k == 0), stop=(k == 2))
                    last.then_inc(de.sem, 1)

        @block.sync
        def _(sp):
            dst = out.rearrange("b t c -> t b c")
            with sp.Fori(0, NIT) as it:
                for p in range(2):
                    sp.wait_ge(dd.sem, dd.done(it, f"add{p}"))
                    at = bass.ds((it * 2 + p) * CH, CH)
                    sp.dma_start(dst[:, at, :], mem.x[:, at, :]).then_inc(stored, 16)
            sp.wait_ge(stored, 16 * NCH)


def build(nc, x, ctx_tokens, pack, rows, b_proj, w_fc, w_proj, v_mask, out):
    with ExitStack() as ctx:
        mem = Memory(nc, ctx)
        load_block(nc, mem, ctx, x, pack, rows, b_proj)
        time_mix_block(nc, mem, ctx)
        attention_block(nc, mem, ctx, 0, v_mask, ctx_tokens)
        experts_block(nc, mem, ctx, w_fc, w_proj)
        state_space_block(nc, mem, ctx)
        attention_block(nc, mem, ctx, 1, v_mask, ctx_tokens)
        quantised_ffn_block(nc, mem, ctx, out)


def lay_out(inp):
    import numpy as np

    f = {k: np.asarray(v) for k, v in inp.items()}
    a, x0, m, x1, g = "L0_attn_", "L0_xattn_", "L1_attn_", "L1_xattn_", "L1_ffn_"

    def blocks(w):
        return w.reshape(-1, 128, w.shape[1]).transpose(1, 0, 2).reshape(128, -1)

    parts = {
        "ln1_w": f[a + "ln1_w"], "ln1_b": f[a + "ln1_b"], "ln2_w": f[a + "ln2_w"], "ln2_b": f[a + "ln2_b"],
        "tmk": f[a + "att_tmk"], "tmv": f[a + "att_tmv"], "tmr": f[a + "att_tmr"],
        "decay": f[a + "time_decay"], "first": f[a + "time_first"],
        "ftmk": f[a + "ffn_tmk"], "ftmr": f[a + "ffn_tmr"], "bq": f[x0 + "bq"], "bk": f[x0 + "bk"], "bv": f[x0 + "bv"],
        "m_ln1_g": f[m + "ln1_g"], "m_ln1_b": f[m + "ln1_b"], "in_b0": f[m + "in_b"][:C], "in_b1": f[m + "in_b"][C:],
        "dw0": f[m + "dw_W"][:, 0, 0], "dw1": f[m + "dw_W"][:, 0, 1], "dw2": f[m + "dw_W"][:, 0, 2],
        "dw_b": f[m + "dw_b"], "dt_b": f[m + "dt_b"], "b_b": f[m + "b_b"], "c_b": f[m + "c_b"],
        "a_log": f[m + "a_log"], "d_skip": f[m + "d_skip"], "m_ln2_g": f[m + "ln2_g"], "m_ln2_b": f[m + "ln2_b"],
        "f1_b0": f[m + "f1_b"][:C], "f1_b1": f[m + "f1_b"][C:],
        "b_fc": f["L0_ffn_b_fc"].reshape(E, 4, 128).transpose(2, 0, 1),
        "WkT": f[a + "Wk"].T, "WvT": f[a + "Wv"].T, "WrT": f[a + "Wr"].T, "WoT": f[a + "Wo"].T,
        "WkeyT": f[a + "Wkey"].T, "WrecT": f[a + "Wrec"].T, "WvalT": blocks(f[a + "Wval"].T),
        "qT0": f[x0 + "Wq"].T, "kT0": f[x0 + "Wk"].T, "vT0": f[x0 + "Wv"].T, "oT0": f[x0 + "Wo"].T,
        "qT1": f[x1 + "Wq"].T, "kT1": f[x1 + "Wk"].T, "vT1": f[x1 + "Wv"].T, "oT1": f[x1 + "Wo"].T,
        "router": f["L0_ffn_router_w"].T, "in_W": f[m + "in_W"], "dt_W": f[m + "dt_W"], "b_W": f[m + "b_W"],
        "c_W": f[m + "c_W"], "out_W": f[m + "out_W"], "f1_W": f[m + "f1_W"], "f2_W": blocks(f[m + "f2_W"]),
        "gate": blocks(f[g + "w_gate"]), "up": blocks(f[g + "w_up"]), "down": f[g + "w_down"],
    }
    head_of = np.arange(128) % 32 // HD
    parts["head_mask"] = (np.arange(128)[:, None] // HD == np.arange(H)[None, :]).astype(np.float32)
    parts["rank"] = np.broadcast_to(np.arange(E, 0, -1, dtype=np.float32), (128, E))
    parts["ident"] = np.eye(128, dtype=np.float32)
    parts["causal"] = np.where(np.arange(S)[None, :] > np.arange(128)[:, None], np.float32(-1e30), np.float32(0))
    v_mask = np.broadcast_to(head_of[None, :] == np.arange(4)[:, None], (128, 4, C)).astype(np.float32)
    pack = np.concatenate([np.asarray(parts[n]).reshape(128, w) for n, w in LAYOUT], axis=1)
    rows = np.concatenate([f[x0 + "bo"], f[m + "out_b"], f[m + "f2_b"], f[x1 + "bo"]])[None, :]
    return {
        "x": f["x"], "ctx_tokens": f["ctx_1024"], "pack": pack, "rows": rows, "b_proj": f["L0_ffn_b_proj"],
        "w_fc": f["L0_ffn_w_fc"].transpose(1, 0, 2).reshape(128, E * HID),
        "w_proj": f["L0_ffn_w_proj"].reshape(E, 4, 128, C).transpose(2, 0, 1, 3).reshape(128, E * 4 * C),
        "v_mask": v_mask,
    }


def kernel(**inputs):
    import numpy as np
    import concourse.bacc as bacc
    from concourse.bass_utils import run_bass_kernel_spmd

    arrays = {f"in_{k}": np.ascontiguousarray(v) for k, v in lay_out(inputs).items()}
    nc = bacc.Bacc("TRN2", target_bir_lowering=False, num_devices=1)
    args = [nc.dram_tensor(k, v.shape, F32, kind="ExternalInput").ap() for k, v in arrays.items()]
    out = nc.dram_tensor("out", (B, T, C), F32, kind="ExternalOutput").ap()
    build(nc, *args, out)
    r = run_bass_kernel_spmd(nc, [arrays], core_ids=[0])
    return r.results[0]["out"]
```

```python
import concourse.bass as bass
import numpy as np
from concourse import mybir
from contextlib import ExitStack, contextmanager

F32 = mybir.dt.float32
BF16 = mybir.dt.bfloat16
F32R = mybir.dt.float32r
ACT = mybir.ActivationFunctionType
ALU = mybir.AluOpType
AX = mybir.AxisListType

B, T, C = 32, 128, 128
S = 77
CH = 4
NCH = B // CH
W = CH * T
NIT = NCH // 2
H, HD = 16, 8
E, HID = 8, 512
EPS = 1e-5
ATT_SCALE = float(HD) ** -0.5
NEG = -1e38

VECTORS = ["ln1_w", "ln1_b", "ln2_w", "ln2_b", "tmk", "tmv", "tmr", "decay", "first", "ftmk", "ftmr",
           "bq", "bk", "bv", "m_ln1_g", "m_ln1_b", "in_b0", "in_b1", "dw0", "dw1", "dw2", "dw_b", "dt_b",
           "b_b", "c_b", "a_log", "d_skip", "m_ln2_g", "m_ln2_b", "f1_b0", "f1_b1"]
LAYOUT = ([(n, 1) for n in VECTORS] +
          [("b_fc", E * 4), ("head_mask", H), ("rank", E), ("ident", 128), ("causal", S),
           ("WkT", C), ("WvT", C), ("WrT", C), ("WoT", C), ("WkeyT", 512), ("WrecT", C), ("WvalT", 4 * C),
           ("qT0", C), ("kT0", C), ("vT0", C), ("oT0", C), ("qT1", C), ("kT1", C), ("vT1", C), ("oT1", C),
           ("router", 32), ("in_W", 2 * C), ("dt_W", C), ("b_W", C), ("c_W", C), ("out_W", C),
           ("f1_W", 2 * C), ("f2_W", 2 * C), ("gate", 3 * C), ("up", 3 * C), ("down", 3 * C)])
AT, NPACK = {}, 0
for _n, _w in LAYOUT:
    AT[_n] = (NPACK, _w)
    NPACK += _w
ROWS = ["bo0", "m_out_b", "f2_b", "bo1"]

ARENA = 34096
KEPT_WORDS = B * S + B * C


class Steps:

    def __init__(self, sem, names, ahead=0, base=0):
        self.sem, self.names, self.ahead, self.base = sem, names.split(), ahead, base
        assert len(set(self.names)) == len(self.names)

    def done(self, turn, name):
        return turn * len(self.names) + (self.base + self.ahead * len(self.names) + self.names.index(name) + 1)

    def previous(self, turn, p, name):
        return self.done(turn, f"{name}0") if p else self.done(turn - 1, f"{name}1")

    def credit(self):
        return self.ahead * len(self.names)


class Memory:

    def __init__(self, nc, ctx):
        def sb(name, shape, dt=F32):
            return ctx.enter_context(nc.sbuf_tensor(name, shape, dt))

        self.x = sb("x_res", [128, B, C])
        self.xl = sb("x_norm", [128, B, C])
        self.hT = sb("hT", [128, B, T + 1])
        self.pack = sb("pack", [128, NPACK])
        self.rows = sb("rows", [1, len(ROWS) * C])
        self.b_proj = sb("b_proj", [128, C])
        self.ones = sb("ones", [128, 128])
        self.half = sb("half", [128, B // 2])
        self.bn = sb("bn", [128, B, 6])
        self.stats_taken = False
        self.tmp = sb("bn_sums", [128, 2, 5, B // 2])
        self.mean = sb("mean", [128, B])
        self.rs = sb("rs", [128, 4, B])
        self.eps = sb("eps", [128, B // 2])
        self.ps = ctx.enter_context(nc.psum_tensor("psum", [128, 8 * W], F32))
        self.norm_sems = [ctx.enter_context(nc.semaphore(f"norm_{n}")) for n in ("stats", "pool", "rooted")]
        self.norm_counts = [0, 0, 0]
        self.nc = nc
        self.hn = None

    @contextmanager
    def block_memory(self, name, words):
        with self.nc.sbuf_tensor(name, [128, words], F32) as self.arena:
            self.at, self.size = 0, words
            yield

    @contextmanager
    def kept_memory(self):
        with self.nc.sbuf_tensor("kv1", [128, KEPT_WORDS], F32) as self.kv1:
            yield

    def col(self, name, i=0):
        o = AT[name][0] + i
        return self.pack[:, o:o + 1]

    def mat(self, name, i=0, w=C):
        o = AT[name][0] + i * w
        return self.pack[:, o:o + w]

    def row(self, name):
        i = ROWS.index(name)
        return self.rows[0:1, i * C:(i + 1) * C]

    def bank(self, i):
        return self.ps[:, i * W:(i + 1) * W]

    def take(self, *shape):
        n = 1
        for s in shape:
            n *= s
        self.at += n
        assert self.at <= self.size, (self.at, self.size)
        v = self.arena[:, self.at - n:self.at]
        if len(shape) == 1:
            return v
        names = "abcde"[:len(shape)]
        return v.rearrange(f"p ({' '.join(names)}) -> p {' '.join(names)}", **dict(zip(names[:-1], shape)))


class Norm:

    def __init__(self, nc, mem, ctx, tag, src, double=False, affine=None, whole=False, banks=(6, 7), loaded=None):
        def sem(n):
            return ctx.enter_context(nc.semaphore(f"{tag}_{n}"))

        self.mem, self.src, self.double, self.affine, self.banks, self.loaded = mem, src, double, affine, banks, loaded
        self.taken = src is mem.x and mem.stats_taken
        mem.stats_taken = False
        (stats, pool, self.rooted), counts = mem.norm_sems, mem.norm_counts
        self.stats = Steps(stats, ("" if self.taken else "bn ") + "diff square mean var veps", base=counts[0])
        self.pool = Steps(pool, "r1 a b c", base=counts[1])
        self.rooted_before = counts[2]
        counts[0] += 2 * len(self.stats.names)
        counts[1] += 2 * len(self.pool.names) if double else 0
        counts[2] += NIT
        self.dve = Steps(sem("dve"), "centred inner amax" if whole else
                         "centred0 centred1 inner0 inner1 scaled0 scaled1" if double else "centred0 centred1 scaled0 scaled1", 1)
        self.pe = Steps(sem("pe"), "turned0 turned1", 1)
        self.act = Steps(sem("act"), "ready0 ready1", 1)

    def vector_stats(self, dve):
        m, d, N = self.mem, self.stats, B // 2
        for h in range(2):
            at = slice(h * N, h * N + N)
            stat, tmp = m.bn[:, at], m.tmp[:, h]

            def after(name):
                dve.wait_ge(d.sem, d.done(h, name))

            if self.loaded:
                dve.wait_ge(self.loaded[h], 16)
            if not self.taken:
                for n in range(N):
                    last = dve.bn_stats(stat[:, n, :], self.src[:, h * N + n, :])
                last.then_inc(d.sem, 1)
                after("bn")
            dve.tensor_tensor(tmp[:, 0, :], stat[:, :, 1], stat[:, :, 4], ALU.subtract).then_inc(d.sem, 1)
            dve.tensor_tensor(tmp[:, 2, :], stat[:, :, 2], stat[:, :, 5], ALU.add)
            dve.tensor_tensor(tmp[:, 3, :], stat[:, :, 1], stat[:, :, 4], ALU.add)
            after("diff")
            dve.tensor_tensor(tmp[:, 1, :], tmp[:, 0, :], tmp[:, 0, :], ALU.mult).then_inc(d.sem, 1)
            after("square")
            dve.tensor_scalar(m.mean[:, at], tmp[:, 3, :], 0.5, None, ALU.mult).then_inc(d.sem, 1)
            dve.scalar_tensor_tensor(tmp[:, 4, :], tmp[:, 1, :], 32.0, tmp[:, 2, :], ALU.mult, ALU.add).then_inc(d.sem, 1)
            after("var")
            dve.tensor_scalar(m.rs[:, 3, at], tmp[:, 4, :], 1.0 / C, None, ALU.mult)
            dve.tensor_scalar(m.rs[:, 0, at], tmp[:, 4, :], 1.0 / C, EPS, ALU.mult, ALU.add).then_inc(d.sem, 1)

    def pool_pass(self, pool):
        rs, g, N = self.mem.rs, self.pool, B // 2
        half, eps = self.mem.half[:, 0:N], self.mem.eps[:, 0:N]
        for h in range(2):
            at = slice(h * N, h * N + N)

            def after(name):
                pool.wait_ge(g.sem, g.done(h, name))

            pool.wait_ge(self.stats.sem, self.stats.done(h, "veps"))
            root = pool.tensor_tensor(rs[:, 1, at], rs[:, 0, at], half, ALU.pow)
            if not self.double:
                root.then_inc(self.rooted, 2)
                continue
            root.then_inc(g.sem, 1)
            after("r1")
            pool.tensor_tensor(rs[:, 2, at], rs[:, 3, at], rs[:, 1, at], ALU.mult).then_inc(g.sem, 1)
            after("a")
            pool.tensor_tensor(rs[:, 0, at], rs[:, 2, at], rs[:, 1, at], ALU.mult).then_inc(g.sem, 1)
            after("b")
            pool.tensor_tensor(rs[:, 3, at], rs[:, 0, at], eps, ALU.add).then_inc(g.sem, 1)
            after("c")
            pool.tensor_tensor(rs[:, 2, at], rs[:, 3, at], half, ALU.pow).then_inc(self.rooted, 2)

    def vector_scale(self, dve, it):
        m, d = self.mem, self.dve

        def wide(v, p):
            return v[:, bass.ds((it * 2 + p) * CH, CH)].unsqueeze(2).broadcast_to([128, CH, C])

        def first(p):
            return chunk(m.xl, it, p) if self.double else m.hn[:, p]

        def free(p):
            dve.wait_ge(self.pe.sem, self.pe.done(it - 1, f"turned{p}"))

        dve.wait_ge(self.rooted, it + (self.rooted_before + 1))
        for p in range(2):
            if not self.double:
                free(p)
            dve.tensor_tensor(first(p), chunk(self.src, it, p), wide(m.mean, p), ALU.subtract).then_inc(d.sem, 1)
        for p in range(2):
            dve.wait_ge(d.sem, d.done(it, f"centred{p}"))
            dve.tensor_tensor(first(p), first(p), wide(m.rs[:, 1], p), ALU.mult).then_inc(d.sem, 1)
        if self.double:
            for p in range(2):
                dve.wait_ge(d.sem, d.done(it, f"inner{p}"))
                free(p)
                dve.tensor_tensor(m.hn[:, p], first(p), wide(m.rs[:, 2], p), ALU.mult).then_inc(d.sem, 1)

    def vector_scale_whole(self, dve, it, amax):
        m, d, N = self.mem, self.dve, 2 * CH
        at = bass.ds(it * N, N)
        dve.wait_ge(self.rooted, it + (self.rooted_before + 1))
        for name, src, v, op in (("centred", self.src, m.mean[:, at], ALU.subtract), ("inner", m.xl, m.rs[:, 1, at], ALU.mult)):
            dve.tensor_tensor(m.xl[:, at, :], src[:, at, :], v.unsqueeze(2).broadcast_to([128, N, C]), op).then_inc(d.sem, 1)
            dve.wait_ge(d.sem, d.done(it, name))
        dve.tensor_reduce(amax[:, bass.ds(it, 1)], m.xl[:, at, :], AX.XY, ALU.max, apply_absolute_value=True).then_inc(d.sem, 1)

    def vector_begin(self, dve):
        dve.sem_inc(self.dve.sem, self.dve.credit())
        self.vector_stats(dve)
        dve.wait_ge(self.stats.sem, self.stats.done(1, "veps"))

    def vector_pass(self, dve, amax=None):
        self.vector_begin(dve)
        with dve.Fori(0, NIT) as it:
            if amax is None:
                self.vector_scale(dve, it)
            else:
                self.vector_scale_whole(dve, it, amax)

    def tensor_turn(self, pe, it):
        m = self.mem
        for p in range(2):
            pe.wait_ge(self.dve.sem, self.dve.done(it, f"scaled{p}"))
            pe.wait_ge(self.act.sem, self.act.done(it - 1, f"ready{p}"))
            for j in range(CH):
                last = pe.transpose(m.bank(self.banks[p])[:, j * T:(j + 1) * T], m.hn[:, p, j, :], m.mat("ident"))
            last.then_inc(self.pe.sem, 1)

    def scalar_turn(self, act, it):
        m = self.mem
        for p in range(2):
            c = (it * 2 + p) * CH
            act.wait_ge(self.pe.sem, self.pe.done(it, f"turned{p}"))
            out = m.hT[:, bass.ds(c, CH), 1:T + 1]
            src = m.bank(self.banks[p]).rearrange("p (b t) -> p b t", b=CH)
            if self.affine:
                ins = act.activation(out, src, ACT.Identity, bias=m.col(self.affine[1]), scale=m.col(self.affine[0]))
            else:
                ins = act.activation(out, src, ACT.Copy)
            ins.then_inc(self.act.sem, 1)


def take_stats(dve, mem, it, p):
    mem.stats_taken = True
    for j in range(CH):
        at = bass.ds((it * 2 + p) * CH + j, 1)
        dve.bn_stats(mem.bn[:, at, :].rearrange("p a s -> p (a s)"), mem.x[:, at, :].rearrange("p a c -> p (a c)"))


def chunk(buf, it, p):
    return buf[:, bass.ds((it * 2 + p) * CH, CH), :]


def skewed(eng, turns, items, *stages):
    behind = any(kind == -1 for kind, stage in stages)

    def turn(it, first, last):
        for n in range(items):
            for kind, stage in stages:
                if kind == 0:
                    stage(it, n)
                elif kind == 1 and n + 1 < items:
                    stage(it, n + 1)
                elif kind == 1 and not last:
                    stage(it + 1, 0)
                elif kind == -1 and n > 0:
                    stage(it, n - 1)
                elif kind == -1 and not first:
                    stage(it - 1, items - 1)
                elif kind == "turn" and n == items - 2 and not last:
                    stage(it + 1)

    for kind, stage in stages:
        if kind == "turn":
            stage(0)
    for kind, stage in stages:
        if kind == 1:
            stage(0, 0)
    if behind:
        turn(0, True, False)
    with eng.Fori(1 if behind else 0, turns - 1) as it:
        turn(it, False, False)
    turn(turns - 1, False, True)
    for kind, stage in stages:
        if kind == -1:
            stage(turns - 1, items - 1, final=True)




def load_block(nc, mem, ctx, x, pack, rows, b_proj):
    def sem(n):
        return ctx.enter_context(nc.semaphore(n))

    x_loaded, loaded = [sem("x_loaded0"), sem("x_loaded1")], sem("loaded")
    with nc.Block() as block:
        @block.sync
        def _(sp):
            for h in range(2):
                at = slice(h * B // 2, (h + 1) * B // 2)
                sp.dma_start(mem.x[:, at, :], x[at].rearrange("b t c -> t b c")).then_inc(x_loaded[h], 16)

        @block.scalar
        def _(act):
            act.dma_start(mem.pack[:, :], pack).then_inc(loaded, 16)
            act.dma_start(mem.rows[:, :], rows).then_inc(loaded, 16)
            act.dma_start(mem.b_proj[:, :], b_proj).then_inc(loaded, 16)

        @block.gpsimd
        def _(pool):
            pool.memset(mem.ones[:, :], 1.0)
            pool.memset(mem.half[:, :], -0.5)
            pool.memset(mem.eps[:, :], EPS)
            pool.memset(mem.hT[:, :, 0:1], 0.0)
    return x_loaded, loaded


def time_mix_block(nc, mem, ctx, x_loaded, loaded):
    def sem(n):
        return ctx.enter_context(nc.semaphore(n))

    mem.hn = mem.take(2, CH, C)
    PAD = T + 1
    kp = mem.take(B, PAD)
    vT = mem.take(B, T)
    sr = mem.take(B, T)
    mark = mem.at
    mixd = mem.take(W)
    mixed = mem.take(2, 3, W)
    wpad = mem.take(CH, PAD)
    wneg = mem.take(2)
    P = mem.take(2, CH, PAD)
    expo = mem.take(2, 4, CH, T)
    keep = mem.take(2, 2, CH, PAD)
    outw = mem.take(2, 2, CH, T)
    qmax = mem.take(2, CH, T)
    bv = mem.take(2, CH, PAD)
    aa = mem.take(2, CH, PAD)
    bb = mem.take(2, CH, PAD)
    num = mem.take(2, 2, CH, T)
    rw = mixed[:, :, 0]
    den = [mixed[:, p, 1].rearrange("p (b t) -> p b t", b=CH) for p in range(2)]
    inv = [mixed[:, p, 2].rearrange("p (b t) -> p b t", b=CH) for p in range(2)]
    top = mem.at
    mem.at = mark + W + 6 * W
    relu = mem.take(4, W)
    kk = mem.take(2, CH, W)
    gate = mem.take(2, W)
    gated = mem.take(2, W)
    mem.at = max(mem.at, top)

    n1 = Norm(nc, mem, ctx, "n1", mem.x, double=True, affine=("ln1_w", "ln1_b"), loaded=x_loaded)
    n2 = Norm(nc, mem, ctx, "n2", mem.xl, affine=("ln2_w", "ln2_b"))
    init = Steps(sem("tm_init_pool"), "kp keep bv wpad")
    decay_made = sem("tm_decay")
    md = Steps(sem("mix_dve"), "d0 k0 v0 r0 d1 k1 v1 r1", 1)
    mp = Steps(sem("mix_pe"), "k0 v0 r0 k1 v1 r1", 1)
    ma = Steps(sem("mix_act"), "k0 v0 r0 k1 v1 r1", 1)
    wd = Steps(sem("wkv_dve"), "P0 P1 decay0 q0 decay1 q1 ww0 ww1 bb0 aa0 bb1 aa1 d10 d11 den0 n10 den1 n11 "
               "y0 y1 rw0 rw1", 1)
    wo = Steps(sem("wkv_add"), "add0 add1")
    wp = Steps(sem("wkv_pool"), "key0 key1 past0 past1 bv0 bv1 n20 n21 num0 num1", 1)
    wa = Steps(sem("wkv_act"), "keep0 keep1 outw0 outw1 ln0 inv0 ln1 inv1", 1)
    we = Steps(sem("wkv_pe"), "out0 out1", 1)
    cx = Steps(sem("cm_mix"), "d0 k0 r0 d1 k1 r1", 1)
    cs = Steps(sem("cm_square"), "sq00 sq02 sq10 sq12", 1)
    cd = Steps(sem("cm_add"), "res0 res1 gated0 add0 gated1 add1", 1)
    ce = Steps(sem("cm_pe"), "key00 key01 key02 key03 rec0 key10 key11 key12 key13 rec1 val0 val1", 1)
    ca = Steps(sem("cm_act"), "relu00 relu01 sq01 relu02 relu03 sq03 gate0 relu10 relu11 sq11 relu12 relu13 sq13 gate1", 1)
    bank = mem.bank

    def batches(v):
        return v.rearrange("p (b t) -> p b t", b=CH)

    with nc.Block() as block:
        @block.gpsimd
        def _(pool):
            pool.memset(kp[:, :, 0:1], NEG).then_inc(init.sem, 1)
            pool.memset(keep[:, :, :, :, :], 0.0).then_inc(init.sem, 1)
            pool.memset(bv[:, :, :, :], 0.0).then_inc(init.sem, 1)
            pool.memset(wpad[:, :, :], NEG).then_inc(init.sem, 1)
            pool.sem_inc(wp.sem, wp.credit())
            n1.pool_pass(pool)
            with pool.Fori(0, NIT) as it:
                for p in range(2):
                    pool.wait_ge(wd.sem, wd.done(it, f"P{p}"))
                    pool.wait_ge(wa.sem, wa.done(it - 1, f"outw{p}"))
                    pool.tensor_tensor(expo[:, p, 1], chunk(kp, it, p)[:, :, 1:PAD], P[:, p, :, 1:PAD],
                                       ALU.subtract).then_inc(wp.sem, 1)
                for p in range(2):
                    pool.wait_ge(wd.sem, wd.done(it, f"q{p}"))
                    pool.tensor_tensor(expo[:, p, 2], P[:, p, :, 0:T], qmax[:, p], ALU.subtract).then_inc(wp.sem, 1)
                for p in range(2):
                    pool.wait_ge(wa.sem, wa.done(it, f"keep{p}"))
                    pool.wait_ge(wd.sem, wd.done(it - 1, f"aa{p}"))
                    pool.tensor_tensor(bv[:, p, :, 1:PAD], keep[:, p, 1, :, 1:PAD], chunk(vT, it, p), ALU.mult).then_inc(wp.sem, 1)
                for p in range(2):
                    pool.wait_ge(wa.sem, wa.done(it, f"outw{p}"))
                    pool.wait_ge(wd.sem, wd.done(it, f"aa{p}"))
                    pool.tensor_tensor(num[:, p, 1], outw[:, p, 0], aa[:, p, :, 0:T], ALU.mult).then_inc(wp.sem, 1)
                for p in range(2):
                    pool.wait_ge(wp.sem, wp.done(it, f"n2{p}"))
                    pool.wait_ge(wd.sem, wd.done(it, f"n1{p}"))
                    pool.tensor_tensor(num[:, p, 0], num[:, p, 0], num[:, p, 1], ALU.add).then_inc(wp.sem, 1)
            n2.pool_pass(pool)

        @block.vector
        def _(dve):
            for s in (md, wd, cx, cs, cd):
                dve.sem_inc(s.sem, s.credit())
            n1.vector_pass(dve)
            dve.wait_ge(loaded, 48)
            dve.wait_ge(decay_made, 1)
            dve.tensor_scalar(wneg[:, 1:2], wneg[:, 0:1], -1.0, None, ALU.mult).then_inc(decay_made, 1)
            dve.wait_ge(decay_made, 2)
            dve.wait_ge(init.sem, 4)
            dve.tensor_scalar(wpad[:, :, 1:PAD],
                              mem.x[:, 0:CH, :], 0.0, wneg[:, 1:2], ALU.mult, ALU.add).then_inc(decay_made, 1)
            with dve.Fori(0, NIT) as it:
                for p in range(2):
                    hc = chunk(mem.hT, it, p)
                    h, hh = hc[:, :, 1:T + 1], hc[:, :, 0:T]
                    dve.wait_ge(n1.act.sem, n1.act.done(it, f"ready{p}"))
                    dve.wait_ge(md.sem, md.previous(it, p, "r"))
                    dve.tensor_tensor(batches(mixd[:, :]), h, hh, ALU.subtract).then_inc(md.sem, 1)
                    dve.wait_ge(md.sem, md.done(it, f"d{p}"))
                    for i, name in enumerate("kvr"):
                        dve.wait_ge(mp.sem, mp.done(it - 1, f"{name}{p}"))
                        dve.scalar_tensor_tensor(batches(mixed[:, p, i]), batches(mixd[:, :]), mem.col(f"tm{name}"), hh,
                                                 ALU.mult, ALU.add).then_inc(md.sem, 1)
            with dve.Fori(0, NIT) as it:
                k = [chunk(kp, it, p)[:, :, 1:PAD] for p in range(2)]
                past, now = [P[:, p, :, 0:T] for p in range(2)], [P[:, p, :, 1:PAD] for p in range(2)]

                def flat(v):
                    return v.rearrange("p b t -> p (b t)")

                def after(name):
                    dve.wait_ge(wd.sem, wd.done(it, name))

                for p in range(2):
                    dve.wait_ge(ma.sem, ma.done(it, f"r{p}"))
                    dve.wait_ge(decay_made, 3)
                    dve.wait_ge(wp.sem, wp.done(it - 1, f"past{p}"))
                    dve.tensor_tensor_scan(flat(P[:, p]), flat(wpad), flat(chunk(kp, it, p)), NEG,
                                           ALU.add, ALU.max).then_inc(wd.sem, 1)
                for p in range(2):
                    after(f"P{p}")
                    dve.wait_ge(wa.sem, wa.done(it - 1, f"outw{p}"))
                    dve.scalar_tensor_tensor(expo[:, p, 0], past[p], wneg[:, 1:2], now[p],
                                             ALU.add, ALU.subtract).then_inc(wd.sem, 1)
                    dve.scalar_tensor_tensor(qmax[:, p], k[p], mem.col("first"), past[p],
                                             ALU.add, ALU.max).then_inc(wd.sem, 1)
                for p in range(2):
                    after(f"q{p}")
                    dve.scalar_tensor_tensor(expo[:, p, 3], k[p], mem.col("first"), qmax[:, p],
                                             ALU.add, ALU.subtract).then_inc(wd.sem, 1)
                for p in range(2):
                    dve.wait_ge(wa.sem, wa.done(it, f"keep{p}"))
                    dve.tensor_tensor_scan(flat(bb[:, p]), flat(keep[:, p, 0]), flat(keep[:, p, 1]), 0.0,
                                           ALU.mult, ALU.add).then_inc(wd.sem, 1)
                    dve.wait_ge(wp.sem, wp.done(it, f"bv{p}"))
                    dve.tensor_tensor_scan(flat(aa[:, p]), flat(keep[:, p, 0]), flat(bv[:, p]), 0.0,
                                           ALU.mult, ALU.add).then_inc(wd.sem, 1)
                dve.wait_ge(mp.sem, mp.done(NIT - 1, "r1"))
                for p in range(2):
                    after(f"bb{p}")
                    dve.wait_ge(wa.sem, wa.done(it, f"outw{p}"))
                    dve.tensor_tensor(den[p], outw[:, p, 0], bb[:, p, :, 0:T], ALU.mult).then_inc(wd.sem, 1)
                for p in range(2):
                    after(f"d1{p}")
                    dve.tensor_tensor(den[p], den[p], outw[:, p, 1], ALU.add).then_inc(wd.sem, 1)
                    dve.tensor_tensor(num[:, p, 0], outw[:, p, 1], chunk(vT, it, p), ALU.mult).then_inc(wd.sem, 1)
                for p in range(2):
                    dve.wait_ge(wp.sem, wp.done(it, f"num{p}"))
                    dve.wait_ge(wa.sem, wa.done(it, f"inv{p}"))
                    dve.tensor_tensor(num[:, p, 0], num[:, p, 0], inv[p], ALU.mult).then_inc(wd.sem, 1)
                for p in range(2):
                    after(f"y{p}")
                    dve.wait_ge(we.sem, we.done(it - 1, f"out{p}"))
                    dve.tensor_tensor(batches(rw[:, p]), num[:, p, 0], chunk(sr, it, p), ALU.mult).then_inc(wd.sem, 1)
            with dve.Fori(0, NIT) as it:
                for p in range(2):
                    xl = chunk(mem.xl, it, p)
                    dve.wait_ge(we.sem, we.done(it, f"out{p}"))
                    dve.tensor_tensor(xl, xl, batches(mem.ps[:, bass.ds((it * 2 + p) * W, W)]), ALU.add).then_inc(wo.sem, 1)
            dve.wait_ge(wo.sem, wo.done(NIT - 1, "add1"))
            n2.vector_pass(dve)

            def mix(it):
                for p in range(2):
                    hc = chunk(mem.hT, it, p)
                    h, hh = hc[:, :, 1:T + 1], hc[:, :, 0:T]
                    dve.wait_ge(n2.act.sem, n2.act.done(it, f"ready{p}"))
                    dve.wait_ge(cx.sem, cx.previous(it, p, "r"))
                    dve.tensor_tensor(batches(mixd[:, :]), h, hh, ALU.subtract).then_inc(cx.sem, 1)
                    dve.wait_ge(cx.sem, cx.done(it, f"d{p}"))
                    dve.wait_ge(ce.sem, ce.done(it - 1, f"rec{p}"))
                    for i, name in enumerate("kr"):
                        dve.scalar_tensor_tensor(batches(mixed[:, p, i]), batches(mixd[:, :]), mem.col(f"ftm{name}"), hh,
                                                 ALU.mult, ALU.add).then_inc(cx.sem, 1)

            def squares(it):
                for p in range(2):
                    for k in (0, 2):
                        dve.wait_ge(ca.sem, ca.done(it, f"relu{p}{k}"))
                        dve.wait_ge(ce.sem, ce.done(it - 1, f"val{p}"))
                        dve.tensor_tensor(kk[:, p, k], relu[:, k], relu[:, k], ALU.mult).then_inc(cs.sem, 1)

            def add(it):
                for p in range(2):
                    x = chunk(mem.x, it, p)
                    dve.tensor_tensor(x, x, chunk(mem.xl, it, p), ALU.add).then_inc(cd.sem, 1)
                for p in range(2):
                    x = chunk(mem.x, it, p)
                    dve.wait_ge(ca.sem, ca.done(it, f"gate{p}"))
                    dve.wait_ge(ce.sem, ce.done(it, f"val{p}"))
                    dve.tensor_tensor(gated[:, p], gate[:, p], bank(6 + p)[:, :], ALU.mult).then_inc(cd.sem, 1)
                    dve.wait_ge(cd.sem, cd.done(it, f"gated{p}"))
                    dve.tensor_tensor(x, x, batches(gated[:, p]), ALU.add).then_inc(cd.sem, 1)
                for p in range(2):
                    dve.wait_ge(cd.sem, cd.done(it, f"add{p}"))
                    take_stats(dve, mem, it, p)

            mix(0)
            with dve.Fori(0, NIT - 1) as it:
                squares(it)
                mix(it + 1)
                add(it)
            squares(NIT - 1)
            add(NIT - 1)

        @block.scalar
        def _(act):
            for s in (n1.act, n2.act, ma, wa, ca):
                act.sem_inc(s.sem, s.credit())
            act.wait_ge(loaded, 48)
            act.activation(wneg[:, 0:1], mem.col("decay"), ACT.Exp).then_inc(decay_made, 1)
            with act.Fori(0, NIT) as it:
                n1.scalar_turn(act, it)
            act.preload_act_table(ACT.Sigmoid)
            with act.Fori(0, NIT) as it:
                for p in range(2):
                    act.wait_ge(mp.sem, mp.done(it, f"k{p}"))
                    act.wait_ge(init.sem, 1)
                    act.activation(chunk(kp, it, p)[:, :, 1:PAD], batches(bank(p)[:, :]), ACT.Copy).then_inc(ma.sem, 1)
                    act.wait_ge(mp.sem, mp.done(it, f"v{p}"))
                    act.activation(chunk(vT, it, p), batches(bank(2 + p)[:, :]), ACT.Copy).then_inc(ma.sem, 1)
                    act.wait_ge(mp.sem, mp.done(it, f"r{p}"))
                    act.activation(chunk(sr, it, p), batches(bank(4 + p)[:, :]), ACT.Sigmoid).then_inc(ma.sem, 1)
            act.preload_act_table_set("natural_log_exp_and_others")
            act.wait_ge(init.sem, 3)
            with act.Fori(0, NIT) as it:
                for p in range(2):
                    act.wait_ge(wd.sem, wd.done(it, f"decay{p}"))
                    act.wait_ge(wp.sem, wp.done(it, f"key{p}"))
                    act.wait_ge(wd.sem, wd.done(it - 1, f"bb{p}"))
                    act.wait_ge(wd.sem, wd.done(it - 1, f"aa{p}"))
                    act.activation(keep[:, p].rearrange("p a b t -> p (a b) t")[:, :, 1:PAD],
                                   expo[:, p, 0:2].rearrange("p a b t -> p (a b) t"), ACT.Exp).then_inc(wa.sem, 1)
                for p in range(2):
                    act.wait_ge(wd.sem, wd.done(it, f"ww{p}"))
                    act.wait_ge(wp.sem, wp.done(it, f"past{p}"))
                    act.wait_ge(wd.sem, wd.done(it - 1, f"n1{p}"))
                    act.wait_ge(wp.sem, wp.done(it - 1, f"n2{p}"))
                    act.activation(outw[:, p].rearrange("p a b t -> p (a b t)"),
                                   expo[:, p, 2:4].rearrange("p a b t -> p (a b t)"), ACT.Exp).then_inc(wa.sem, 1)
                for p in range(2):
                    act.wait_ge(wd.sem, wd.done(it, f"den{p}"))
                    act.wait_ge(wd.sem, wd.done(it - 1, f"y{p}"))
                    act.activation(inv[p], den[p], ACT.Ln).then_inc(wa.sem, 1)
                    act.wait_ge(wa.sem, wa.done(it, f"ln{p}"))
                    act.activation(inv[p], inv[p], ACT.Exp, scale=-1.0).then_inc(wa.sem, 1)
            with act.Fori(0, NIT) as it:
                n2.scalar_turn(act, it)
            act.preload_act_table(ACT.Sigmoid)
            with act.Fori(0, NIT) as it:
                for p in range(2):
                    for k in range(4):
                        act.wait_ge(ce.sem, ce.done(it, f"key{p}{k}"))
                        turn, before = (it, 0) if p else (it - 1, 1)
                        squared = cs if k % 2 == 0 else ca
                        act.wait_ge(squared.sem, squared.done(turn, f"sq{before}{k}"))
                        act.activation(relu[:, k], bank(k)[:, :], ACT.Relu).then_inc(ca.sem, 1)
                        if k % 2 == 1:
                            act.wait_ge(ca.sem, ca.done(it, f"relu{p}{k}"))
                            act.wait_ge(ce.sem, ce.done(it - 1, f"val{p}"))
                            act.activation(kk[:, p, k], relu[:, k], ACT.Square).then_inc(ca.sem, 1)
                    act.wait_ge(ce.sem, ce.done(it, f"rec{p}"))
                    act.wait_ge(cd.sem, cd.done(it - 1, f"gated{p}"))
                    act.activation(gate[:, p], bank(4 + p)[:, :], ACT.Sigmoid).then_inc(ca.sem, 1)

        @block.tensor
        def _(pe):
            for s in (n1.pe, n2.pe, mp, we, ce):
                pe.sem_inc(s.sem, s.credit())
            pe.wait_ge(loaded, 48)
            with pe.Fori(0, NIT) as it:
                n1.tensor_turn(pe, it)
            with pe.Fori(0, NIT) as it:
                for p in range(2):
                    for i, name in enumerate("kvr"):
                        pe.wait_ge(md.sem, md.done(it, f"{name}{p}"))
                        pe.wait_ge(ma.sem, ma.done(it - 1, f"{name}{p}"))
                        pe.matmul(bank(2 * i + p)[:, :], mem.mat(f"W{name}T"), mixed[:, p, i], start=True, stop=True).then_inc(mp.sem, 1)
            with pe.Fori(0, NIT) as it:
                for p in range(2):
                    pe.wait_ge(wd.sem, wd.done(it, f"rw{p}"))
                    for j in range(CH):
                        out = mem.ps[:, bass.ds((it * 2 + p) * W + j * T, T)]
                        last = pe.matmul(out, rw[:, p, j * T:(j + 1) * T], mem.mat("WoT"),
                                         start=True, stop=True)
                    last.then_inc(we.sem, 1)
            with pe.Fori(0, NIT) as it:
                n2.tensor_turn(pe, it)
            with pe.Fori(0, NIT) as it:
                for p in range(2):
                    pe.wait_ge(cx.sem, cx.done(it, f"k{p}"))
                    for k in range(4):
                        pe.wait_ge(ca.sem, ca.done(it, f"relu0{k}") if p else ca.done(it - 1, f"relu1{k}"))
                        pe.matmul(bank(k)[:, :], mem.mat("WkeyT", k), mixed[:, p, 0], start=True, stop=True).then_inc(ce.sem, 1)
                    pe.wait_ge(cx.sem, cx.done(it, f"r{p}"))
                    pe.wait_ge(ca.sem, ca.done(it - 1, f"gate{p}"))
                    for j in range(CH):
                        last = pe.matmul(bank(4 + p)[:, j * T:(j + 1) * T], mixed[:, p, 1, j * T:(j + 1) * T], mem.mat("WrecT"),
                                         start=True, stop=True)
                    last.then_inc(ce.sem, 1)
                for p in range(2):
                    pe.wait_ge(cs.sem, cs.done(it, f"sq{p}2"))
                    pe.wait_ge(ca.sem, ca.done(it, f"sq{p}3"))
                    pe.wait_ge(cd.sem, cd.done(it - 1, f"gated{p}"))
                    for j in range(CH):
                        for k in range(4):
                            last = pe.matmul(bank(6 + p)[:, j * T:(j + 1) * T], kk[:, p, k, j * T:(j + 1) * T],
                                             mem.mat("WvalT", k), start=(k == 0), stop=(k == 3))
                    last.then_inc(ce.sem, 1)


def kv_views(v):
    return (v[:, 0:B * S].rearrange("p (b s) -> p b s", b=B),
            v[:, B * S:KEPT_WORDS].rearrange("p (b c) -> p b c", b=B))


class Context:

    def __init__(self, nc, mem, ctx, tokens, kv):
        def sem(n):
            return ctx.enter_context(nc.semaphore(n))

        self.mem = mem
        self.keys, self.values = zip(*kv)
        self.cn = mem.take(2, CH, C)
        self.cT = mem.take(2, CH * S)
        self.loaded = [sem("ctx_loaded0"), sem("ctx_loaded1")]
        self.pe = Steps(sem("ctx_pe"), "turned0 turned1 k00 k10 v00 v10 k01 k11 v01 v11", 1)
        self.act = Steps(sem("ctx_act"), "cT0 cT1 k00 k10 v00 v10 k01 k11 v01 v11", 1)
        self.src = tokens.rearrange("b s c -> s b c")

    def load_turn(self, sp, it):
        for p in range(2):
            sp.wait_ge(self.pe.sem, self.pe.done(it - 1, f"turned{p}"))
            sp.dma_start(self.cn[0:S, p], self.src[:, bass.ds((it * 2 + p) * CH, CH), :]).then_inc(self.loaded[p], 16)

    def tensor_turn(self, pe, it):
        mem, e, a = self.mem, self.pe, self.act
        for p in range(2):
            pe.wait_ge(self.loaded[p], it * 16 + 16)
            pe.wait_ge(a.sem, a.done(it - 1, f"cT{p}"))
            for j in range(CH):
                last = pe.transpose(mem.bank(4 + p)[:, j * S:(j + 1) * S], self.cn[0:S, p, j, :], mem.mat("ident")[0:S, 0:S])
            last.then_inc(e.sem, 1)
        for p in range(2):
            pe.wait_ge(a.sem, a.done(it, f"cT{p}"))
            for l in range(2):
                pe.wait_ge(a.sem, a.previous(it, p, f"k{l}"))
                pe.matmul(mem.bank(l)[:, 0:CH * S], mem.mat(f"kT{l}"), self.cT[:, p], start=True, stop=True).then_inc(e.sem, 1)
            for l in range(2):
                pe.wait_ge(a.sem, a.previous(it, p, f"v{l}"))
                for j in range(CH):
                    last = pe.matmul(mem.bank(2 + l)[0:S, j * C:(j + 1) * C], self.cT[:, p, j * S:(j + 1) * S],
                                     mem.mat(f"vT{l}"), start=True, stop=True)
                last.then_inc(e.sem, 1)

    def scalar_turn(self, act, it):
        mem, e, a = self.mem, self.pe, self.act
        for p in range(2):
            act.wait_ge(e.sem, e.done(it, f"turned{p}"))
            act.wait_ge(e.sem, e.done(it - 1, f"v1{p}"))
            act.activation(self.cT[:, p], mem.bank(4 + p)[:, 0:CH * S], ACT.Copy).then_inc(a.sem, 1)
        for p in range(2):
            for l in range(2):
                act.wait_ge(e.sem, e.done(it, f"k{l}{p}"))
                out, src = chunk(self.keys[l], it, p), mem.bank(l)[:, 0:CH * S].rearrange("p (b s) -> p b s", b=CH)
                if l == 0:
                    ins = act.activation(out, src, ACT.Identity, bias=mem.col("bk"))
                else:
                    ins = act.activation(out, src, ACT.Copy)
                ins.then_inc(a.sem, 1)
            for l in range(2):
                act.wait_ge(e.sem, e.done(it, f"v{l}{p}"))
                act.activation(chunk(self.values[l][0:S], it, p), mem.bank(2 + l)[0:S, :].rearrange("p (b c) -> p b c", b=CH),
                               ACT.Copy).then_inc(a.sem, 1)


SCORE_WORDS = 4 * W + 4 * H * S


def attention_block(nc, mem, ctx, layer, v_mask_in, tokens, split):
    def sem(n):
        return ctx.enter_context(nc.semaphore(f"at{layer}_{n}"))

    causal = layer == 0
    xl = mem.xl[:, :, :].rearrange("p b c -> p (b c)")
    mem.hn = xl[:, 0:1024].rearrange("p (q b c) -> p q b c", q=2, b=CH)
    q32 = xl[:, 1024:1024 + W]
    k_lo = xl[:, 1024 + W:1024 + W + B * S].rearrange("p (b s) -> p b s", b=B)
    q_hi, q_lo = (split[:, i * 2 * W:(i + 1) * 2 * W].rearrange("p (q w) -> p q w", q=2) for i in range(2))
    km_hi, km_lo = (split[:, (4 * W + i * 2 * H * S):(4 * W + (i + 1) * 2 * H * S)]
                    .rearrange("p (q h s) -> p q h s", q=2, h=H) for i in range(2))
    kv = [kv_views(mem.take(KEPT_WORDS)) if causal else None, kv_views(mem.kv1[:, :])]
    kT, vals = kv[layer]
    NB = 2 * CH
    vm = mem.take(2, 4, C)
    v_mask = mem.take(4, C)
    shifted = mem.take(2, H, S)
    mx = mem.take(2, H)
    prob = mem.take(2, H, S)
    pT = mem.take(4, 4 * T)
    k_hi = shifted.rearrange("p q h s -> p (q h s)").rearrange("p (b s) -> p b s", b=B)
    rden = mem.take(T)
    oT = mem.take(2, CH, T)
    bias = mem.take(C)
    bias_row = mem.take(C)
    causal_b = mem.take(4 * S // 2).bitcast(BF16)
    ident_b = mem.take(64).bitcast(BF16)
    context = Context(nc, mem, ctx, tokens, kv) if causal else None
    norm = Norm(nc, mem, ctx, f"at{layer}n", mem.x)
    masks = sem("masks")
    setup = sem("setup") if causal else None
    padded = sem("padded")
    bias_pe, bias_dve = sem("bias_pe"), sem("bias_dve")

    e = Steps(sem("pe_scores"), " ".join(f"S{n}a S{n}b" for n in range(NB)), 1)
    eq, aq = Steps(sem("pe_queries"), "q0 q1", 1), Steps(sem("act_queries"), "q0 hi0 q1 hi1", 1)
    d = Steps(sem("dve_scores"), " ".join(f"max{n}{h} sub{n}{h}" for n in range(NB) for h in "ab"), 1)
    dq = Steps(sem("dve_queries"), "q0 q1", 1)
    k_split = sem("k_split")
    a = Steps(sem("act_scores"), " ".join(f"exp{n}a exp{n}b" for n in range(NB)), 1)
    ef = Steps(sem("pe_out"), " ".join(f"T{n}0 T{n}1 T{n}2 T{n}3 O{n}"
                                       for n in range(NB)), 1)
    df = Steps(sem("dve_out"), " ".join(f"rec{n} o{n}" for n in range(NB)), 1)
    eo, do = Steps(sem("pe_project"), "out0 out1", 1), Steps(sem("dve_add"), "add0 add1", 1)
    af = Steps(sem("act_out"), " ".join(f"p{n}0 p{n}1 p{n}2 p{n}3" for n in range(NB)), 1)
    g = Steps(sem("pool"), " ".join(f"hi{n} km{n} vm{n}" for n in range(NB)), 1)
    gb = Steps(sem("pool_bias"), "bias0 bias1")
    bank = mem.bank
    scores = mem.ps[:, 0:4 * W].rearrange("p (g w) -> p g w", g=4)[:, :, 0:4 * S].rearrange("p g (j s) -> p g j s", j=4)

    def by_group(v):
        return v.rearrange("p (g j) s -> p g j s", g=2)

    HALF = {"a": 0, "b": 1}

    def n_of(steps, it, name, n, more=""):
        return steps.done(it, f"{name}{n}{more}") if n >= 0 else steps.done(it - 1, f"{name}{n + NB}{more}")

    with nc.Block() as block:
        @block.sync
        def _(sp):
            sp.dma_start(v_mask[:, :, :], v_mask_in).then_inc(masks, 16)
            if context:
                with sp.Fori(0, NIT) as it:
                    context.load_turn(sp, it)
            sp.wait_ge(masks, 16)

        @block.gpsimd
        def _(pool):
            pool.sem_inc(g.sem, g.credit())
            pool.memset(pT[64:128, :, :], 0.0).then_inc(padded, 1)
            pool.memset(vm[64:128, :, :, :], 0.0).then_inc(padded, 1)
            pool.wait_ge(padded, 2)
            pool.wait_ge(masks, 16)
            norm.pool_pass(pool)
            if context:
                pool.wait_ge(context.act.sem, context.act.done(NIT - 1, "v11"))
            pool.wait_ge(norm.dve.sem, norm.dve.done(NIT - 1, "scaled1"))
            pool.wait_ge(k_split, 2)
            pool.wait_ge(bias_dve, 2)
            with pool.Fori(0, NIT) as it:
                for n in range(NB):
                    p, b = n // CH, n % CH
                    at = (it * 2 + p) * CH + b
                    mask = mem.mat("head_mask", 0, H).unsqueeze(2).broadcast_to([128, H, S])
                    pool.wait_ge(e.sem, n_of(e, it, "S", n - 2, "b"))
                    pool.tensor_tensor(km_hi[:, n % 2], kT[:, bass.ds(at, 1), :].broadcast_to([128, H, S]),
                                       mask, ALU.mult).then_inc(g.sem, 1)
                    pool.tensor_tensor(km_lo[:, n % 2], k_lo[:, bass.ds(at, 1), :].broadcast_to([128, H, S]),
                                       mask, ALU.mult).then_inc(g.sem, 1)
                    pool.wait_ge(ef.sem, n_of(ef, it, "O", n - 2))
                    vc = vals[0:S, bass.ds(at, 1), :]
                    pool.tensor_tensor(vm[0:S, n % 2], vc.broadcast_to([S, 4, C]), v_mask[0:S], ALU.mult).then_inc(g.sem, 1)
                    if b == 1:
                        x = chunk(mem.x, it, p)
                        pool.tensor_tensor(x, x, bias.unsqueeze(1).broadcast_to([128, CH, C]), ALU.add).then_inc(gb.sem, 1)

        @block.vector
        def _(dve):
            for s in (d, dq, df, do):
                dve.sem_inc(s.sem, s.credit())
            if causal:
                dve.tensor_copy(causal_b.rearrange("p (j s) -> p j s", j=4),
                                mem.mat("causal", 0, S).unsqueeze(1).broadcast_to([128, 4, S])).then_inc(setup, 1)
                dve.tensor_copy(ident_b, mem.mat("ident")).then_inc(setup, 1)
            norm.vector_pass(dve)
            if causal:
                dve.wait_ge(bias_pe, 1)
                dve.tensor_tensor(bias_row[0:1, :], mem.row("bo0"), bank(5)[0:1, 0:C], ALU.add).then_inc(bias_dve, 1)
            else:
                dve.tensor_copy(bias_row[0:1, :], mem.row("bo1")).then_inc(bias_dve, 1)
            dve.wait_ge(bias_pe, 2)
            dve.tensor_copy(bias[:, :], bank(5)[:, C:2 * C]).then_inc(bias_dve, 1)

            dve.wait_ge(k_split, 1)
            dve.tensor_tensor(k_lo, kT, k_hi, ALU.subtract).then_inc(k_split, 1)
            dve.wait_ge(k_split, 2)

            def first(it, n):
                for h, i in HALF.items():
                    heads = slice(8 * i, 8 * i + 8)
                    dve.wait_ge(e.sem, e.done(it, f"S{n}{h}"))
                    dve.wait_ge(d.sem, n_of(d, it, "sub", n - 2, h))
                    dve.tensor_reduce(by_group(mx[:, n % 2, heads].unsqueeze(2))[:, :, :, 0], scores[:, 2 * i:2 * i + 2],
                                      AX.X, ALU.max).then_inc(d.sem, 1)
                    dve.wait_ge(d.sem, d.done(it, f"max{n}{h}"))
                    dve.wait_ge(a.sem, n_of(a, it, "exp", n - 2, h))
                    dve.tensor_tensor(by_group(shifted[:, n % 2, heads]), scores[:, 2 * i:2 * i + 2],
                                      by_group(mx[:, n % 2, heads].unsqueeze(2).broadcast_to([128, 8, S])),
                                      ALU.subtract).then_inc(d.sem, 1)

            def queries(it, q):
                dve.wait_ge(aq.sem, aq.done(it, f"hi{q}"))
                dve.wait_ge(e.sem, e.done(it - 1, f"S{CH * q + CH - 1}b"))
                dve.tensor_tensor(q_lo[:, q], q32, q_hi[:, q].bitcast(F32), ALU.subtract).then_inc(dq.sem, 1)

            def second_queries(it, n):
                if n == CH - 1:
                    queries(it, 1)

            def second(it, n):
                p = n // CH
                dve.wait_ge(ef.sem, ef.done(it, f"O{n}"))
                dve.wait_ge(df.sem, n_of(df, it, "o", n - 1))
                dve.reciprocal(rden[:, :], bank(7)[:, 0:T]).then_inc(df.sem, 1)
                dve.wait_ge(df.sem, df.done(it, f"rec{n}"))
                dve.wait_ge(eo.sem, eo.done(it - 1, f"out{p}"))
                dve.tensor_tensor(oT[:, p, n % CH], bank(6)[:, 0:T], rden[:, :], ALU.mult).then_inc(df.sem, 1)

            def add(it, n, final=False):
                if n % CH == CH - 1:
                    p = n // CH
                    x = chunk(mem.x, it, p)
                    dve.wait_ge(eo.sem, eo.done(it, f"out{p}"))
                    dve.wait_ge(gb.sem, gb.done(it, f"bias{p}"))
                    dve.tensor_tensor(x, x, bank(5)[:, :].rearrange("p (b c) -> p b c", b=CH), ALU.add).then_inc(do.sem, 1)
                    dve.wait_ge(do.sem, do.done(it, f"add{p}"))
                    take_stats(dve, mem, it, p)

            skewed(dve, NIT, NB, (1, first), ("turn", lambda it: queries(it, 0)), (1, second_queries), (-1, add), (0, second))

        @block.scalar
        def _(act):
            for s in (norm.act, a, aq, af) + ((context.act,) if context else ()):
                act.sem_inc(s.sem, s.credit())
            act.preload_act_table(ACT.Exp)
            with act.Fori(0, NIT) as it:
                if context:
                    context.scalar_turn(act, it)
                norm.scalar_turn(act, it)

            act.wait_ge(padded, 2)

            if context:
                act.wait_ge(context.act.sem, context.act.done(NIT - 1, "v11"))
            act.activation(k_hi.bitcast(F32R), kT, ACT.Copy).then_inc(k_split, 1)

            def queries(it, q):
                act.wait_ge(eq.sem, eq.done(it, f"q{q}"))
                act.wait_ge(dq.sem, dq.previous(it, q, "q"))
                if causal:
                    ins = act.activation(q32, bank(5)[:, :], ACT.Identity, bias=mem.col("bq"))
                else:
                    ins = act.activation(q32, bank(5)[:, :], ACT.Copy)
                ins.then_inc(aq.sem, 1)
                act.wait_ge(aq.sem, aq.done(it, f"q{q}"))
                act.wait_ge(e.sem, e.done(it - 1, f"S{CH * q + CH - 1}b"))
                act.activation(q_hi[:, q], q32, ACT.Copy).then_inc(aq.sem, 1)

            def second_queries(it, n):
                if n == CH - 1:
                    queries(it, 1)

            def exponentials(it, n):
                for h, i in HALF.items():
                    heads = slice(8 * i, 8 * i + 8)
                    act.wait_ge(d.sem, d.done(it, f"sub{n}{h}"))
                    act.wait_ge(ef.sem, n_of(ef, it, "T", n - 2, "3"))
                    act.activation(prob[:, n % 2, heads].rearrange("p h s -> p (h s)"),
                                   shifted[:, n % 2, heads].rearrange("p h s -> p (h s)"), ACT.Exp, scale=ATT_SCALE).then_inc(a.sem, 1)

            def copies(quarters):
                def stage(it, n):
                    for j in quarters:
                        act.wait_ge(ef.sem, ef.done(it, f"T{n}{j}"))
                        act.wait_ge(ef.sem, n_of(ef, it, "O", n - 1))
                        act.activation(pT[0:S, j], bank(4 + j % 2)[0:S, :], ACT.Copy).then_inc(af.sem, 1)
                return stage

            skewed(act, NIT, NB, (0, copies((0, 1))), ("turn", lambda it: queries(it, 0)), (1, second_queries),
                   (0, copies((2, 3))), (1, exponentials))

        @block.tensor
        def _(pe):
            for s in (norm.pe, e, eq, ef, eo) + ((context.pe,) if context else ()):
                pe.sem_inc(s.sem, s.credit())
            with pe.Fori(0, NIT) as it:
                if context:
                    context.tensor_turn(pe, it)
                norm.tensor_turn(pe, it)
            if context:
                pe.wait_ge(context.act.sem, context.act.done(NIT - 1, "v11"))
                pe.matmul(bank(5)[0:1, 0:C], mem.col("bv"), mem.mat("oT0"), start=True, stop=True).then_inc(bias_pe, 1)
            else:
                pe.sem_inc(bias_pe, 1)
            pe.wait_ge(bias_dve, 1)
            pe.matmul(bank(5)[:, C:2 * C], mem.ones[0:1, :], bias_row[0:1, :], start=True, stop=True).then_inc(bias_pe, 1)
            pe.wait_ge(bias_dve, 2)
            pe.wait_ge(norm.act.sem, norm.act.done(NIT - 1, "ready1"))
            if causal:
                pe.wait_ge(setup, 2)

            pe.wait_ge(padded, 2)
            pe.wait_ge(masks, 16)

            def queries(it, q, n):
                pe.wait_ge(af.sem, n_of(af, it, "p", n, "1"))
                pe.matmul(bank(5)[:, :].rearrange("p (b t) -> p b t", b=CH), mem.mat(f"qT{layer}"),
                          chunk(mem.hT, it, q)[:, :, 1:T + 1], start=True, stop=True).then_inc(eq.sem, 1)

            def first_queries(it):
                queries(it, 0, -2)

            def queries_copied(it):
                pe.wait_ge(aq.sem, aq.done(it, "q0"))

            def first(it, n):
                p, b = n // CH, n % CH
                pe.wait_ge(dq.sem, dq.done(it, f"q{p}"))
                pe.wait_ge(g.sem, g.done(it, f"km{n}"))
                lhs_hi, lhs_lo = (v[:, p, b * T:(b + 1) * T] for v in (q_hi, q_lo))
                for grp in range(4):
                    if grp % 2 == 0:
                        pe.wait_ge(d.sem, n_of(d, it, "sub", n - 1, "ab"[grp // 2]))
                    out = bank(grp)[:, 0:4 * S]
                    hi, lo = (v[:, n % 2, 4 * grp:4 * grp + 4].rearrange("p j s -> p (j s)") for v in (km_hi, km_lo))
                    pe.matmul(out, lhs_hi, lo, start=True, stop=False)
                    pe.matmul(out, lhs_lo, hi, start=False, stop=False)
                    last = pe.matmul(out, lhs_hi, hi, start=False, stop=not causal)
                    if causal:
                        last = pe.matmul(out, ident_b, causal_b, start=False, stop=True)
                    if grp % 2:
                        last.then_inc(e.sem, 1)
                if n == CH - 1:
                    queries(it, 1, n - 1)

            def turn(it, n, j):
                pe.wait_ge(af.sem, af.done(it, f"p{n}{j - 2}") if j >= 2 else n_of(af, it, "p", n - 1, f"{j + 2}"))
                for grp in range(4):
                    last = pe.transpose(bank(4 + j % 2)[0:S, grp * T:(grp + 1) * T], prob[:, n % 2, 4 * grp + j, :],
                                        mem.mat("ident"))
                last.then_inc(ef.sem, 1)

            def weigh(it, n, j):
                pe.wait_ge(af.sem, af.done(it, f"p{n}{j}"))
                for out, lhs in ((bank(6), vm[:, n % 2, j]), (bank(7), v_mask[:, j])):
                    for grp in range(4):
                        rows = slice(32 * grp, 32 * grp + 32)
                        last = pe.matmul(out[rows, 0:T], lhs[:, rows],
                                         pT[:, j, grp * T:(grp + 1) * T], start=(j == 0), stop=(j == 3))
                return last

            def early_turns(it, n):
                pe.wait_ge(a.sem, a.done(it, f"exp{n}b"))
                turn(it, n, 0)
                turn(it, n, 1)

            def third_turn(it, n):
                turn(it, n, 2)
                pe.wait_ge(g.sem, g.done(it, f"vm{n}"))
                pe.wait_ge(df.sem, n_of(df, it, "o", n - 1))
                weigh(it, n, 0)

            def second(it, n):
                if n == CH - 2:
                    pe.wait_ge(aq.sem, aq.done(it, "q1"))
                if n % CH == 0:
                    pe.wait_ge(do.sem, do.done(it, "add0") if n else do.done(it - 1, "add1"))
                turn(it, n, 3)
                weigh(it, n, 1)
                weigh(it, n, 2)
                weigh(it, n, 3).then_inc(ef.sem, 1)

            def project(it, n, final=False):
                if n % CH == CH - 1:
                    p = n // CH
                    pe.wait_ge(df.sem, df.done(it, f"o{n}"))
                    if final:
                        pe.wait_ge(af.sem, af.done(it, f"p{n}3"))
                    else:
                        pe.wait_ge(af.sem, af.done(it, f"p{n + 1}1") if p == 0 else af.done(it + 1, "p01"))
                    for j in range(CH):
                        last = pe.matmul(bank(5)[:, j * C:(j + 1) * C], oT[:, p, j], mem.mat(f"oT{layer}"),
                                         start=True, stop=True)
                    last.then_inc(eo.sem, 1)

            skewed(pe, NIT, NB, (0, early_turns), (1, first), ("turn", first_queries), (-1, project), (0, third_turn),
                   ("turn", queries_copied), (0, second))


ROUTED = 20
PIECE = 256
EXP_AFTER = 26
PIECES = E * HID // PIECE
SPLIT_WORDS = 4 * E * HID + 2 * 2 * 4 * W + 3 * W + E


def experts_block(nc, mem, ctx, w_fc, w_proj):
    with ExitStack() as ctx_in:
        experts(nc, mem, ctx, ctx_in, w_fc, w_proj)


def experts(nc, mem, ctx, ctx_in, w_fc, w_proj):
    def sem(n):
        return ctx.enter_context(nc.semaphore(f"moe_{n}"))

    split = ctx_in.enter_context(nc.sbuf_tensor("experts_split", [128, SPLIT_WORDS], F32R))
    ctx_in.enter_context(mem.block_memory("experts", ARENA - KEPT_WORDS - SPLIT_WORDS))
    at = [0]

    def part_of_split(*shape):
        n = int(np.prod(shape))
        at[0] += n
        v = split[:, at[0] - n:at[0]]
        names = "abcd"[:len(shape)]
        return v.rearrange(f"p ({' '.join(names)}) -> p {' '.join(names)}", **dict(zip(names[:-1], shape))) if len(shape) > 1 else v

    both = part_of_split(2, 2 * E * 4, 128)
    wf = both[:, :, 0:E * 4]
    wp = both[:, :, E * 4:2 * E * 4]
    hid_hi = part_of_split(2, 4, W)
    hid_lo = part_of_split(2, 4, W)
    h_hi = part_of_split(CH, T)
    h_lo = part_of_split(CH, T)
    cT = part_of_split(W)
    sel = part_of_split(E)
    assert at[0] == SPLIT_WORDS

    def f(v):
        return v.bitcast(F32)

    comb = mem.take(B, E)
    comb_hi = mem.take(B, E)
    cs = mem.take(CH, 128)
    xl = mem.xl[:, :, :].rearrange("p b c -> p (b c)")
    hid = xl.rearrange("p (q k w) -> p q k w", q=2, k=4)
    stage = [mem.take(PIECE)] + [xl[:, B * C - (i + 1) * PIECE:B * C - i * PIECE] for i in range(3)]
    NS = len(stage)
    mem.hn = xl[:, 0:1024].rearrange("p (q b c) -> p q b c", q=2, b=CH)
    lgT = xl[:, 1024:2048].rearrange("p (q w) -> p q w", q=2)
    lg, one1, one2, cand = (xl[:, 2048 + i * B * E:2048 + (i + 1) * B * E].rearrange("p (b e) -> p b e", b=B) for i in range(4))
    best = xl[:, 3072:3072 + 6 * B].rearrange("p (k b) -> p k b", k=6)

    norm = Norm(nc, mem, ctx, "moen", mem.x)
    loaded = [sem(f"loaded{i}") for i in range(NS)]
    split_hi, split_lo = sem("weights_hi"), sem("weights_lo")
    pieces = [src[:, i * PIECE:(i + 1) * PIECE] for src in (w_fc, w_proj) for i in range(PIECES)]
    hi_of_all, lo_of_all = (both[:, part].rearrange("p e h -> p (e h)") for part in range(2))
    route_pe, route_act = sem("route_pe"), sem("route_act")
    rd = sem("route_dve")
    top = sem("top")
    gap, zeroed = sem("gap"), sem("zeroed")
    wd = Steps(sem("comb_dve"), "hi lo", 1)
    we = Steps(sem("comb_pe"), "turned", 1)
    wa = Steps(sem("comb_act"), "cT h_hi", 1)
    wl = Steps(sem("comb_lo"), "h_lo", 1)
    ep = Steps(sem("hidden_pe"), " ".join(f"c{e} " + " ".join(f"f{e}{k}" for k in range(4)) for e in range(E)), 1)
    eo = Steps(sem("out_pe"), " ".join(f"y{e}" for e in range(E)), 1)
    ag = Steps(sem("gelu_act"), " ".join(f"g{e}{k}" for e in range(E) for k in range(4)), 1)
    ah = Steps(sem("hi_act"), " ".join(f"hi{e}{h}" for e in range(E) for h in range(2)), 1)
    ao = Steps(sem("out_act"), "out", 1)
    dw = Steps(sem("weigh_dve"), " ".join(f"w{e}0 w{e}1 lo{e}0 lo{e}1" for e in range(E)), 1)
    final_pe, final_dve = sem("final_pe"), sem("final_dve")
    bank = mem.bank

    def piece(n, part):
        return (hi_of_all, lo_of_all)[part][:, n * PIECE:(n + 1) * PIECE]

    def wide(v):
        return v.unsqueeze(2).broadcast_to([128, B, E])

    def two_back(steps, it, name, e, more=""):
        return steps.done(it, f"{name}{e - 2}{more}") if e > 1 else steps.done(it - 1, f"{name}{e + E - 2}{more}")

    with nc.Block() as block:
        @block.sync
        def _(sp):
            for n, src in enumerate(pieces):
                if n >= NS:
                    sp.wait_ge(split_lo, n - NS + 1)
                sp.dma_start(stage[n % NS], src).then_inc(loaded[n % NS], 16)

        @block.gpsimd
        def _(pool):
            pool.memset(cs[:, :, :], 0.0).then_inc(zeroed, 1)
            pool.tensor_tensor(sel, mem.mat("ident")[:, 0:E], mem.mat("ident")[:, 32:32 + E], ALU.add).then_inc(zeroed, 1)
            norm.pool_pass(pool)
            for n in range(len(pieces)):
                pool.wait_ge(loaded[n % NS], n // NS * 16 + 16)
                pool.wait_ge(split_hi, n + 1)
                pool.tensor_tensor(piece(n, 1), stage[n % NS], f(piece(n, 0)), ALU.subtract).then_inc(split_lo, 1)

        @block.vector
        def _(dve):
            for s in (wd, wl, dw):
                dve.sem_inc(s.sem, s.credit())
            norm.vector_pass(dve)
            for q in range(2):
                dve.wait_ge(route_pe, 2 + q + 1)
                dve.tensor_copy(lg[:, q * 16:(q + 1) * 16].rearrange("p (i j) e -> p j i e", j=CH),
                                bank(2 + q).rearrange("p (j i w) -> p j i w", j=CH, w=32)[:, :, :, 0:E]).then_inc(rd, 1)
            rank = mem.mat("rank", 0, E).unsqueeze(1).broadcast_to([128, B, E])
            dve.wait_ge(rd, 2)
            n = 0
            for k, one in enumerate((one1, one2)):
                src = lg if k == 0 else cand
                dve.tensor_reduce(best[:, 3 * k, :], src[:, :, :], AX.X, ALU.max).then_inc(top, 1)
                n += 1
                dve.wait_ge(top, n)
                dve.tensor_tensor(one, src, wide(best[:, 3 * k, :]), ALU.is_equal).then_inc(top, 1)
                n += 1
                dve.wait_ge(top, n)
                dve.tensor_tensor(one, one, rank, ALU.mult).then_inc(top, 1)
                n += 1
                dve.wait_ge(top, n)
                dve.tensor_reduce(best[:, 3 * k + 1, :], one[:, :, :], AX.X, ALU.max).then_inc(top, 1)
                n += 1
                dve.wait_ge(top, n)
                dve.tensor_tensor(one, rank, wide(best[:, 3 * k + 1, :]), ALU.is_equal).then_inc(top, 1)
                n += 1
                dve.wait_ge(top, n)
                if k == 0:
                    dve.scalar_tensor_tensor(cand, one, -1e30, lg, ALU.mult, ALU.add).then_inc(top, 1)
                    n += 1
                    dve.wait_ge(top, n)
            dve.tensor_tensor(best[:, 2, :], best[:, 3, :], best[:, 0, :], ALU.subtract).then_inc(top, 1)
            n += 1
            dve.wait_ge(gap, 1)
            dve.tensor_scalar(best[:, 4, :], best[:, 5, :], 1.0, None, ALU.add).then_inc(top, 1)
            n += 1
            dve.wait_ge(top, n)
            dve.reciprocal(best[:, 1, :], best[:, 4, :]).then_inc(top, 1)
            n += 1
            dve.wait_ge(top, n)
            dve.tensor_tensor(best[:, 2, :], best[:, 5, :], best[:, 1, :], ALU.mult).then_inc(top, 1)
            dve.tensor_tensor(one1, one1, wide(best[:, 1, :]), ALU.mult).then_inc(top, 1)
            n += 2
            dve.wait_ge(top, n)
            dve.tensor_tensor(one2, one2, wide(best[:, 2, :]), ALU.mult).then_inc(top, 1)
            n += 1
            dve.wait_ge(top, n)
            dve.tensor_tensor(comb, one1, one2, ALU.add).then_inc(top, 1)
            n += 1
            dve.wait_ge(top, n)
            dve.tensor_copy(comb_hi.bitcast(F32R), comb).then_inc(top, 1)
            n += 1
            dve.wait_ge(top, n)
            dve.tensor_tensor(comb, comb, comb_hi, ALU.subtract).then_inc(top, 1)
            n += 1
            assert n == ROUTED
            dve.wait_ge(top, n)
            dve.wait_ge(zeroed, 2)

            def columns(it):
                dve.wait_ge(we.sem, we.done(it - 1, "turned"))
                dve.tensor_copy(cs[:, :, 0:E], comb_hi[:, bass.ds(it * CH, CH), :]).then_inc(wd.sem, 1)
                dve.tensor_copy(cs[:, :, 32:32 + E], comb[:, bass.ds(it * CH, CH), :]).then_inc(wd.sem, 1)

            def weigh(it, e):
                for h in range(2):
                    g = hid[:, e % 2, 2 * h:2 * h + 2]
                    dve.wait_ge(ep.sem, ep.done(it, f"c{e}"))
                    dve.wait_ge(ag.sem, ag.done(it, f"g{e}{2 * h + 1}"))
                    dve.tensor_tensor(g, g, bank(4 + e % 2).unsqueeze(1).broadcast_to([128, 2, W]), ALU.mult).then_inc(dw.sem, 1)

            def h_low(it):
                dve.wait_ge(wa.sem, wa.done(it, "h_hi"))
                dve.wait_ge(ep.sem, ep.done(it - 1, f"f{E - 1}3"))
                dve.tensor_tensor(h_lo, mem.hT[:, bass.ds(it * CH, CH), 1:T + 1], f(h_hi), ALU.subtract).then_inc(wl.sem, 1)

            def lows(it, e):
                for h in range(2):
                    g = hid[:, e % 2, 2 * h:2 * h + 2]
                    dve.wait_ge(ah.sem, ah.done(it, f"hi{e}{h}"))
                    dve.tensor_tensor(hid_lo[:, e % 2, 2 * h:2 * h + 2], g, f(hid_hi[:, e % 2, 2 * h:2 * h + 2]), ALU.subtract).then_inc(dw.sem, 1)

            skewed(dve, NCH, E, ("turn", columns), (1, weigh), ("turn", h_low), (1, lows))
            for c in range(NCH):
                x = mem.x[:, c * CH:(c + 1) * CH, :]
                dve.wait_ge(final_pe, c + 1)
                dve.tensor_tensor(x, x, bank(c % 2).rearrange("p (b c) -> p b c", b=CH), ALU.add).then_inc(final_dve, 1)

        @block.scalar
        def _(act):
            for s in (norm.act, wa, ag, ah, ao):
                act.sem_inc(s.sem, s.credit())
            def split_piece(n):
                act.wait_ge(loaded[n % NS], n // NS * 16 + 16)
                act.activation(piece(n, 0), stage[n % NS], ACT.Copy).then_inc(split_hi, 1)

            for n in range(NS):
                split_piece(n)
            with act.Fori(0, NIT) as it:
                norm.scalar_turn(act, it)
                for i in range(NS):
                    act.wait_ge(loaded[i], it * 16 + 32)
                    act.activation(hi_of_all[:, bass.ds((it * NS + NS + i) * PIECE, PIECE)], stage[i], ACT.Copy).then_inc(split_hi, 1)
            for q in range(2):
                act.wait_ge(route_pe, q + 1)
                act.activation(lgT[:, q], bank(q), ACT.Copy).then_inc(route_act, 1)
            for n in range(NS + NIT * NS, len(pieces)):
                split_piece(n)
                if n == EXP_AFTER:
                    act.wait_ge(top, 12)
                    act.activation(best[:, 5, :], best[:, 2, :], ACT.Exp).then_inc(gap, 1)
            act.preload_act_table(ACT.Gelu_apprx_tanh)
            act.wait_ge(top, ROUTED)

            def turned(it):
                act.wait_ge(we.sem, we.done(it, "turned"))
                act.wait_ge(ep.sem, ep.done(it - 1, f"c{E - 1}"))
                act.activation(cT, bank(7), ACT.Copy).then_inc(wa.sem, 1)
                act.wait_ge(ep.sem, ep.done(it - 1, f"f{E - 1}3"))
                act.activation(h_hi, mem.hT[:, bass.ds(it * CH, CH), 1:T + 1], ACT.Copy).then_inc(wa.sem, 1)

            def gelus(it, e):
                act.wait_ge(eo.sem, two_back(eo, it, "y", e))
                for k in range(4):
                    act.wait_ge(ep.sem, ep.done(it, f"f{e}{k}"))
                    act.activation(hid[:, e % 2, k], bank(k), ACT.Gelu_apprx_tanh, bias=mem.col("b_fc", e * 4 + k)).then_inc(ag.sem, 1)

            def highs(it, e):
                for h in range(2):
                    act.wait_ge(dw.sem, dw.done(it, f"w{e}{h}"))
                    act.activation(hid_hi[:, e % 2, 2 * h:2 * h + 2], hid[:, e % 2, 2 * h:2 * h + 2], ACT.Copy).then_inc(ah.sem, 1)

            def output(it, e):
                if e == E - 1:
                    act.wait_ge(eo.sem, eo.done(it, f"y{e}"))
                    act.activation(mem.hT[:, bass.ds(it * CH, CH), 1:T + 1], bank(6).rearrange("p (b t) -> p b t", b=CH),
                                   ACT.Copy).then_inc(ao.sem, 1)

            skewed(act, NCH, E, (1, gelus), ("turn", turned), (1, highs), (0, output))

        @block.tensor
        def _(pe):
            for s in (norm.pe, we, ep, eo):
                pe.sem_inc(s.sem, s.credit())
            with pe.Fori(0, NIT) as it:
                norm.tensor_turn(pe, it)
            for q in range(2):
                pe.wait_ge(norm.act.sem, norm.act.done(2 * q + 1, "ready1"))
                for i in range(4):
                    at = (4 * q + i) * CH
                    last = pe.matmul(bank(q)[32 * i:32 * i + 32, :].rearrange("p (b t) -> p b t", b=CH), mem.mat("router", 0, 32),
                                     mem.hT[:, at:at + CH, 1:T + 1], start=True, stop=True)
                last.then_inc(route_pe, 1)
            for q in range(2):
                pe.wait_ge(route_act, q + 1)
                for j in range(CH):
                    last = pe.transpose(bank(2 + q)[:, j * 128:(j + 1) * 128], lgT[:, q, j * T:(j + 1) * T], mem.mat("ident"))
                last.then_inc(route_pe, 1)
            pe.wait_ge(rd, 2)
            pe.wait_ge(split_lo, len(pieces))
            pe.wait_ge(top, ROUTED)

            def product(out, w_hi, w_lo, x_hi, x_lo, start=True, stop=True):
                pe.matmul(out, w_hi, x_lo, start=start, stop=False)
                pe.matmul(out, w_lo, x_hi, start=False, stop=False)
                return pe.matmul(out, w_hi, x_hi, start=False, stop=stop)

            def turn(it):
                pe.wait_ge(wd.sem, wd.done(it, "lo"))
                pe.wait_ge(wa.sem, wa.done(it - 1, "cT"))
                for j in range(CH):
                    last = pe.transpose(bank(7)[:, j * T:(j + 1) * T], cs[:, j, :], mem.mat("ident"))
                last.then_inc(we.sem, 1)

            def hidden(it, e):
                pe.wait_ge(wa.sem, wa.done(it, "cT"))
                pe.wait_ge(wl.sem, wl.done(it, "h_lo"))
                pe.wait_ge(dw.sem, two_back(dw, it, "w", e, "1"))
                pe.matmul(bank(4 + e % 2), sel[:, e:e + 1].broadcast_to([128, 128]), cT, start=True, stop=True).then_inc(ep.sem, 1)
                for k in range(4):
                    pe.wait_ge(ag.sem, ag.done(it, f"g{e - 1}{k}") if e else ag.done(it - 1, f"g{E - 1}{k}"))
                    product(bank(k), wf[:, 0, e * 4 + k], wf[:, 1, e * 4 + k],
                            h_hi.rearrange("p b t -> p (b t)"), h_lo.rearrange("p b t -> p (b t)")).then_inc(ep.sem, 1)

            def output(it, e):
                if e == 0:
                    pe.wait_ge(ao.sem, ao.done(it - 1, "out"))
                    pe.matmul(bank(6), mem.b_proj[:, :], f(cT), start=True, stop=False)
                pe.wait_ge(dw.sem, dw.done(it, f"lo{e}1"))
                for k in range(4):
                    last = product(bank(6), wp[:, 0, e * 4 + k], wp[:, 1, e * 4 + k],
                                   hid_hi[:, e % 2, k], hid_lo[:, e % 2, k], start=False, stop=(e == E - 1 and k == 3))
                last.then_inc(eo.sem, 1)

            skewed(pe, NCH, E, (1, hidden), ("turn", turn), (0, output))
            for c in range(NCH):
                pe.wait_ge(ao.sem, ao.done(c, "out"))
                if c >= 2:
                    pe.wait_ge(final_dve, c - 1)
                for j in range(CH):
                    last = pe.transpose(bank(c % 2)[:, j * C:(j + 1) * C], mem.hT[:, c * CH + j, 1:T + 1], mem.mat("ident"))
                last.then_inc(final_pe, 1)


def state_space_block(nc, mem, ctx):
    def sem(n):
        return ctx.enter_context(nc.semaphore(f"ssm_{n}"))

    mem.hn = mem.take(2, CH, C)
    mark = mem.at
    xp = mem.take(B, T + 2)
    gt = mem.take(B, T)
    mix = mem.take(B, T)
    dz = mem.take(B, T)
    bm = mem.take(B, T)
    ct = mem.take(B, T)
    neg_a = mem.take(2)
    tb = mem.take(2, CH, T)
    state = tb
    bias = mem.take(2, C)
    mem.at = mark
    soft = mem.take(2, 2, CH, T)
    decay = mem.take(2, CH, T)
    u = mem.take(2, CH, T)
    yT = mem.hn[:, :, :, :].rearrange("p a b c -> p a (b c)")
    mem.at = mark
    act1 = mem.take(2, 2, W)
    n4 = Norm(nc, mem, ctx, "ssmn", mem.x, double=True, affine=("m_ln1_g", "m_ln1_b"))
    n5 = Norm(nc, mem, ctx, "ffn", mem.xl, affine=("m_ln2_g", "m_ln2_b"))
    padded, a_made = sem("padded"), sem("a_made")
    ie = Steps(sem("in_pe"), "x0 g0 x1 g1", 1)
    ia = Steps(sem("in_act"), "x0 g0 x1 g1", 1)
    cd = Steps(sem("conv_dve"), "a0 b0 c0 a1 b1 c1")
    ce = Steps(sem("conv_pe"), "dt0 b0 c0 dt1 b1 c1", 1)
    ca = Steps(sem("conv_act"), "dt0 b0 c0 dt1 b1 c1", 1)
    cg = Steps(sem("conv_pool"), "bm0 bm1", 1)
    sa = Steps(sem("scan_act"), "abs0 abs1 exp0 exp1 ln0 ln1 decay0 decay1", 1)
    sd = Steps(sem("scan_dve"), "dt0 dt1 start0 start1 state0 state1 cs0 cs1 skip0 skip1 y0 y1", 1)
    so = Steps(sem("scan_add"), "add0 add1")
    sg = Steps(sem("scan_pool"), "u0 u1", 1)
    bias_pe, bias_act, bias_pool = sem("bias_pe"), sem("bias_act"), sem("bias_pool")
    se = Steps(sem("scan_pe"), "out0 out1", 1)
    fe = Steps(sem("ff_pe"), "h00 h01 h10 h11 out0 out1", 1)
    fa = Steps(sem("ff_act"), "g00 g01 g10 g11", 1)
    fd = Steps(sem("ff_dve"), "res0 res1 add0 add1", 1)
    bank = mem.bank

    def bt(v):
        return v.rearrange("p (b t) -> p b t", b=CH)

    def flat(v):
        return v.rearrange("p b t -> p (b t)")

    with nc.Block() as block:
        @block.gpsimd
        def _(pool):
            pool.sem_inc(cg.sem, cg.credit())
            pool.sem_inc(sg.sem, sg.credit())
            pool.memset(xp[:, :, 0:1], 0.0).then_inc(padded, 1)
            pool.memset(xp[:, :, T + 1:T + 2], 0.0).then_inc(padded, 1)
            n4.pool_pass(pool)
            pool.wait_ge(n4.dve.sem, n4.dve.done(NIT - 1, "scaled1"))
            pool.wait_ge(bias_act, 1)
            pool.tensor_tensor(mem.xl[:, :, :], mem.xl[:, :, :], bias[:, 0:1, :].broadcast_to([128, B, C]), ALU.add).then_inc(bias_pool, 1)
            with pool.Fori(0, NIT) as it:
                for p in range(2):
                    pool.wait_ge(ca.sem, ca.done(it, f"b{p}"))
                    pool.tensor_tensor(chunk(bm, it, p), tb[:, p], chunk(mix, it, p), ALU.mult).then_inc(cg.sem, 1)
            with pool.Fori(0, NIT) as it:
                for p in range(2):
                    pool.wait_ge(sd.sem, sd.done(it, f"dt{p}"))
                    pool.wait_ge(sd.sem, sd.done(it - 1, f"state{p}"))
                    pool.tensor_tensor(u[:, p], soft[:, p, 0], chunk(bm, it, p), ALU.mult).then_inc(sg.sem, 1)
                for p in range(2):
                    x = chunk(mem.x, it, p)
                    pool.tensor_tensor(x, x, bias[:, 1:2, :].broadcast_to([128, CH, C]), ALU.add).then_inc(bias_pool, 1)
            n5.pool_pass(pool)

        @block.vector
        def _(dve):
            for s in (sd, fd):
                dve.sem_inc(s.sem, s.credit())
            dve.wait_ge(a_made, 1)
            dve.tensor_scalar(neg_a[:, 1:2], neg_a[:, 0:1], -1.0, None, ALU.mult).then_inc(a_made, 1)
            n4.vector_pass(dve)
            with dve.Fori(0, NIT) as it:
                for p in range(2):
                    m = chunk(mix, it, p)
                    dve.wait_ge(ia.sem, ia.done(it, f"x{p}"))
                    dve.tensor_scalar(m, chunk(xp, it, p)[:, :, 1:T + 1], mem.col("dw1"), mem.col("dw_b"), ALU.mult, ALU.add).then_inc(cd.sem, 1)
                    dve.wait_ge(cd.sem, cd.done(it, f"a{p}"))
                    dve.scalar_tensor_tensor(m, chunk(xp, it, p)[:, :, 0:T], mem.col("dw0"), m, ALU.mult, ALU.add).then_inc(cd.sem, 1)
                    dve.wait_ge(cd.sem, cd.done(it, f"b{p}"))
                    dve.scalar_tensor_tensor(m, chunk(xp, it, p)[:, :, 2:T + 2], mem.col("dw2"), m, ALU.mult, ALU.add).then_inc(cd.sem, 1)
            with dve.Fori(0, NIT) as it:
                def after(name):
                    dve.wait_ge(sd.sem, sd.done(it, name))

                for p in range(2):
                    dve.wait_ge(sa.sem, sa.done(it, f"ln{p}"))
                    dve.scalar_tensor_tensor(soft[:, p, 0], chunk(dz, it, p), 0.0, soft[:, p, 1], ALU.max, ALU.add).then_inc(sd.sem, 1)
                for p in range(2):
                    dve.wait_ge(sa.sem, sa.done(it, f"decay{p}"))
                    dve.memset(decay[:, p, :, 0:1], 0.0).then_inc(sd.sem, 1)
                for p in range(2):
                    after(f"start{p}")
                    dve.wait_ge(sg.sem, sg.done(it, f"u{p}"))
                    dve.tensor_tensor_scan(flat(state[:, p]), flat(decay[:, p]), flat(u[:, p]), 0.0, ALU.mult, ALU.add).then_inc(sd.sem, 1)
                for p in range(2):
                    after(f"state{p}")
                    dve.tensor_tensor(state[:, p], state[:, p], chunk(ct, it, p), ALU.mult).then_inc(sd.sem, 1)
                for p in range(2):
                    after(f"cs{p}")
                    dve.scalar_tensor_tensor(state[:, p], chunk(mix, it, p), mem.col("d_skip"), state[:, p], ALU.mult, ALU.add).then_inc(sd.sem, 1)
                for p in range(2):
                    after(f"skip{p}")
                    dve.wait_ge(se.sem, se.done(it - 1, f"out{p}"))
                    dve.tensor_tensor(bt(yT[:, p]), state[:, p], chunk(gt, it, p), ALU.mult).then_inc(sd.sem, 1)
            dve.wait_ge(bias_pool, 1 + NCH)
            with dve.Fori(0, NIT) as it:
                for p in range(2):
                    xl = chunk(mem.xl, it, p)
                    dve.wait_ge(se.sem, se.done(it, f"out{p}"))
                    dve.tensor_tensor(xl, xl, bt(mem.ps[:, bass.ds((it * 2 + p) * W, W)]), ALU.add).then_inc(so.sem, 1)
            dve.wait_ge(so.sem, so.done(NIT - 1, "add1"))
            n5.vector_begin(dve)

            def add(it, n):
                for p in range(2):
                    x = chunk(mem.x, it, p)
                    dve.tensor_tensor(x, x, chunk(mem.xl, it, p), ALU.add).then_inc(fd.sem, 1)
                for p in range(2):
                    x = chunk(mem.x, it, p)
                    dve.wait_ge(fd.sem, fd.done(it, f"res{p}"))
                    dve.wait_ge(fe.sem, fe.done(it, f"out{p}"))
                    dve.tensor_tensor(x, x, bt(bank(4 + p)), ALU.add).then_inc(fd.sem, 1)

            skewed(dve, NIT, 1, (1, lambda it, n: n5.vector_scale(dve, it)), (0, add))

        @block.scalar
        def _(act):
            for s in (n4.act, n5.act, ia, ca, sa, fa):
                act.sem_inc(s.sem, s.credit())
            act.activation(neg_a[:, 0:1], mem.col("a_log"), ACT.Exp).then_inc(a_made, 1)
            act.wait_ge(bias_pe, 1)
            act.activation(bias, bank(5)[:, 0:2 * C].rearrange("p (k c) -> p k c", k=2), ACT.Copy).then_inc(bias_act, 1)
            act.preload_act_table(ACT.Sigmoid)
            act.wait_ge(padded, 2)
            with act.Fori(0, NIT) as it:
                n4.scalar_turn(act, it)
                for p in range(2):
                    act.wait_ge(ie.sem, ie.done(it, f"x{p}"))
                    act.activation(chunk(xp, it, p)[:, :, 1:T + 1], bt(bank(p)), ACT.Identity, bias=mem.col("in_b0")).then_inc(ia.sem, 1)
                    act.wait_ge(ie.sem, ie.done(it, f"g{p}"))
                    act.activation(chunk(gt, it, p), bt(bank(2 + p)), ACT.Sigmoid, bias=mem.col("in_b1")).then_inc(ia.sem, 1)
            with act.Fori(0, NIT) as it:
                for p in range(2):
                    act.wait_ge(ce.sem, ce.done(it, f"dt{p}"))
                    act.activation(chunk(dz, it, p), bt(bank(4)), ACT.Identity, bias=mem.col("dt_b")).then_inc(ca.sem, 1)
                    act.wait_ge(ce.sem, ce.done(it, f"b{p}"))
                    act.wait_ge(cg.sem, cg.done(it - 1, f"bm{p}"))
                    act.activation(tb[:, p], bt(bank(5)), ACT.Tanh, bias=mem.col("b_b")).then_inc(ca.sem, 1)
                    act.wait_ge(ce.sem, ce.done(it, f"c{p}"))
                    act.activation(chunk(ct, it, p), bt(bank(6 + p)), ACT.Tanh, bias=mem.col("c_b")).then_inc(ca.sem, 1)
            act.wait_ge(ca.sem, ca.done(NIT - 1, "c1"))
            act.wait_ge(cd.sem, cd.done(NIT - 1, "c1"))
            act.wait_ge(cg.sem, cg.done(NIT - 1, "bm1"))
            act.wait_ge(a_made, 2)
            act.preload_act_table_set("natural_log_exp_and_others")
            with act.Fori(0, NIT) as it:
                for p in range(2):
                    act.wait_ge(sg.sem, sg.done(it - 1, f"u{p}"))
                    act.wait_ge(sa.sem, sa.done(it - 1, f"decay{p}"))
                    act.activation(soft[:, p, 0], chunk(dz, it, p), ACT.Abs).then_inc(sa.sem, 1)
                for p in range(2):
                    act.wait_ge(sa.sem, sa.done(it, f"abs{p}"))
                    act.activation(soft[:, p, 1], soft[:, p, 0], ACT.Exp, scale=-1.0).then_inc(sa.sem, 1)
                for p in range(2):
                    act.wait_ge(sa.sem, sa.done(it, f"exp{p}"))
                    act.activation(soft[:, p, 1], soft[:, p, 1], ACT.Ln, bias=1.0).then_inc(sa.sem, 1)
                for p in range(2):
                    act.wait_ge(sd.sem, sd.done(it, f"dt{p}"))
                    act.wait_ge(sd.sem, sd.done(it - 1, f"state{p}"))
                    act.activation(decay[:, p], soft[:, p, 0], ACT.Exp, scale=neg_a[:, 1:2]).then_inc(sa.sem, 1)
            act.preload_act_table(ACT.Gelu)

            def gelus(it, n):
                for p in range(2):
                    for k in range(2):
                        act.wait_ge(fe.sem, fe.done(it, f"h{p}{k}"))
                        if k == 0:
                            act.wait_ge(fe.sem, fe.done(it - 1, f"out{p}"))
                        act.activation(act1[:, p, k], bank(2 * p + k), ACT.Gelu, bias=mem.col(f"f1_b{k}")).then_inc(fa.sem, 1)

            skewed(act, NIT, 1, (1, lambda it, n: n5.scalar_turn(act, it)), (0, gelus))

        @block.tensor
        def _(pe):
            for s in (n4.pe, n5.pe, ie, ce, se, fe):
                pe.sem_inc(s.sem, s.credit())
            for k, name in enumerate(("m_out_b", "f2_b")):
                last = pe.matmul(bank(5)[:, k * C:(k + 1) * C], mem.ones[0:1, :], mem.row(name), start=True, stop=True)
            last.then_inc(bias_pe, 1)
            with pe.Fori(0, NIT) as it:
                n4.tensor_turn(pe, it)
                for p in range(2):
                    h = chunk(mem.hT, it, p)[:, :, 1:T + 1]
                    pe.wait_ge(n4.act.sem, n4.act.done(it, f"ready{p}"))
                    for k, name in enumerate("xg"):
                        pe.wait_ge(ia.sem, ia.done(it - 1, f"{name}{p}"))
                        pe.matmul(bt(bank(2 * k + p)), mem.mat("in_W", k), h, start=True, stop=True).then_inc(ie.sem, 1)
            pe.wait_ge(bias_act, 1)
            with pe.Fori(0, NIT) as it:
                for p in range(2):
                    m = chunk(mix, it, p)
                    pe.wait_ge(cd.sem, cd.done(it, f"c{p}"))
                    for name, i in (("dt", 4), ("b", 5), ("c", 6 + p)):
                        pe.wait_ge(ca.sem, ca.done(it - 1, f"c{p}") if name == "c" else ca.previous(it, p, name))
                        pe.matmul(bt(bank(i)), mem.mat(f"{name}_W"), m, start=True, stop=True).then_inc(ce.sem, 1)
            with pe.Fori(0, NIT) as it:
                for p in range(2):
                    pe.wait_ge(sd.sem, sd.done(it, f"y{p}"))
                    for j in range(CH):
                        out = mem.ps[:, bass.ds((it * 2 + p) * W + j * C, C)]
                        last = pe.matmul(out, yT[:, p, j * T:(j + 1) * T], mem.mat("out_W"), start=True, stop=True)
                    last.then_inc(se.sem, 1)
            pe.wait_ge(so.sem, so.done(NIT - 1, "add1"))

            def feed_forward(it, n):
                for p in range(2):
                    h = chunk(mem.hT, it, p)[:, :, 1:T + 1]
                    pe.wait_ge(n5.act.sem, n5.act.done(it, f"ready{p}"))
                    for k in range(2):
                        pe.wait_ge(fa.sem, fa.done(it - 1, f"g{p}{k}"))
                        pe.matmul(bt(bank(2 * p + k)), mem.mat("f1_W", k), h, start=True, stop=True).then_inc(fe.sem, 1)
                for p in range(2):
                    pe.wait_ge(fa.sem, fa.done(it, f"g{p}1"))
                    pe.wait_ge(fd.sem, fd.done(it - 1, f"add{p}"))
                    for j in range(CH):
                        out = bank(4 + p)[:, j * C:(j + 1) * C]
                        for k in range(2):
                            last = pe.matmul(out, act1[:, p, k, j * T:(j + 1) * T], mem.mat("f2_W", k), start=(k == 0), stop=(k == 1))
                    last.then_inc(fe.sem, 1)

            skewed(pe, NIT, 1, (1, lambda it, n: n5.tensor_turn(pe, it)), (0, feed_forward))


MAGIC = 12582912.0
Q16 = 32767.0
NG = 12
GW = 3 * B * T // NG
HALVES = [[(0, "u", 0), (0, "g", 1), (1, "u", 0)], [(1, "g", 1), (2, "u", 0), (2, "g", 1)]]


def quantised_ffn_block(nc, mem, ctx, out):
    def sem(n):
        return ctx.enter_context(nc.semaphore(f"q_{n}"))

    up = mem.take(3, B * T)
    gate = mem.take(3, B * T)
    wT = mem.take(3, 3 * C)
    qx = mem.take(2, CH, C)
    qxT = mem.take(2, W)
    top = mem.at
    mem.at = 0
    wq = mem.take(36, 32)
    ws = mem.take(3, 36)
    mem.at = top
    amax = mem.take(16)
    amax_u = mem.take(16)
    glob = mem.take(16)
    row = mem.take(128)
    t1 = mem.take(2, GW)
    t2 = mem.take(2, GW)
    consts = mem.take(2)
    n = Norm(nc, mem, ctx, "qn", mem.x, whole=True)
    wd = sem("weights_dve")
    we = Steps(sem("weights_pe"), "0 1 2")
    wa = Steps(sem("weights_act"), "0 1 2")
    gd, ge = sem("max_dve"), sem("max_pe")
    px = Steps(sem("quant_dve"), "q0 q1", 1)
    pt = Steps(sem("quant_act"), "t0 xT0 t1 xT1", 1)
    pq = Steps(sem("quant_pe"), "turned0 turned1", 1)
    names = " ".join(f"u{p}{k} g{p}{k}" for p in range(2) for k in range(3))
    pd, pe_, pa = (Steps(sem(f"proj_{n}"), names, 1) for n in ("dve", "pe", "act"))
    sa = Steps(sem("sig_act"), "sig0 sig1 u0 u1", 1)
    sd = Steps(sem("sig_dve"), "v0 v1 g0 g1 m0 m1", 1)
    rounded_pool, gate_int, up_int = sem("rounded_pool"), sem("gate_int"), sem("up_int")
    oa = Steps(sem("prod_act"), "t0 t1", 1)
    od = Steps(sem("prod_dve"), "o0 o1 m0 m1", 1)
    da = Steps(sem("down_act"), "t0 t1", 1)
    dd = Steps(sem("down_dve"), "i0 i1", 1)
    dx = Steps(sem("down_add"), "add0 add1", 1)
    de = Steps(sem("down_pe"), "out0 out1", 1)
    magic_set = sem("magic")
    stored = sem("stored")
    bank = mem.bank
    used = [0]
    gflat, uflat = gate.rearrange("p k t -> p (k t)"), up.rearrange("p k t -> p (k t)")
    qt = t1[:, :, 0:W].rearrange("p q (b c) -> p q b c", b=CH)
    pmax = t2[:, 0, 0:2 * 3 * NCH].rearrange("p (n c k) -> p n c k", n=2, k=3)
    prod = uflat[:, 0:2 * 3 * W].rearrange("p (q k t) -> p q k t", q=2, k=3)
    rounded = uflat[:, 2 * 3 * W:4 * 3 * W].rearrange("p (q k t) -> p q k t", q=2, k=3)

    def piece(v, it, p):
        return v[:, bass.ds((it * 2 + p) * GW, GW)]

    def bt(v):
        return v.rearrange("p (b t) -> p b t", b=CH)

    X, U, G, G2, O = range(5)

    def scale(i):
        return glob[:, 2 * i:2 * i + 1]

    def inverse(i):
        return glob[:, 2 * i + 1:2 * i + 2]

    def find_scale_vector(dve, i, src, unit=None):
        def step(ins):
            used[0] += 1
            ins.then_inc(gd, 1)
            dve.wait_ge(gd, used[0])

        step(dve.tensor_reduce(row[:, 0:1], src, AX.X, ALU.max))
        dve.wait_ge(ge, 2 * i + 1)
        step(dve.tensor_reduce(row[0:1, 1:2], bank(7)[0:1, 0:128], AX.X, ALU.max))
        dve.wait_ge(ge, 2 * i + 2)
        step(dve.tensor_scalar(row[:, 2:3], bank(7)[:, 128:129], 1.0 / Q16, 1.0 if unit is None else unit, ALU.mult, ALU.mult))
        step(dve.tensor_scalar(scale(i), row[:, 2:3], 1e-12, None, ALU.max))
        step(dve.reciprocal(inverse(i), scale(i)))
        if unit is None:
            step(dve.tensor_copy(row[:, 3:4], row[:, 2:3]))
        else:
            step(dve.tensor_tensor(inverse(i), inverse(i), unit, ALU.mult))

    def find_scale_tensor(pe, i):
        pe.wait_ge(gd, 6 * i + 1)
        pe.transpose(bank(7)[0:1, 0:128], row[:, 0:1], mem.mat("ident")).then_inc(ge, 1)
        pe.wait_ge(gd, 6 * i + 2)
        pe.matmul(bank(7)[:, 128:129], mem.ones[0:1, :], row[0:1, 1:2], start=True, stop=True).then_inc(ge, 1)

    def ready(eng, i):
        eng.wait_ge(gd, 6 * i + 6)

    with nc.Block() as block:
        @block.gpsimd
        def _(pool):
            pool.memset(consts[:, 0:1], MAGIC).then_inc(magic_set, 1)
            n.pool_pass(pool)
            ready(pool, G)
            pool.wait_ge(pa.sem, pa.done(NIT - 1, "g12"))
            for k, (v, s) in enumerate(((gflat, G), (uflat, U))):
                for i in range(NG):
                    part = v[:, i * GW:(i + 1) * GW]
                    pool.tensor_scalar(part, part, inverse(s), MAGIC, ALU.mult, ALU.add).then_inc(rounded_pool, 1)
                    pool.wait_ge(rounded_pool, k * NG + i + 1)
                    pool.tensor_scalar(part, part, 1.0, -MAGIC, ALU.mult, ALU.add).then_inc((gate_int, up_int)[k], 1)

        @block.vector
        def _(dve):
            for s in (px, pd, sd, od, dd, dx):
                dve.sem_inc(s.sem, s.credit())
            k = 0

            def step(ins):
                nonlocal k
                k += 1
                ins.then_inc(wd, 1)
                dve.wait_ge(wd, k)

            w = mem.mat("gate", 0, 9 * C).rearrange("p (n k) -> p n k", k=32)
            step(dve.tensor_reduce(ws[:, 0, :], w, AX.X, ALU.max, apply_absolute_value=True))
            step(dve.tensor_scalar(ws[:, 1, :], ws[:, 0, :], 1.0 / 7.0, 1e-12, ALU.mult, ALU.max))
            step(dve.reciprocal(ws[:, 2, :], ws[:, 1, :]))
            step(dve.tensor_tensor(wq[:, :, :], w, ws[:, 2, :].unsqueeze(2).broadcast_to([128, 36, 32]), ALU.mult))
            step(dve.tensor_scalar(wq[:, :, :], wq[:, :, :], MAGIC, MAGIC, ALU.add, ALU.subtract))
            step(dve.tensor_scalar(wq[:, :, :], wq[:, :, :], 7.0, -8.0, ALU.min, ALU.max))
            step(dve.tensor_tensor(wq[:, :, :], wq[:, :, :], ws[:, 1, :].unsqueeze(2).broadcast_to([128, 36, 32]), ALU.mult))
            n.vector_pass(dve, amax)
            dve.wait_ge(n.dve.sem, n.dve.done(NIT - 1, "amax"))
            find_scale_vector(dve, X, amax[:, 0:NIT])

            def quantise(it, p):
                dve.wait_ge(pt.sem, pt.done(it, f"t{p}"))
                dve.wait_ge(pq.sem, pq.done(it - 1, f"turned{p}"))
                dve.tensor_scalar(qx[:, p], qt[:, p], MAGIC, scale(X), ALU.subtract, ALU.mult).then_inc(px.sem, 1)

            def largest(it, p):
                for j, name, kk in HALVES[0] + HALVES[1]:
                    dve.wait_ge(pe_.sem, pe_.done(it, f"{name}{p}{j}"))
                    dve.tensor_reduce(pmax[:, kk, bass.ds(it * 2 + p, 1), j], bank(2 * j + kk), AX.X, ALU.max,
                                      apply_absolute_value=True).then_inc(pd.sem, 1)

            skewed(dve, NIT, 2, (1, quantise), (0, largest))
            dve.wait_ge(pd.sem, pd.done(NIT - 1, "g12"))
            find_scale_vector(dve, U, pmax[:, 0].rearrange("p c k -> p (c k)"))
            find_scale_vector(dve, G, pmax[:, 1].rearrange("p c k -> p (c k)"))
            dve.tensor_scalar(row[:, 4:5], scale(G), 2.0 ** -16, None, ALU.mult).then_inc(wd, 1)
            dve.wait_ge(wd, k + 1)
            with dve.Fori(0, NG // 2) as it:
                for p in range(2):
                    dve.wait_ge(sa.sem, sa.done(it, f"u{p}"))
                    dve.tensor_scalar(t2[:, p, :], t2[:, p, :], MAGIC, 65535.0, ALU.subtract, ALU.min).then_inc(sd.sem, 1)
                for p in range(2):
                    dve.wait_ge(sd.sem, sd.done(it, f"v{p}"))
                    dve.wait_ge(gate_int, it * 2 + p + 1)
                    g = piece(gflat, it, p)
                    dve.tensor_tensor(g, g, t2[:, p, :], ALU.mult).then_inc(sd.sem, 1)
                for p in range(2):
                    dve.wait_ge(sd.sem, sd.done(it, f"g{p}"))
                    dve.tensor_reduce(amax[:, bass.ds(it * 2 + p, 1)], piece(gflat, it, p), AX.X, ALU.max,
                                      apply_absolute_value=True).then_inc(sd.sem, 1)
            dve.wait_ge(sd.sem, sd.done(NG // 2 - 1, "m1"))
            find_scale_vector(dve, G2, amax[:, 0:NG], unit=row[:, 4:5])
            dve.tensor_tensor(row[:, 5:6], scale(G2), scale(U), ALU.mult).then_inc(wd, 1)
            dve.wait_ge(wd, k + 2)
            with dve.Fori(0, NG // 2) as it:
                for p in range(2):
                    dve.wait_ge(oa.sem, oa.done(it, f"t{p}"))
                    dve.wait_ge(up_int, it * 2 + p + 1)
                    dve.scalar_tensor_tensor(piece(gflat, it, p), t1[:, p], MAGIC, piece(uflat, it, p), ALU.subtract, ALU.mult).then_inc(od.sem, 1)
                for p in range(2):
                    dve.wait_ge(od.sem, od.done(it, f"o{p}"))
                    dve.tensor_reduce(amax_u[:, bass.ds(it * 2 + p, 1)], piece(gflat, it, p), AX.X, ALU.max,
                                      apply_absolute_value=True).then_inc(od.sem, 1)
            dve.wait_ge(od.sem, od.done(NG // 2 - 1, "m1"))
            find_scale_vector(dve, O, amax_u[:, 0:NG], unit=row[:, 5:6])

            def integers(it, p):
                dve.wait_ge(da.sem, da.done(it, f"t{p}"))
                dve.wait_ge(de.sem, de.done(it - 1, f"out{p}"))
                dve.tensor_scalar(prod[:, p], rounded[:, p], MAGIC, None, ALU.subtract).then_inc(dd.sem, 1)

            def add(it, p):
                x = chunk(mem.x, it, p)
                dve.wait_ge(de.sem, de.done(it, f"out{p}"))
                dve.scalar_tensor_tensor(x, bt(bank(p)), scale(O), x, ALU.mult, ALU.add).then_inc(dx.sem, 1)

            skewed(dve, NIT, 2, (1, integers), (0, add))

        @block.scalar
        def _(act):
            for s in (pt, pa, sa, oa, da):
                act.sem_inc(s.sem, s.credit())
            act.preload_act_table(ACT.Sigmoid)
            for i in range(3):
                act.wait_ge(we.sem, i + 1)
                act.activation(wT[:, i, :], bank(i)[:, 0:3 * C], ACT.Copy).then_inc(wa.sem, 1)
            act.wait_ge(wd, 7)
            act.wait_ge(magic_set, 1)

            def quantise(it, p):
                act.wait_ge(px.sem, px.done(it - 1, f"q{p}"))
                act.activation(qt[:, p], chunk(mem.xl, it, p), ACT.Identity, bias=consts[:, 0:1], scale=inverse(X)).then_inc(pt.sem, 1)

            def turned(it, p):
                act.wait_ge(pq.sem, pq.done(it, f"turned{p}"))
                act.wait_ge(pe_.sem, pe_.done(it - 1, f"g{p}2"))
                act.activation(qxT[:, p], bank(6 + p), ACT.Copy).then_inc(pt.sem, 1)

            def keep(part):
                def stage(it, p):
                    for j, name, kk in HALVES[part]:
                        dst = gate if kk else up
                        act.wait_ge(pd.sem, pd.done(it, f"{name}{p}{j}"))
                        act.activation(dst[:, j, bass.ds((it * 2 + p) * W, W)], bank(2 * j + kk), ACT.Copy).then_inc(pa.sem, 1)
                return stage

            ready(act, X)
            skewed(act, NIT, 2, (1, quantise), (0, keep(0)), (1, turned), (0, keep(1)))
            ready(act, G)
            act.wait_ge(pa.sem, pa.done(NIT - 1, "g12"))
            with act.Fori(0, NG // 2) as it:
                for p in range(2):
                    act.wait_ge(sd.sem, sd.done(it - 1, f"g{p}"))
                    act.wait_ge(gate_int, it * 2 + p + 1)
                    act.activation(t2[:, p, :], piece(gflat, it, p), ACT.Sigmoid, scale=scale(G)).then_inc(sa.sem, 1)
                for p in range(2):
                    act.wait_ge(sa.sem, sa.done(it, f"sig{p}"))
                    act.activation(t2[:, p, :], t2[:, p, :], ACT.Identity, bias=consts[:, 0:1], scale=65536.0).then_inc(sa.sem, 1)
            ready(act, G2)
            with act.Fori(0, NG // 2) as it:
                for p in range(2):
                    act.wait_ge(od.sem, od.done(it - 1, f"o{p}"))
                    act.activation(t1[:, p], piece(gflat, it, p), ACT.Identity, bias=consts[:, 0:1], scale=inverse(G2)).then_inc(oa.sem, 1)
            ready(act, O)
            with act.Fori(0, NIT) as it:
                for p in range(2):
                    act.wait_ge(dd.sem, dd.done(it - 1, f"i{p}"))
                    act.activation(rounded[:, p], gate[:, :, bass.ds((it * 2 + p) * W, W)], ACT.Identity,
                                   bias=consts[:, 0:1], scale=inverse(O)).then_inc(da.sem, 1)

        @block.tensor
        def _(pe):
            for s in (pq, pe_, de):
                pe.sem_inc(s.sem, s.credit())
            pe.wait_ge(wd, 7)
            wflat = wq.rearrange("p n k -> p (n k)")
            for i in range(3):
                for j in range(3):
                    last = pe.transpose(bank(i)[:, j * C:(j + 1) * C], wflat[:, (3 * i + j) * C:(3 * i + j + 1) * C], mem.mat("ident"))
                last.then_inc(we.sem, 1)
            find_scale_tensor(pe, X)
            pe.wait_ge(wa.sem, 3)

            def turn(it, p):
                pe.wait_ge(px.sem, px.done(it, f"q{p}"))
                pe.wait_ge(pt.sem, pt.done(it - 1, f"xT{p}"))
                for j in range(CH):
                    last = pe.transpose(bank(6 + p)[:, j * T:(j + 1) * T], qx[:, p, j, :], mem.mat("ident"))
                last.then_inc(pq.sem, 1)

            def project(part):
                def stage(it, p):
                    pe.wait_ge(pt.sem, pt.done(it, f"xT{p}"))
                    for j, name, kk in HALVES[part]:
                        pe.wait_ge(pa.sem, pa.done(it, f"{name}0{j}") if p else pa.done(it - 1, f"{name}1{j}"))
                        pe.matmul(bank(2 * j + kk), wT[:, 1 - kk, j * C:(j + 1) * C], qxT[:, p], start=True, stop=True).then_inc(pe_.sem, 1)
                return stage

            skewed(pe, NIT, 2, (0, project(0)), (1, turn), (0, project(1)))
            pe.wait_ge(pt.sem, pt.done(NIT - 1, "xT1"))
            for i in (U, G, G2, O):
                find_scale_tensor(pe, i)
            with pe.Fori(0, NIT) as it:
                for p in range(2):
                    pe.wait_ge(dd.sem, dd.done(it, f"i{p}"))
                    pe.wait_ge(dx.sem, dx.done(it - 1, f"add{p}"))
                    for j in range(CH):
                        for k in range(3):
                            last = pe.matmul(bank(p)[:, j * C:(j + 1) * C], prod[:, p, k, j * T:(j + 1) * T],
                                             wT[:, 2, k * C:(k + 1) * C], start=(k == 0), stop=(k == 2))
                    last.then_inc(de.sem, 1)

        @block.sync
        def _(sp):
            dst = out.rearrange("b t c -> t b c")
            with sp.Fori(0, NIT) as it:
                for p in range(2):
                    sp.wait_ge(dx.sem, dx.done(it, f"add{p}"))
                    at = bass.ds((it * 2 + p) * CH, CH)
                    sp.dma_start(dst[:, at, :], mem.x[:, at, :]).then_inc(stored, 16)
            sp.wait_ge(stored, 16 * NCH)


def build(nc, x, ctx_tokens, pack, rows, b_proj, w_fc, w_proj, v_mask, out):
    with ExitStack() as ctx:
        mem = Memory(nc, ctx)
        x_loaded, loaded = load_block(nc, mem, ctx, x, pack, rows, b_proj)
        with mem.block_memory("time_mix", ARENA):
            time_mix_block(nc, mem, ctx, x_loaded, loaded)
        with mem.kept_memory():
            with nc.sbuf_tensor("scores_split0", [128, SCORE_WORDS], F32R) as split, \
                    mem.block_memory("attention0", ARENA - KEPT_WORDS - SCORE_WORDS):
                attention_block(nc, mem, ctx, 0, v_mask, ctx_tokens, split)
            experts_block(nc, mem, ctx, w_fc, w_proj)
            with mem.block_memory("state_space", ARENA - KEPT_WORDS):
                state_space_block(nc, mem, ctx)
            with nc.sbuf_tensor("scores_split1", [128, SCORE_WORDS], F32R) as split, \
                    mem.block_memory("attention1", ARENA - KEPT_WORDS - SCORE_WORDS):
                attention_block(nc, mem, ctx, 1, v_mask, ctx_tokens, split)
        with mem.block_memory("ffn", ARENA):
            quantised_ffn_block(nc, mem, ctx, out)


def lay_out(inp):
    import numpy as np

    f = {k: np.asarray(v) for k, v in inp.items()}
    a, x0, m, x1, g = "L0_attn_", "L0_xattn_", "L1_attn_", "L1_xattn_", "L1_ffn_"

    def blocks(w):
        return w.reshape(-1, 128, w.shape[1]).transpose(1, 0, 2).reshape(128, -1)

    parts = {
        "ln1_w": f[a + "ln1_w"], "ln1_b": f[a + "ln1_b"], "ln2_w": f[a + "ln2_w"], "ln2_b": f[a + "ln2_b"],
        "tmk": f[a + "att_tmk"], "tmv": f[a + "att_tmv"], "tmr": f[a + "att_tmr"],
        "decay": f[a + "time_decay"], "first": f[a + "time_first"],
        "ftmk": f[a + "ffn_tmk"], "ftmr": f[a + "ffn_tmr"], "bq": f[x0 + "bq"], "bk": f[x0 + "bk"], "bv": f[x0 + "bv"],
        "m_ln1_g": f[m + "ln1_g"], "m_ln1_b": f[m + "ln1_b"], "in_b0": f[m + "in_b"][:C], "in_b1": f[m + "in_b"][C:],
        "dw0": f[m + "dw_W"][:, 0, 0], "dw1": f[m + "dw_W"][:, 0, 1], "dw2": f[m + "dw_W"][:, 0, 2],
        "dw_b": f[m + "dw_b"], "dt_b": f[m + "dt_b"], "b_b": f[m + "b_b"], "c_b": f[m + "c_b"],
        "a_log": f[m + "a_log"], "d_skip": f[m + "d_skip"], "m_ln2_g": f[m + "ln2_g"], "m_ln2_b": f[m + "ln2_b"],
        "f1_b0": f[m + "f1_b"][:C], "f1_b1": f[m + "f1_b"][C:],
        "b_fc": f["L0_ffn_b_fc"].reshape(E, 4, 128).transpose(2, 0, 1),
        "WkT": f[a + "Wk"].T, "WvT": f[a + "Wv"].T, "WrT": f[a + "Wr"].T, "WoT": f[a + "Wo"].T,
        "WkeyT": f[a + "Wkey"].T, "WrecT": f[a + "Wrec"].T, "WvalT": blocks(f[a + "Wval"].T),
        "qT0": f[x0 + "Wq"].T, "kT0": f[x0 + "Wk"].T, "vT0": f[x0 + "Wv"].T, "oT0": f[x0 + "Wo"].T,
        "qT1": f[x1 + "Wq"].T, "kT1": f[x1 + "Wk"].T, "vT1": f[x1 + "Wv"].T, "oT1": f[x1 + "Wo"].T,
        "router": np.pad(f["L0_ffn_router_w"].T, ((0, 0), (0, 32 - E))), "in_W": f[m + "in_W"], "dt_W": f[m + "dt_W"], "b_W": f[m + "b_W"],
        "c_W": f[m + "c_W"], "out_W": f[m + "out_W"], "f1_W": f[m + "f1_W"], "f2_W": blocks(f[m + "f2_W"]),
        "gate": blocks(f[g + "w_gate"]), "up": blocks(f[g + "w_up"]), "down": f[g + "w_down"],
    }
    head_of = np.arange(128) % 32 // HD
    parts["head_mask"] = (np.arange(128)[:, None] // HD == np.arange(H)[None, :]).astype(np.float32)
    parts["rank"] = np.broadcast_to(np.arange(E, 0, -1, dtype=np.float32), (128, E))
    parts["ident"] = np.eye(128, dtype=np.float32)
    parts["causal"] = np.where(np.arange(S)[None, :] > np.arange(128)[:, None], np.float32(-1e30), np.float32(0))
    v_mask = np.broadcast_to(head_of[None, :] == np.arange(4)[:, None], (128, 4, C)).astype(np.float32)
    pack = np.concatenate([np.asarray(parts[n]).reshape(128, w) for n, w in LAYOUT], axis=1)
    rows = np.concatenate([f[x0 + "bo"], f[m + "out_b"], f[m + "f2_b"], f[x1 + "bo"]])[None, :]
    b_proj = np.zeros((128, C), np.float32)
    b_proj[0:E] = b_proj[32:32 + E] = f["L0_ffn_b_proj"]
    return {
        "x": f["x"], "ctx_tokens": f["ctx_1024"], "pack": pack, "rows": rows, "b_proj": b_proj,
        "w_fc": f["L0_ffn_w_fc"].transpose(1, 0, 2).reshape(128, E * HID),
        "w_proj": f["L0_ffn_w_proj"].reshape(E, 4, 128, C).transpose(2, 0, 1, 3).reshape(128, E * 4 * C),
        "v_mask": v_mask,
    }


def kernel(**inputs):
    import numpy as np
    import concourse.bacc as bacc
    from concourse.bass_utils import run_bass_kernel_spmd

    arrays = {f"in_{k}": np.ascontiguousarray(v) for k, v in lay_out(inputs).items()}
    nc = bacc.Bacc("TRN2", target_bir_lowering=False, num_devices=1)
    args = [nc.dram_tensor(k, v.shape, F32, kind="ExternalInput").ap() for k, v in arrays.items()]
    out = nc.dram_tensor("out", (B, T, C), F32, kind="ExternalOutput").ap()
    build(nc, *args, out)
    r = run_bass_kernel_spmd(nc, [arrays], core_ids=[0])
    return r.results[0]["out"]
```
